# Optimizing a Trainium2 kernel written in Bass

```python
import numpy as np
import jax
import jax.numpy as jnp

def _softmax(x, axis=-1):
    return jax.nn.softmax(x, axis=axis)

def _gelu(x):
    return jax.nn.gelu(x, approximate=True)

def _silu(x):
    return jax.nn.silu(x)

def _sigmoid(x):
    return jax.nn.sigmoid(x)

def _layernorm(x, axis=-1, eps=1e-05):
    m = jnp.mean(x, axis=axis, keepdims=True)
    v = jnp.var(x, axis=axis, keepdims=True)
    return (x - m) / jnp.sqrt(v + eps)

def _scatter_add(tgt, idx, src, axis=0):
    return tgt.at[idx].add(src)

def _segment_sum(src, seg, n):
    return jax.ops.segment_sum(src, seg, n)
kernel_name = 'mk_xattn_ffn_d1_seqx_r8_d8fa98'

def setup_inputs(seed: int=0):
    np.random.seed(seed)
    _w = jnp.asarray

    def _rec_inputs():
        import jax
        import jax.numpy as jnp
        _rk = jax.random.key(seed)
        x = 7.22e-05 + 1 * jax.random.normal(jax.random.fold_in(_rk, 1), (32, 64, 512), jnp.float32)
        _lenS = 64 - jax.random.randint(jax.random.fold_in(_rk, 7), (32,), 0, max(1, 64 // 4) + 1, jnp.int32)
        _lenS2 = 64 - jax.random.randint(jax.random.fold_in(_rk, 8), (32,), 0, max(1, 64 // 4) + 1, jnp.int32)
        _ctx_4096P = jax.random.normal(jax.random.fold_in(_rk, 11), (32, 16, 512), jnp.float32)
        _ctx_4096c = jax.random.dirichlet(jax.random.fold_in(_rk, 511), 0.3 * jnp.ones((16,), jnp.float32), (32, 64))
        _ctx_4096t = jnp.einsum('bsk,bkd->bsd', _ctx_4096c, _ctx_4096P)
        _ctx_4096t = _ctx_4096t * jax.lax.rsqrt(jnp.mean(jnp.square(_ctx_4096t)) + 1e-12) * 0.953939
        ctx_4096 = 4.13588e-05 + 0.999923 * (_ctx_4096t + 0.3 * jax.random.normal(jax.random.fold_in(_rk, 611), (32, 64, 512), jnp.float32))
        return (x, ctx_4096)
    x, ctx_4096 = _rec_inputs()

    def _L0_xattn_setup():
        import jax, jax.numpy as jnp
        import numpy as np
        import math
        D_MODEL = 128
        NHEAD = 16
        MAX_SUP = 4
        DK = D_MODEL // NHEAD
        DM = D_MODEL * MAX_SUP
        B, S = (2, 128)
        key = jax.random.key(seed)
        ks = jax.random.split(key, 12)
        std = 0.02
        inp = {'q': jax.random.normal(ks[0], (B, S, DM), jnp.float32), 'k': jax.random.normal(ks[1], (B, S, DM), jnp.float32), 'v': jax.random.normal(ks[2], (B, S, DM), jnp.float32), 'Wq': jax.random.normal(ks[3], (DM, DM), jnp.float32) * std, 'bq': jnp.zeros((DM,), jnp.float32), 'Wk': jax.random.normal(ks[4], (DM, DM), jnp.float32) * std, 'bk': jnp.zeros((DM,), jnp.float32), 'Wv': jax.random.normal(ks[5], (DM, DM), jnp.float32) * std, 'bv': jnp.zeros((DM,), jnp.float32), 'interference': jax.random.normal(ks[6], (NHEAD, MAX_SUP, MAX_SUP), jnp.float32), 'amp': jnp.ones((1,), jnp.float32), 'Wo': jax.random.normal(ks[7], (DM, DM), jnp.float32) * std, 'bo': jnp.zeros((DM,), jnp.float32)}
        return inp
    _L0_xattn_all = _L0_xattn_setup()
    _L0_xattn_in = {k: v for k, v in _L0_xattn_all.items() if k in ('Wq', 'bq', 'Wk', 'bk', 'Wv', 'bv', 'interference', 'amp', 'Wo', 'bo')}
    del _L0_xattn_all

    def _L0_ffn_setup():
        import jax, jax.numpy as jnp
        import numpy as np
        HIDDEN = 512
        INTER = 1376
        GROUP = 128
        B, S = (4, 256)
        NIB = jnp.uint32(15)

        def _pack_rows(nib):
            r = nib.reshape(-1, 8, nib.shape[-1])
            shifts = (jnp.arange(8, dtype=jnp.uint32) * 4)[None, :, None]
            return jnp.sum(r << shifts, axis=1, dtype=jnp.uint32)

        def _pack_cols(nib):
            r = nib.reshape(nib.shape[0], -1, 8)
            shifts = (jnp.arange(8, dtype=jnp.uint32) * 4)[None, None, :]
            return jnp.sum(r << shifts, axis=2, dtype=jnp.uint32)

        def _dequant(qw, qz, sc, g_idx):
            shifts = jnp.arange(8, dtype=jnp.uint32) * 4
            wq = qw[:, None, :] >> shifts[None, :, None] & NIB
            wq = wq.reshape(-1, qw.shape[1]).astype(jnp.float32)
            zq = qz[:, :, None] >> shifts[None, None, :] & NIB
            zq = zq.reshape(qz.shape[0], -1).astype(jnp.float32) + 1.0
            return sc[g_idx] * (wq - zq[g_idx])
        key = jax.random.key(seed)
        ks = jax.random.split(key, 7)
        n_groups = HIDDEN // GROUP
        n_groups_d = INTER // GROUP
        x = jax.random.normal(ks[0], (B, S, HIDDEN), jnp.float32)
        nib_w_gu = jax.random.randint(ks[1], (HIDDEN, 2 * INTER), 0, 16).astype(jnp.uint32)
        nib_z_gu = jax.random.randint(ks[2], (n_groups, 2 * INTER), 0, 15).astype(jnp.uint32)
        qweight_gu = _pack_rows(nib_w_gu)
        qzeros_gu = _pack_cols(nib_z_gu)
        scales_gu = jax.random.uniform(ks[3], (n_groups, 2 * INTER), jnp.float32, 0.005, 0.02)
        g_idx_gu = jnp.arange(HIDDEN, dtype=jnp.int32) // GROUP
        nib_w_d = jax.random.randint(ks[4], (INTER, HIDDEN), 0, 16).astype(jnp.uint32)
        nib_z_d = jax.random.randint(ks[5], (n_groups_d, HIDDEN), 0, 15).astype(jnp.uint32)
        qweight_down = _pack_rows(nib_w_d)
        qzeros_down = _pack_cols(nib_z_d)
        scales_down = jax.random.uniform(ks[6], (n_groups_d, HIDDEN), jnp.float32, 0.005, 0.02)
        g_idx_down = jnp.arange(INTER, dtype=jnp.int32) // GROUP
        return {'x': x, 'qweight_gu': qweight_gu, 'qzeros_gu': qzeros_gu, 'scales_gu': scales_gu, 'g_idx_gu': g_idx_gu, 'qweight_down': qweight_down, 'qzeros_down': qzeros_down, 'scales_down': scales_down, 'g_idx_down': g_idx_down}
    _L0_ffn_all = _L0_ffn_setup()
    _L0_ffn_in = {k: v for k, v in _L0_ffn_all.items() if k in ('qweight_gu', 'qzeros_gu', 'scales_gu', 'g_idx_gu', 'qweight_down', 'qzeros_down', 'scales_down', 'g_idx_down')}
    del _L0_ffn_all
    return {'x': x, 'ctx_4096': ctx_4096, 'L0_xattn_Wq': _L0_xattn_in['Wq'], 'L0_xattn_bq': _L0_xattn_in['bq'], 'L0_xattn_Wk': _L0_xattn_in['Wk'], 'L0_xattn_bk': _L0_xattn_in['bk'], 'L0_xattn_Wv': _L0_xattn_in['Wv'], 'L0_xattn_bv': _L0_xattn_in['bv'], 'L0_xattn_interference': _L0_xattn_in['interference'], 'L0_xattn_amp': _L0_xattn_in['amp'], 'L0_xattn_Wo': _L0_xattn_in['Wo'], 'L0_xattn_bo': _L0_xattn_in['bo'], 'L0_ffn_qweight_gu': _L0_ffn_in['qweight_gu'], 'L0_ffn_qzeros_gu': _L0_ffn_in['qzeros_gu'], 'L0_ffn_scales_gu': _L0_ffn_in['scales_gu'], 'L0_ffn_g_idx_gu': _L0_ffn_in['g_idx_gu'], 'L0_ffn_qweight_down': _L0_ffn_in['qweight_down'], 'L0_ffn_qzeros_down': _L0_ffn_in['qzeros_down'], 'L0_ffn_scales_down': _L0_ffn_in['scales_down'], 'L0_ffn_g_idx_down': _L0_ffn_in['g_idx_down']}

def reference(x, ctx_4096, L0_xattn_Wq, L0_xattn_bq, L0_xattn_Wk, L0_xattn_bk, L0_xattn_Wv, L0_xattn_bv, L0_xattn_interference, L0_xattn_amp, L0_xattn_Wo, L0_xattn_bo, L0_ffn_qweight_gu, L0_ffn_qzeros_gu, L0_ffn_scales_gu, L0_ffn_g_idx_gu, L0_ffn_qweight_down, L0_ffn_qzeros_down, L0_ffn_scales_down, L0_ffn_g_idx_down):
    import jax
    import jax.numpy as jnp

    def _L0_xattn_ref(q, k, v, Wq, bq, Wk, bk, Wv, bv, interference, amp, Wo, bo):
        import jax, jax.numpy as jnp
        import numpy as np
        import math
        D_MODEL = 128
        NHEAD = 16
        MAX_SUP = 4
        DK = D_MODEL // NHEAD
        DM = D_MODEL * MAX_SUP
        B, S = (2, 128)
        b, s, dm = q.shape
        H, M = (interference.shape[0], interference.shape[1])
        dk = dm // (H * M)

        def proj(x, W, bias):
            y = x @ W.T + bias
            y = y.reshape(b, s, H, dk, M)
            return jnp.transpose(y, (0, 2, 1, 3, 4))
        qh = proj(q, Wq, bq)
        kh = proj(k, Wk, bk)
        vh = proj(v, Wv, bv)

        def interfere(x):
            return x + 0.1 * amp[0] * jnp.einsum('bhsdi,hij->bhsdj', x, interference)
        qh, kh, vh = (interfere(qh), interfere(kh), interfere(vh))
        scores = jnp.einsum('bhqdm,bhkdm->bhqkm', qh, kh) / math.sqrt(dk)
        weights = jax.nn.softmax(scores, axis=3)
        out = jnp.einsum('bhqkm,bhkdm->bhqdm', weights, vh)
        out = jnp.transpose(out, (0, 2, 1, 3, 4)).reshape(b, s, dm)
        return out @ Wo.T + bo

    def _L0_ffn_ref(x, qweight_gu, qzeros_gu, scales_gu, g_idx_gu, qweight_down, qzeros_down, scales_down, g_idx_down):
        import jax, jax.numpy as jnp
        import numpy as np
        HIDDEN = 512
        INTER = 1376
        GROUP = 128
        B, S = (4, 256)
        NIB = jnp.uint32(15)

        def _pack_rows(nib):
            r = nib.reshape(-1, 8, nib.shape[-1])
            shifts = (jnp.arange(8, dtype=jnp.uint32) * 4)[None, :, None]
            return jnp.sum(r << shifts, axis=1, dtype=jnp.uint32)

        def _pack_cols(nib):
            r = nib.reshape(nib.shape[0], -1, 8)
            shifts = (jnp.arange(8, dtype=jnp.uint32) * 4)[None, None, :]
            return jnp.sum(r << shifts, axis=2, dtype=jnp.uint32)

        def _dequant(qw, qz, sc, g_idx):
            shifts = jnp.arange(8, dtype=jnp.uint32) * 4
            wq = qw[:, None, :] >> shifts[None, :, None] & NIB
            wq = wq.reshape(-1, qw.shape[1]).astype(jnp.float32)
            zq = qz[:, :, None] >> shifts[None, None, :] & NIB
            zq = zq.reshape(qz.shape[0], -1).astype(jnp.float32) + 1.0
            return sc[g_idx] * (wq - zq[g_idx])
        w_gu = _dequant(qweight_gu, qzeros_gu, scales_gu, g_idx_gu)
        inter = jnp.einsum('bsh,hf->bsf', x, w_gu)
        gate, up = (inter[..., :INTER], inter[..., INTER:])
        h = jax.nn.silu(gate) * up
        w_d = _dequant(qweight_down, qzeros_down, scales_down, g_idx_down)
        return jnp.einsum('bsf,fh->bsh', h, w_d)
    x = x + _L0_xattn_ref(_layernorm(x, axis=-1), ctx_4096, ctx_4096, L0_xattn_Wq, L0_xattn_bq, L0_xattn_Wk, L0_xattn_bk, L0_xattn_Wv, L0_xattn_bv, L0_xattn_interference, L0_xattn_amp, L0_xattn_Wo, L0_xattn_bo)
    x = x + _L0_ffn_ref(_layernorm(x, axis=-1), L0_ffn_qweight_gu, L0_ffn_qzeros_gu, L0_ffn_scales_gu, L0_ffn_g_idx_gu, L0_ffn_qweight_down, L0_ffn_qzeros_down, L0_ffn_scales_down, L0_ffn_g_idx_down)
    return x

_drawn_inputs = setup_inputs


def setup_inputs(seed=0):
    import zlib

    import numpy as np

    out = dict(_drawn_inputs(seed))
    spreads = {'L0_xattn_bq': (0.0, 0.8),
     'L0_xattn_bk': (0.0, 0.8),
     'L0_xattn_bv': (0.0, 0.1),
     'L0_xattn_bo': (0.0, 0.1)}
    factors = {'L0_xattn_Wq': 4.326, 'L0_xattn_Wk': 4.162}
    for name, (base, spread) in spreads.items():
        noise = np.random.default_rng([zlib.crc32(name.encode()), seed]).standard_normal(out[name].shape)
        drawn = base * np.exp(spread * noise) if base else spread * noise
        out[name] = jnp.asarray(drawn.astype(out[name].dtype))
    for name, factor in factors.items():
        out[name] = (out[name] * factor).astype(out[name].dtype)
    return out
```

```python
from contextlib import ExitStack

import concourse.bass as bass
from concourse import mybir

P = 128
F32 = mybir.dt.float32
F16 = mybir.dt.float16
I32 = mybir.dt.int32
U32 = mybir.dt.uint32
ALU = mybir.AluOpType
ACT = mybir.ActivationFunctionType
AX_X = mybir.AxisListType.X
ABSMAX = bass.bass_isa.ReduceOp.absmax

BATCH, SEQ, DM = 32, 64, 512
HEADS, SUP, DK = 16, 4, 8
INTER, GROUPS_GU, GROUPS_D = 1376, 4, 10
EPS = 1e-5

KB = DM // P
TOK = 256
TILES = TOK // P
NCHUNK = BATCH * SEQ // TOK
NB = TOK // SEQ
SLOTS = NB * HEADS // 4
FB = (INTER + P - 1) // P
UNITS = (FB + 1) // 2
VROW = 2 * 2 * DK + 1
LN_SCALE = 64.0
P_SCALE = 4096.0
TOP = 14

PASSES = ((0, 0), (0, 1), (1, 0))

OT_STEP = 10
T_ORDER = (["x2T0", "x2T1", "xT0", "xT1"] + [f"pT{s}" for s in range(OT_STEP)] + ["oT0"]
           + [f"pT{s}" for s in range(OT_STEP, SLOTS)] + ["oT1", "cT0", "cT1"])
T_USES = len(T_ORDER)
STEPS = SLOTS + 2
SLICES = 2 * STEPS


def width(block):
    return min(P, INTER - P * block)


def reached(engine, semaphore, value):
    if isinstance(value, int) and value <= 0:
        return
    engine.wait_ge(semaphore, value)


def build(nc, x, ctx_in, Wq, bq, Wk, bk, Wv, bv, interference, amp, Wo, bo,
          qw_gu, qz_gu, sc_gu, gi_gu, qw_d, qz_d, sc_d, gi_d, out):
    with ExitStack() as stack:
        def sb(name, shape, dt):
            return stack.enter_context(nc.sbuf_tensor(name, shape, dt))

        def sem(name):
            return stack.enter_context(nc.semaphore(name))

        WT = sb("WT", [P, 4, 2, KB, DM], F16)
        WGU = sb("WGU", [P, 2, KB, 2 * INTER], F16)
        WD = sb("WD", [P, 2, FB, DM], F16)

        ident = sb("ident", [P, P], F32)
        bv_row = sb("bv_row", [P, DM], F32)
        bo_row = sb("bo_row", [P, DM], F32)
        small = sb("small", [P, 104], F32)
        smalli = sb("smalli", [P, 8], I32)
        bqk = sb("bqk", [P, 2, KB], F32)
        stats = sb("stats", [P, 4, 6], F32)
        mv = sb("mv", [P, 4, 2], F32)
        vareps = sb("vareps", [P, 4], F32)
        rstd = sb("rstd", [P, 4], F32)
        negmax = sb("negmax", [P, 2, 8], F32)
        osum = sb("osum", [P, 2, 8, DK], F32)
        rinv = sb("rinv", [P, 2, 8], F32)

        arena_bytes = 105 * 1024
        arena = sb("arena", [P, arena_bytes // 4], F32)
        at = [0]

        def carve(nbytes, dt, start=None):
            a = at[0] if start is None else start
            if start is None:
                at[0] += nbytes
            assert a % 4 == 0 and nbytes % 4 == 0 and a + nbytes <= arena_bytes, (a, nbytes)
            v = arena[:, a // 4:(a + nbytes) // 4]
            return v if dt == F32 else v.bitcast(dt)

        qstack = carve(16384, F16).rearrange("p (h n) -> p h n", h=HEADS)
        kstack = carve(16384, F16).rearrange("p (h n) -> p h n", h=HEADS)
        xin = carve(4096, F32).rearrange("p (t n) -> p t n", t=TILES)
        cin = carve(4096, F32).rearrange("p (t n) -> p t n", t=TILES)
        x2 = carve(4096, F32).rearrange("p (t n) -> p t n", t=TILES)
        xln = carve(4096, F32).rearrange("p (t n) -> p t n", t=TILES)
        actT = carve(4096, F16).rearrange("p (s k t) -> p s k t", s=2, k=KB)
        x2T = carve(4096, F16).rearrange("p (s k t) -> p s k t", s=2, k=KB)
        masked = carve(8192, F16).rearrange("p (r s n v t) -> p r s n v t", r=2, s=2, n=8, v=2)
        vsb = carve(2 * 2 * HEADS * VROW * 2, F16).rearrange("p (r q h n) -> p r q h n", r=2, q=2, h=HEADS)
        vv_words = carve(NB * 2 * HEADS * VROW * 2, F32)
        vv = vv_words.bitcast(F16).rearrange("p (b q h n) -> p b q h n", b=NB, q=2, h=HEADS)
        pring = carve(4096, F32).rearrange("p (r n) -> p r n", r=2)
        phl = carve(4096, F16).rearrange("p (r s n) -> p r s n", r=2, s=2)
        obuf = carve(2048, F32).rearrange("p (r n) -> p r n", r=2)
        hbuf = carve(4096, F32).rearrange("p (r n) -> p r n", r=2)
        hT = carve(FB * TOK * 2 * 2, F16).rearrange("p (s f t) -> p s f t", s=2, f=FB)

        wraw = carve(32768, F32, 0).rearrange("p (w g n) -> p w g n", w=4, g=KB)
        qw_bytes = FB * DM * 4
        qw_st = [carve(qw_bytes, U32, 32768 + i * qw_bytes) for i in range(2)]
        so = 32768 + 2 * qw_bytes
        tmat = carve(2048, F32, so).rearrange("p (g n) -> p g n", g=KB)
        maskm = carve(512, F32, so + 2048)
        iv = carve(64, F32, so + 2560)
        eye4 = carve(16, F32, so + 2624)
        zraw = carve(4 * 344, U32, so + 2688)
        so2 = so + 2688 + 4 * 344
        hot_gu = carve(2048, F32, so2)
        hot_d = carve(INTER * 4, F32, so2 + 2048)
        scd = carve(2048, F32, so2 + 7552)
        zd = carve(2048, F32, so2 + 9600)
        so3 = so2 + 11648
        cmax_st = carve(8192, F32, so3).rearrange("p (r n) -> p r n", r=2)
        gidx = carve(INTER * 4, F32, so3)
        wop = [hot_gu, hot_d[:, 0:DM], hot_d[:, DM:2 * DM], carve(2048, F32, so3 + 8192)]
        zint = carve(0 + 2 * INTER * 4, U32, 0)
        dq = [carve(2048, F32, 16384 + 2048 * i) for i in range(4)]
        wint = [carve(2048, U32, 24576 + 2048 * i) for i in range(2)]
        scgu = WD[:, :, :, :].rearrange("p s f n -> p (s f n)").bitcast(F32)[:, 0:2 * INTER]
        zgu = WD[:, :, :, :].rearrange("p s f n -> p (s f n)").bitcast(F32)[:, 2 * INTER:4 * INTER]

        bank = [stack.enter_context(nc.psum_tensor(f"bank{i}", [P, 512], F32)) for i in range(8)]
        SB, TB, JB, GB, UB = bank[0:2], bank[2:4], bank[4:6], bank[6], bank[7]

        MX = small[:, 0:10]
        MR = small[:, 10:20]
        BD = small[:, 20:31]
        PW = small[:, 31:42]
        SC = small[:, 42:53]
        IV = small[:, 53:64]
        KQ, KK, KV, KSM, KWO, KTANH, KH, KY = (small[:, 64 + i:65 + i] for i in range(8))
        T1, T2, T3, T4 = (small[:, 72 + i:73 + i] for i in range(4))
        MASK = small[:, 76:80]
        AMP = small[:, 80:81]
        GID = small[:, 81:82]
        NHALF = small[:, 82:83]
        BQR = small[:, 84:92]
        MXC = small[:, 92:92 + NCHUNK]
        bvx = zd

        S = {n: sem(n) for n in (
            "w_loaded", "wo_permuted", "const_loaded", "ctxm_loaded0", "ctxm_loaded1", "sc_loaded", "qwg_loaded", "qwu_loaded", "qwd_loaded", "gi_loaded",
            "pool_const", "pool_iv", "dve_setup", "t_ready", "fold_done", "fold_evicted", "bias_done", "bias_evicted",
            "max_ready", "max_all", "scale_ready", "whi_done", "wlo_done", "cmax_done",
            "sczu_done", "d_int", "d_sub", "d_w", "d_hi", "d_lo", "prep_done", "zero_done",
            "x_loaded", "ctx_loaded", "k_stacked", "q_stacked", "v_stacked", "y_stored0", "y_stored1",
            "tr_done", "proj_done", "s_done", "pv_done", "wo_done", "g_done", "u_done", "d_done",
            "t_hi", "qk_evicted", "v_hi", "exp_done", "tanh_done", "h_hi",
            "t_lo", "m_hi", "qm_ready", "v_evicted", "v_lo", "max_done", "sub_done", "o_step", "o_ready",
            "x2_part", "x2_ready", "ln_step", "ln_var", "xln_ready", "x2ln_ready", "g_freed", "h_ready", "y_ready",
            "ln_rstd", "h_lo")}

        tile_rows = lambda a: a.rearrange("b s n -> (b s) n").rearrange("(c t p) n -> c p t n", p=P, t=TILES)
        x_d, c_d, y_d = tile_rows(x), tile_rows(ctx_in), tile_rows(out)

        def ap(base, part, nparts, off, dims):
            a = base[part:part + nparts]
            return bass.AP(a.tensor, a.offset + off, [list(a.ap[0])] + [list(d) for d in dims])

        def t_at(c, name):
            if name.startswith("cT") and isinstance(c, int) and c < 0:
                return int(name[2:]) + 1
            if isinstance(c, int) and c == NCHUNK:
                return t_at(c - 1, f"cT{name[-1]}")
            return c * T_USES + T_ORDER.index(name) + 1

        def stack_dmas(e, c, which):
            dst, parts, name, base = ((kstack, (0, 0, 1, 1), "k_stacked", 0) if which == "k" else
                                      (qstack, (0, 1, 0, 1), "q_stacked", 2))
            for G in range(2):
                e.wait_ge(S["qm_ready"], 4 * c + base + G + 1)
                for r, part in enumerate(parts):
                    for a in range(4):
                        e.dma_start(ap(dst, 32 * r, 32, (8 * G + a) * 512, [(4 * 512, 2), (1, 512)]),
                                    ap(masked[:, G], 32 * a, 32, part * 1024, [(512, 2), (1, 512)])
                                    ).then_inc(S[name], 16)

        def v_dmas(e, c):
            for t in range(TILES):
                e.wait_ge(S["v_lo"], 2 * c + t + 1)
                for bb in range(2):
                    for q in range(2):
                        e.dma_start(vv[64 * q:64 * q + 64, 2 * t + bb, q, :, :],
                                    vsb[64 * bb:64 * bb + 64, t, q, :, :]).then_inc(S["v_stacked"], 16)

        def sync_chunk(e, c, first=False, last=False):
            reached(e, S["s_done"], SLOTS * c)
            stack_dmas(e, c, "k")
            reached(e, S["pv_done"], SLOTS * c)
            v_dmas(e, c)
            if not last:
                e.wait_ge(S["tr_done"], t_at(c - 1, "cT1"))
                e.dma_start(cin, c_d[c + 1]).then_inc(S["ctx_loaded"], 16)
            stack_dmas(e, c, "q")
            if not first:
                store(e, c - 1)
            if not last:
                e.wait_ge(S["x2_ready"], 2 * c + 2)
                e.dma_start(xin, x_d[c + 1]).then_inc(S["x_loaded"], 16)

        def store(e, f):
            for t in range(TILES):
                e.wait_ge(S["y_ready"], 2 * f + t + 1)
                e.dma_start(y_d[f, :, t, :], x2[:, t, :]).then_inc(S[f"y_stored{t}"], 16)

        def sync_setup(e):
            for w, a in enumerate((Wq, Wk, Wv, Wo)):
                e.dma_start(wraw[:, w], a.rearrange("(g p) n -> p g n", p=P)).then_inc(S["w_loaded"], 16)
            for g in range(KB):
                for a in range(4):
                    h = 4 * g + a
                    e.dma_start(ap(iv, 32 * a, 32, 4 * g, [(1, 4)]),
                                bass.AP(interference.tensor, interference.offset + 16 * h, [[0, 8], [4, 4], [1, 4]])
                                ).then_inc(S["const_loaded"], 16)
            e.dma_start(AMP, amp.partition_broadcast(P)).then_inc(S["const_loaded"], 16)
            for i, b in enumerate((bq, bk)):
                e.dma_start(BQR[:, 4 * i:4 * i + 4], b.rearrange("(g p) -> p g", p=P), allow_slow_non_contiguous=True).then_inc(S["const_loaded"], 16)
            e.dma_start(bo_row[:, :], bo.partition_broadcast(P)).then_inc(S["const_loaded"], 16)
            e.dma_start(bv_row[:, 0:KB], bv.rearrange("(g p) -> p g", p=P), allow_slow_non_contiguous=True).then_inc(S["const_loaded"], 16)
            for c in range(NCHUNK):
                reached(e, S["cmax_done"], c - 1)
                e.dma_start(cmax_st[:, c % 2].rearrange("p (t n) -> p t n", t=TILES), c_d[c]).then_inc(S[f"ctxm_loaded{c % 2}"], 16)
            e.dma_start(scgu[0:GROUPS_GU, :], sc_gu).then_inc(S["sc_loaded"], 16)
            e.dma_start(scd[0:GROUPS_D, :], sc_d).then_inc(S["sc_loaded"], 16)
            def rows(src, dst, s, r0, blocks, nrow, c0, cols, step, name):
                e.dma_start(bass.AP(dst.tensor, dst[s:s + 1].offset, [[dst.ap[0][0] * 8, nrow], [cols, blocks], [1, cols]]),
                            bass.AP(src.tensor, src.offset + r0 * step + c0, [[step, nrow], [16 * step, blocks], [1, cols]])
                            ).then_inc(S[name], 16)
            for half, name in enumerate(("qwg_loaded", "qwu_loaded")):
                for s in range(8):
                    rows(qw_gu, qw_st[half], s, 0, KB, 16, half * INTER, INTER, 2 * INTER, name)
            e.dma_start(zraw[0:GROUPS_GU, 0:2 * INTER // 8], qz_gu).then_inc(S["gi_loaded"], 16)
            e.wait_ge(S["cmax_done"], NCHUNK)
            e.dma_start(gidx[0:GROUPS_GU, 0:DM].bitcast(I32), gi_gu.partition_broadcast(GROUPS_GU)).then_inc(S["gi_loaded"], 16)
            e.wait_ge(S["prep_done"], 1)
            e.dma_start(gidx[0:GROUPS_D, :].bitcast(I32), gi_d.partition_broadcast(GROUPS_D)).then_inc(S["gi_loaded"], 16)
            e.dma_start(zraw[0:GROUPS_D, 0:DM // 8], qz_d).then_inc(S["gi_loaded"], 16)
            e.wait_ge(S["d_int"], 3 * KB)
            whole = FB - 1
            tail_rows = (INTER - whole * P) // 8
            for s in range(8):
                rows(qw_d, qw_st[0], s, 0, whole, 16, 0, DM, DM, "qwd_loaded")
                e.dma_start(bass.AP(qw_st[0].tensor, qw_st[0][s:s + 1].offset + whole * DM, [[qw_st[0].ap[0][0] * 8, tail_rows], [1, DM]]),
                            bass.AP(qw_d.tensor, qw_d.offset + whole * 16 * DM, [[DM, tail_rows], [1, DM]])
                            ).then_inc(S["qwd_loaded"], 16)

        GU_COLS = [(0, 512), (512, 512), (1024, 352)]
        dequant_units = [(kb, half, c0, n) for half in range(2) for kb in range(KB) for c0, n in GU_COLS]
        ND = len(dequant_units)

        def pe_setup(e):
            e.wait_ge(S["w_loaded"], 64)
            e.wait_ge(S["t_ready"], 1)
            e.wait_ge(S["pool_const"], 1)
            for w in range(4):
                banks = bank[4 * (w % 2):4 * (w % 2) + 4]
                reached(e, S["fold_evicted"], w - 1)
                for cb in range(KB):
                    for g in range(KB):
                        if w < 3:
                            mm = e.matmul(banks[cb][:, g * P:(g + 1) * P], wraw[:, w, g, cb * P:(cb + 1) * P],
                                          tmat[:, g, :], start=True, stop=True)
                        else:
                            if cb == 0 and g == 0:
                                e.wait_ge(S["wo_permuted"], 1)
                            mm = e.transpose(banks[cb][:, g * P:(g + 1) * P], wop[g][:, cb * P:(cb + 1) * P], ident[:, :])
                mm.then_inc(S["fold_done"], 1)
            e.wait_ge(S["fold_evicted"], 4)
            e.wait_ge(S["const_loaded"], 16 * 21)
            for i in range(2):
                for g in range(KB):
                    mm = e.matmul(bank[0][:, 4 * i + g:4 * i + g + 1], tmat[:, g, :], BQR[:, 4 * i + g:4 * i + g + 1],
                                  start=True, stop=True)
            e.wait_ge(S["t_ready"], 2)
            for g in range(KB):
                mm = e.matmul(bank[1][:, g * P:(g + 1) * P], bvx[:, g * P:(g + 1) * P], tmat[:, g, :],
                              start=True, stop=True)
            mm.then_inc(S["bias_done"], 1)
            e.wait_ge(S["prep_done"], 1)
            for n, (kb, half, c0, cols) in enumerate(dequant_units):
                gather(e, n, hot_gu[0:GROUPS_GU, kb * P:(kb + 1) * P],
                       scgu[0:GROUPS_GU, half * INTER + c0:half * INTER + c0 + cols],
                       zgu[0:GROUPS_GU, half * INTER + c0:half * INTER + c0 + cols], P, cols)
            e.wait_ge(S["prep_done"], 2)
            for fb in range(FB):
                m = width(fb)
                gather(e, ND + fb, hot_d[0:GROUPS_D, fb * P:fb * P + m], scd[0:GROUPS_D, :], zd[0:GROUPS_D, :], m, DM)

        def gather(e, n, hot, scales, zeros, rows, cols):
            reached(e, S["d_w"], n - 1)
            e.matmul(bank[2 + 2 * (n % 2)][0:rows, 0:cols], hot, zeros, start=True, stop=True)
            e.matmul(bank[3 + 2 * (n % 2)][0:rows, 0:cols], hot, scales, start=True, stop=True).then_inc(S["sczu_done"], 1)

        def t_free(e, c, name):
            n = t_at(c, name)
            reached(e, S["t_hi"], n - 2)
            reached(e, S["t_lo"], n - 2)
            return TB[(T_ORDER.index(name)) % 2]

        def pe_transpose_tiles(e, c, kind, src, ready, count):
            for t in range(TILES):
                name = f"{kind}{t}"
                tb = t_free(e, c, name)
                e.wait_ge(ready, count(t))
                for kb in range(KB):
                    mm = e.transpose(tb[:, kb * P:(kb + 1) * P], src[:, t, kb * P:(kb + 1) * P], ident[:, :])
                mm.then_inc(S["tr_done"], 1)

        def pe_project(e, w, G, jb):
            for g2 in range(2):
                g = 2 * G + g2
                n = 0
                for kb in range(KB):
                    for sp, mp in PASSES:
                        mm = e.matmul(jb[:, g2 * TOK:(g2 + 1) * TOK], WT[:, w, sp, kb, g * P:(g + 1) * P],
                                      actT[:, mp, kb, :], start=(n == 0), stop=(n == 11))
                        n += 1
            mm.then_inc(S["proj_done"], 1)

        def pe_rows(e, w, t, jb, done):
            n = 0
            for kb in range(KB):
                for sp, mp in PASSES:
                    mm = e.matmul(jb[:, :], actT[:, sp, kb, t * P:(t + 1) * P], WT[:, w, mp, kb, :],
                                  start=(n == 0), stop=(n == 11))
                    n += 1
            mm.then_inc(done, 1)

        def pe_ffn(e, f):
            for u in range(UNITS):
                blocks = range(2 * u, min(2 * u + 2, FB))
                for half, pb in ((0, GB), (1, UB)):
                    if u >= 1:
                        e.wait_ge(S["g_freed" if half == 0 else "h_ready"], UNITS * f + u)
                    for i, fb in enumerate(blocks):
                        m = width(fb)
                        n = 0
                        for kb in range(KB):
                            for sp, mp in PASSES:
                                mm = e.matmul(pb[0:m, i * TOK:(i + 1) * TOK],
                                              WGU[:, sp, kb, half * INTER + fb * P:half * INTER + fb * P + m],
                                              x2T[:, mp, kb, :], start=(n == 0), stop=(n == 11))
                                if i == len(blocks) - 1 and n == 11:
                                    mm.then_inc(S["g_done" if half == 0 else "u_done"], 1)
                                n += 1
                                yield 1
            for t, pb in ((0, GB), (1, UB)):
                e.wait_ge(S["g_freed" if t == 0 else "h_ready"], UNITS * (f + 1))
                n = 0
                for fb in range(FB):
                    if fb % 2 == 0:
                        e.wait_ge(S["h_lo"], UNITS * f + fb // 2 + 1)
                    m = width(fb)
                    for sp, mp in PASSES:
                        mm = e.matmul(pb[:, :], hT[0:m, sp, fb, t * P:(t + 1) * P], WD[0:m, mp, fb, :],
                                      start=(n == 0), stop=(n == 3 * FB - 1))
                        n += 1
                        if n == 3 * FB:
                            mm.then_inc(S["d_done"], 1)
                        yield 2

        def pe_chunk(e, c, first=False, last=False):
            f = None if first else c - 1
            if first:
                pe_transpose_tiles(e, -1, "cT", cin, S["ctx_loaded"], lambda t: 16)
            e.wait_ge(S["t_lo"], t_at(c - 1, "cT1"))
            reached(e, S["x2_part"], 2 * c - 1)
            pe_project(e, 1, 0, JB[0])
            reached(e, S["x2_part"], 2 * c)
            pe_project(e, 1, 1, JB[1])
            if not first:
                pe_transpose_tiles(e, c, "x2T", xln, S["x2ln_ready"], lambda t: 2 * (c - 1) + t + 1)
            for t in range(TILES):
                e.wait_ge(S["qk_evicted"], 4 * c + t + 1)
                pe_rows(e, 2, t, JB[t], S["proj_done"])
            pe_transpose_tiles(e, c, "xT", xln, S["xln_ready"], lambda t: 2 * c + t + 1)
            e.wait_ge(S["t_lo"], t_at(c, "xT1"))
            for G in range(2):
                e.wait_ge(S["v_evicted"], 2 * c + G + 1)
                pe_project(e, 0, G, JB[G])

            ffn = iter(()) if first else pe_ffn(e, f)
            total = 12 * 2 * FB + 2 * 2 * 3 * FB
            spent, due = [0], [0]

            def ffn_slice():
                due[0] += 1
                while spent[0] < total * due[0] / SLICES:
                    cost = next(ffn, None)
                    if cost is None:
                        break
                    spent[0] += cost

            for step in range(STEPS):
                if step < SLOTS:
                    s = step
                    if s == 0:
                        e.wait_ge(S["k_stacked"], 512 * (c + 1))
                        e.wait_ge(S["q_stacked"], 512 * (c + 1))
                    reached(e, S["sub_done"], SLOTS * c + s - 1)
                    b, g = s // 4, s % 4
                    for i in range(4):
                        h = 4 * g + i
                        mm = e.matmul(SB[s % 2][:, i * P:(i + 1) * P], qstack[:, h, b * P:(b + 1) * P],
                                      kstack[:, h, b * P:(b + 1) * P], start=True, stop=True)
                    mm.then_inc(S["s_done"], 1)
                ffn_slice()
                if 1 <= step <= SLOTS:
                    s = step - 1
                    tb = t_free(e, c, f"pT{s}")
                    e.wait_ge(S["exp_done"], SLOTS * c + s + 1)
                    for i in range(4):
                        mm = e.transpose(tb[:, i * P:(i + 1) * P], pring[:, s % 2, i * P:(i + 1) * P], ident[:, :])
                    mm.then_inc(S["tr_done"], 1)
                ffn_slice()
                if step >= 2:
                    s = step - 2
                    b, g = s // 4, s % 4
                    if s == 0:
                        e.wait_ge(S["v_stacked"], 128 * (c + 1))
                    if s < 2:
                        e.wait_ge(S["qk_evicted"], 4 * c + 3 + s)
                    else:
                        reached(e, S["o_ready"], SLOTS * c + s - 1)
                    e.wait_ge(S["t_lo"], t_at(c, f"pT{s}"))
                    for i in range(4):
                        for part in range(2):
                            mm = e.matmul(JB[s % 2][:, i * 2 * VROW:(i + 1) * 2 * VROW], phl[:, s % 2, part, i * P:(i + 1) * P],
                                          vv[:, b, :, 4 * g + i, :], start=(part == 0), stop=(part == 1))
                    mm.then_inc(S["pv_done"], 1)
                if step == OT_STEP:
                    pe_o_transpose(e, c, 0)
            for _ in ffn:
                pass
            pe_o_transpose(e, c, 1)
            e.wait_ge(S["t_lo"], t_at(c, "oT1"))
            for t in range(TILES):
                reached(e, S["o_ready"], SLOTS * c + SLOTS - 1 + t)
                pe_rows(e, 3, t, JB[t], S["wo_done"])
            if not last:
                pe_transpose_tiles(e, c, "cT", cin, S["ctx_loaded"], lambda t: 16 * (c + 2))

        def pe_o_transpose(e, c, pair):
            tb = t_free(e, c, f"oT{pair}")
            e.wait_ge(S["o_ready"], SLOTS * c + 8 * pair + 8)
            for b2 in range(2):
                for hh in range(2):
                    k = 2 * b2 + hh
                    mm = e.transpose(tb[:, k * P:(k + 1) * P], obuf[:, b2, hh * P:(hh + 1) * P], ident[:, :])
            mm.then_inc(S["tr_done"], 1)

        def halves(name):
            tb = TB[T_ORDER.index(name) % 2]
            if name.startswith("pT"):
                s = int(name[2:])
                return tb[:, :], [phl[:, s % 2, i, :] for i in range(2)], P_SCALE
            t = int(name[-1])
            if name.startswith("oT"):
                views = []
                for b2 in range(2):
                    views.append([ap(actT[:, i], 0, P, 128 * t + 64 * b2, [(TOK, 4), (1, 64)]) for i in range(2)])
                return [ap(tb, 0, P, 256 * b2, [(64, 4), (1, 64)]) for b2 in range(2)], views, 1.0
            dst = x2T if name.startswith("x2T") else actT
            scale = SC[:, 4:5] if name.startswith("cT") else 1.0
            return (tb[:, :].rearrange("p (k t) -> p k t", k=KB),
                    [dst[:, i, :, t * P:(t + 1) * P] for i in range(2)], scale)

        def act_hi(e, c, name):
            e.wait_ge(S["tr_done"], t_at(c, name))
            src, dst, scale = halves(name)
            if name.startswith("oT"):
                for b2 in range(2):
                    ins = e.activation(dst[b2][0], src[b2], ACT.Copy)
            else:
                ins = e.activation(dst[0], src, ACT.Copy, scale=scale)
            ins.then_inc(S["t_hi"], 1)

        def dve_lo(e, c, name):
            e.wait_ge(S["t_hi"], t_at(c, name))
            src, dst, scale = halves(name)
            if name.startswith("oT"):
                for b2 in range(2):
                    ins = e.scalar_tensor_tensor(dst[b2][1], src[b2], scale, dst[b2][0], ALU.mult, ALU.subtract)
            else:
                ins = e.scalar_tensor_tensor(dst[1], src, scale, dst[0], ALU.mult, ALU.subtract)
            ins.then_inc(S["t_lo"], 1)

        def ffn_slots():
            total = 12 * 2 * FB + 2 * 2 * 3 * FB
            g, u, spent = [], [], 0
            for n in range(UNITS):
                k = 12 * min(2, FB - 2 * n)
                g.append(spent + k)
                u.append(spent + 2 * k)
                spent += 2 * k
            d = [spent + 6 * FB, spent + 12 * FB]
            where = lambda x: -(-x * SLICES // total) - 1
            return [where(v) for v in g], [where(v) for v in u], [where(v) for v in d]

        G_AT, U_AT, D_AT = ffn_slots()

        def act_setup(e):
            for w in range(4):
                e.wait_ge(S["fold_done"], w + 1)
                for cb in range(KB):
                    ins = e.activation(wraw[:, w, cb], bank[4 * (w % 2) + cb][:, :], ACT.Copy)
                ins.then_inc(S["fold_evicted"], 1)
            e.wait_ge(S["bias_done"], 1)
            e.activation(bv_row[:, :], bank[1][:, :], ACT.Copy)
            e.activation(bqk[:, :, :].rearrange("p a b -> p (a b)"), bank[0][:, 0:8], ACT.Copy).then_inc(S["bias_evicted"], 1)
            e.wait_ge(S["scale_ready"], 1)
            for w in range(4):
                e.activation(WT[:, w, 0], wraw[:, w], ACT.Copy, scale=SC[:, w:w + 1]).then_inc(S["whi_done"], 1)
            for n, (kb, half, c0, cols) in enumerate(dequant_units):
                e.wait_ge(S["d_w"], n + 1)
                e.activation(WGU[:, 0, kb, half * INTER + c0:half * INTER + c0 + cols], dq[n % 4][:, 0:cols],
                             ACT.Copy).then_inc(S["d_hi"], 1)
            for fb in range(FB):
                n = ND + fb
                m = width(fb)
                e.wait_ge(S["d_w"], n + 1)
                e.activation(WD[0:m, 0, fb, :], dq[n % 4][0:m, :], ACT.Copy).then_inc(S["d_hi"], 1)

        def act_qk(e, c, i, w, G):
            e.wait_ge(S["proj_done"], 6 * c + i + 1)
            if w == 1:
                if not (isinstance(c, int) and c == 0):
                    e.wait_ge(S["tr_done"], t_at(c - 1, f"pT{SLOTS - 2 + G}"))
            else:
                e.wait_ge(S["v_lo"], 2 * c + G + 1)
            for g2 in range(2):
                g = 2 * G + g2
                ins = e.activation(pring[:, G, g2 * TOK:(g2 + 1) * TOK], JB[G][:, g2 * TOK:(g2 + 1) * TOK], ACT.Identity,
                                   bias=bqk[:, w, g:g + 1], scale=(KQ if w == 0 else KK))
            ins.then_inc(S["qk_evicted"], 1)

        def act_ffn(e, f, slot):
            for u in range(UNITS):
                blocks = min(2, FB - 2 * u)
                m, cols = width(2 * u), blocks * TOK
                if G_AT[u] == slot:
                    e.wait_ge(S["g_done"], UNITS * f + u + 1)
                    if u >= 2:
                        e.wait_ge(S["h_lo"], UNITS * f + u - 1)
                    e.activation(hbuf[0:m, u % 2, 0:cols], GB[0:m, 0:cols], ACT.Tanh,
                                 scale=KTANH[0:m]).then_inc(S["tanh_done"], 1)
                if U_AT[u] + 1 == slot:
                    e.wait_ge(S["h_ready"], UNITS * f + u + 1)
                    e.activation(hT[0:m, 0, 2 * u:2 * u + blocks, :].rearrange("p a t -> p (a t)"),
                                 hbuf[0:m, u % 2, 0:cols], ACT.Copy).then_inc(S["h_hi"], 1)

        def act_chunk(e, c, first=False, last=False):
            f = None if first else c - 1
            if first:
                act_hi(e, -1, "cT0"), act_hi(e, -1, "cT1")
            act_qk(e, c, 0, 1, 0)
            act_qk(e, c, 1, 1, 1)
            if not first:
                act_hi(e, c, "x2T0"), act_hi(e, c, "x2T1")
            for t in range(TILES):
                e.wait_ge(S["v_evicted"], 2 * c + t + 1)
                reached(e, S["v_stacked"], 128 * c)
                e.activation(ap(vsb[:, t], 0, P, 0, [(VROW, HEADS), (HEADS * VROW, 2), (1, 16)]),
                             pring[:, t, :].rearrange("p (h q n) -> p h q n", h=HEADS, q=2), ACT.Copy).then_inc(S["v_hi"], 1)
            act_hi(e, c, "xT0"), act_hi(e, c, "xT1")
            act_qk(e, c, 4, 0, 0)
            act_qk(e, c, 5, 0, 1)
            for step in range(STEPS + 1):
                if not first:
                    act_ffn(e, f, 2 * step - 1)
                if step == OT_STEP + 1:
                    act_hi(e, c, "oT0")
                if 1 <= step <= SLOTS:
                    s = step - 1
                    reached(e, S["pv_done"], SLOTS * c + s - 1)
                    act_hi(e, c, f"pT{s}")
                if not first:
                    act_ffn(e, f, 2 * step)
                if step < SLOTS:
                    e.wait_ge(S["sub_done"], SLOTS * c + step + 1)
                    e.activation(pring[:, step % 2, :], pring[:, step % 2, :], ACT.Exp, scale=KSM).then_inc(S["exp_done"], 1)
            act_hi(e, c, "oT1")
            if not last:
                e.wait_ge(S["wo_done"], 2 * c + 2)
                act_hi(e, c, "cT0"), act_hi(e, c, "cT1")

        n_setup = [0]

        def link(e, ins):
            n_setup[0] += 1
            ins.then_inc(S["dve_setup"], 1)
            e.wait_ge(S["dve_setup"], n_setup[0])

        def dve_setup(e):
            e.memset(MX, 0.0)
            link(e, e.memset(NHALF, -0.5))
            e.wait_ge(S["pool_iv"], 1)
            link(e, e.tensor_scalar(smalli[:, 1:2], smalli[:, 0:1], 7, 2, ALU.bitwise_and, ALU.logical_shift_left))
            link(e, e.tensor_scalar(smalli[:, 2:3], smalli[:, 0:1], 3, 1, ALU.logical_shift_right, ALU.bitwise_and))
            link(e, e.tensor_scalar(smalli[:, 3:4], smalli[:, 0:1], 4, 1, ALU.logical_shift_right, ALU.bitwise_and))
            link(e, e.tensor_scalar(smalli[:, 4:5], smalli[:, 0:1], 3, None, ALU.bitwise_and))
            for k in range(2):
                for v in range(2):
                    link(e, e.tensor_scalar(MASK[:, 2 * k + v:2 * k + v + 1], smalli[:, 2 + k:3 + k], float(v), None, ALU.is_equal))
            link(e, e.tensor_copy(GID, smalli[:, 0:1]))
            link(e, e.tensor_copy(T1, smalli[:, 4:5]))
            link(e, e.tensor_scalar(eye4, eye4, T1, None, ALU.is_equal))
            e.wait_ge(S["const_loaded"], 16 * 21)
            link(e, e.tensor_scalar(T2, AMP, 0.1, None, ALU.mult))
            for g in range(KB):
                link(e, e.scalar_tensor_tensor(iv[:, 4 * g:4 * g + 4], iv[:, 4 * g:4 * g + 4], T2, eye4, ALU.mult, ALU.add))
            e.wait_ge(S["pool_const"], 2)
            for g in range(KB):
                ins = e.tensor_tensor(tmat[:, g, :].rearrange("p (a m d) -> p a m d", a=4, m=4),
                                      maskm.rearrange("p (a m d) -> p a m d", a=4, m=4),
                                      ap(iv, 0, P, 4 * g, [(0, 4), (1, 4), (0, 8)]), ALU.mult)
            ins.then_inc(S["t_ready"], 1)
            e.wait_ge(S["w_loaded"], 64)
            for g in range(KB):
                for hh in range(2):
                    for j in range(2):
                        ins = e.tensor_copy(wop[g][:, (2 * hh + j) * P:(2 * hh + j + 1) * P].rearrange("p (h q d) -> p h q d", h=8, q=2),
                                            ap(wraw[:, 3, g], 0, P, 256 * hh + j, [(32, 8), (2, 2), (4, 8)]))
            ins.then_inc(S["wo_permuted"], 1)
            e.wait_ge(S["fold_evicted"], 4)
            for w in range(4):
                e.tensor_reduce(MX[:, w:w + 1], wraw[:, w], mybir.AxisListType.XY, ALU.max, apply_absolute_value=True)
            e.wait_ge(S["fold_evicted"], 4)
            for c in range(NCHUNK):
                e.wait_ge(S[f"ctxm_loaded{c % 2}"], 16 * (c // 2 + 1))
                e.tensor_reduce(MXC[:, c:c + 1], cmax_st[:, c % 2], AX_X, ALU.max,
                                apply_absolute_value=True).then_inc(S["cmax_done"], 1)
            e.wait_ge(S["cmax_done"], NCHUNK)
            e.tensor_reduce(MX[:, 4:5], MXC, AX_X, ALU.max)
            e.wait_ge(S["sc_loaded"], 32)
            e.tensor_reduce(MX[0:GROUPS_GU, 8:9], scgu[0:GROUPS_GU, :], AX_X, ALU.max, apply_absolute_value=True)
            link(e, e.tensor_reduce(MX[0:GROUPS_D, 9:10], scd[0:GROUPS_D, :], AX_X, ALU.max, apply_absolute_value=True))
            for g in range(KB):
                ins = e.tensor_copy(bvx[:, g * P:(g + 1) * P], ap(bv_row, 0, P, g, [(0, P)]))
            ins.then_inc(S["t_ready"], 1)
            e.wait_ge(S["bias_evicted"], 1)
            e.tensor_reduce(MX[:, 5:6], bqk[:, 0, :], AX_X, ALU.max, apply_absolute_value=True)
            e.tensor_reduce(MX[:, 6:7], bqk[:, 1, :], AX_X, ALU.max, apply_absolute_value=True)
            e.tensor_reduce(MX[:, 7:8], bv_row[:, :], AX_X, ALU.max, apply_absolute_value=True).then_inc(S["max_ready"], 1)
            e.wait_ge(S["max_all"], 1)
            link(e, e.tensor_copy(BD[:, 0:5], MR[:, 0:5]))
            link(e, e.tensor_scalar(BD[:, 5:7], MR[:, 8:10], 16.0, None, ALU.mult))
            link(e, e.scalar_tensor_tensor(BD[:, 7:8], MR[:, 0:1], float(DM), MR[:, 5:6], ALU.mult, ALU.add))
            link(e, e.tensor_scalar(T1, MR[:, 4:5], float(DM), None, ALU.mult))
            link(e, e.scalar_tensor_tensor(BD[:, 8:9], MR[:, 1:2], T1, MR[:, 6:7], ALU.mult, ALU.add))
            link(e, e.scalar_tensor_tensor(BD[:, 9:10], MR[:, 2:3], T1, MR[:, 7:8], ALU.mult, ALU.add))
            link(e, e.tensor_scalar(T2, BD[:, 5:6], float(DM), None, ALU.mult))
            link(e, e.tensor_tensor(BD[:, 10:11], T2, T2, ALU.mult))
            link(e, e.tensor_scalar(BD, BD, 1e-30, None, ALU.max))
            link(e, e.tensor_scalar(PW.bitcast(I32), BD.bitcast(I32), 0x7F800000, None, ALU.bitwise_and))
            link(e, e.tensor_scalar(SC.bitcast(I32), PW.bitcast(I32), -1.0, float((254 + TOP) << 23), ALU.mult, ALU.add))
            link(e, e.tensor_scalar(IV.bitcast(I32), PW.bitcast(I32), float(-(TOP << 23)), None, ALU.add))

            def product(dst, terms, factor):
                link(e, e.tensor_scalar(dst, terms[0], factor, None, ALU.mult))
                for t in terms[1:]:
                    link(e, e.tensor_scalar(dst, dst, t, None, ALU.mult))

            sc = lambda i: SC[:, i:i + 1]
            inv = lambda i: IV[:, i:i + 1]
            product(KQ, [sc(7), inv(0)], 1.0 / LN_SCALE)
            product(KK, [sc(8), inv(1), inv(4)], 1.0)
            product(KV, [sc(9), inv(2), inv(4)], 1.0)
            product(KSM, [inv(7), inv(8)], DK ** -0.5)
            product(KWO, [inv(9), inv(3)], 1.0)
            product(KTANH, [inv(5)], 0.5 / LN_SCALE)
            product(KH, [inv(5), inv(5), sc(10)], 0.5 / LN_SCALE ** 2)
            product(KY, [inv(10), inv(6)], 1.0)
            link(e, e.tensor_scalar(bqk[:, 0, :], bqk[:, 0, :], sc(7), None, ALU.mult))
            link(e, e.tensor_scalar(bqk[:, 1, :], bqk[:, 1, :], sc(8), None, ALU.mult))
            e.tensor_scalar(bv_row[:, :], bv_row[:, :], sc(9), None, ALU.mult).then_inc(S["scale_ready"], 1)
            for w in range(4):
                e.wait_ge(S["whi_done"], w + 1)
                e.scalar_tensor_tensor(WT[:, w, 1], wraw[:, w], sc(w), WT[:, w, 0], ALU.mult, ALU.subtract).then_inc(S["wlo_done"], 1)
            def prepare(groups, rows, cols, hot, zdst, count):
                e.wait_ge(S["gi_loaded"], count)
                link(e, e.tensor_copy(hot[0:groups, 0:rows], gidx[0:groups, 0:rows].bitcast(I32)))
                link(e, e.tensor_scalar(gidx[0:groups, 0:rows], hot[0:groups, 0:rows], 0.0, float(groups), ALU.is_lt, ALU.mult))
                link(e, e.tensor_tensor(hot[0:groups, 0:rows], hot[0:groups, 0:rows], gidx[0:groups, 0:rows], ALU.add))
                link(e, e.tensor_scalar(hot[0:groups, 0:rows], hot[0:groups, 0:rows], 0.0, float(groups - 1), ALU.max, ALU.min))
                link(e, e.tensor_scalar(hot[0:groups, 0:rows], hot[0:groups, 0:rows], GID[0:groups], None, ALU.is_equal))
                e.wait_ge(S["wlo_done"], 4)
                for k in range(8):
                    ins = e.tensor_scalar(ap(zint, 0, groups, k, [(8, cols // 8)]), zraw[0:groups, 0:cols // 8], 4 * k, 15,
                                          ALU.logical_shift_right, ALU.bitwise_and)
                link(e, ins)
                e.tensor_scalar(zdst[0:groups, 0:cols], zint[0:groups, 0:cols], 1.0, None, ALU.add).then_inc(S["prep_done"], 1)

            prepare(GROUPS_GU, DM, 2 * INTER, hot_gu, zgu, 32)
            prepare(GROUPS_D, INTER, DM, hot_d, zd, 64)
            for n, (kb, half, c0, cols) in enumerate(dequant_units):
                if n == 0:
                    e.wait_ge(S["qwg_loaded"], 128)
                if half == 1 and n == ND // 2:
                    e.wait_ge(S["qwu_loaded"], 128)
                src = qw_st[half][:, kb * INTER + c0:kb * INTER + c0 + cols]
                dve_dequant(e, n, src, P, cols, SC[:, 5:6],
                            [WGU[:, i, kb, half * INTER + c0:half * INTER + c0 + cols] for i in range(2)])
            e.wait_ge(S["qwd_loaded"], 256)
            for fb in range(FB):
                m = width(fb)
                dve_dequant(e, ND + fb, qw_st[0][0:m, fb * DM:(fb + 1) * DM], m, DM, SC[0:m, 6:7],
                            [WD[0:m, i, fb, :] for i in range(2)])

        def dve_dequant(e, n, src, rows, cols, scale, dst):
            k = n % 2
            e.tensor_scalar(wint[k][0:rows, 0:cols], src, smalli[0:rows, 1:2].bitcast(U32), 15,
                            ALU.logical_shift_right, ALU.bitwise_and).then_inc(S["d_int"], 1)
            e.wait_ge(S["d_int"], n + 1)
            e.wait_ge(S["sczu_done"], n + 1)
            w = dq[n % 4][0:rows, 0:cols]
            e.tensor_tensor(w, wint[k][0:rows, 0:cols], bank[2 + 2 * k][0:rows, 0:cols], ALU.subtract).then_inc(S["d_sub"], 1)
            e.wait_ge(S["d_sub"], n + 1)
            e.scalar_tensor_tensor(w, w, scale, bank[3 + 2 * k][0:rows, 0:cols], ALU.mult, ALU.mult).then_inc(S["d_w"], 1)
            e.wait_ge(S["d_hi"], n + 1)
            e.tensor_tensor(dst[1], w, dst[0], ALU.subtract).then_inc(S["d_lo"], 1)

        def ln_stats(e, c, k, src):
            e.bn_stats(stats[:, k, :], src).then_inc(S["ln_step"], 1)
            e.wait_ge(S["ln_step"], 8 * c + 2 * k + 1)
            e.memset(T4, 0.0)
            e.bn_aggr(mv[:, k, :], stats[:, k, :]).then_inc(S["ln_step"], 1)
            e.wait_ge(S["ln_step"], 8 * c + 2 * k + 2)
            e.tensor_scalar(vareps[:, k:k + 1], mv[:, k, 1:2], EPS, LN_SCALE ** -2, ALU.add, ALU.mult).then_inc(S["ln_var"], 1)

        def ln_apply(e, c, k, src, done):
            e.wait_ge(S["ln_rstd"], 4 * c + k + 1)
            e.tensor_scalar(xln[:, k % 2, :], src, mv[:, k, 0:1], rstd[:, k:k + 1], ALU.subtract, ALU.mult).then_inc(done, 1)

        def dve_mask(e, c, n, w, G):
            e.wait_ge(S["qk_evicted"], 4 * c + n + 1)
            if w == 1:
                reached(e, S["q_stacked"], 512 * c)
            else:
                e.wait_ge(S["k_stacked"], 512 * (c + 1))
            src = pring[:, G, :].rearrange("p (n t) -> p n t", n=8)
            for v in range(2):
                mk = MASK[:, 2 * w + v:2 * w + v + 1]
                ins = e.tensor_scalar(masked[:, G, 0, :, v, :], src, mk, None, ALU.mult)
            ins.then_inc(S["m_hi"], 1)
            e.wait_ge(S["m_hi"], 4 * c + n + 1)
            for v in range(2):
                mk = MASK[:, 2 * w + v:2 * w + v + 1]
                ins = e.scalar_tensor_tensor(masked[:, G, 1, :, v, :], src, mk, masked[:, G, 0, :, v, :], ALU.mult, ALU.subtract)
            ins.then_inc(S["qm_ready"], 1)

        def dve_o(e, c, s):
            b, g = s // 4, s % 4
            jb = JB[s % 2]
            e.wait_ge(S["pv_done"], SLOTS * c + s + 1)
            k = s % 2
            for j in range(2):
                e.tensor_reduce(osum[64 * j:64 * j + 64, k, :, :], ap(jb, 64 * j, 64, 8 * j, [(VROW, 8), (1, 8), (16, 2)]), AX_X, ALU.add)
            e.reciprocal(rinv[:, k, :], ap(jb, 0, P, VROW - 1, [(VROW, 8)])).then_inc(S["o_step"], 1)
            e.wait_ge(S["o_step"], SLOTS * c + s + 1)
            if s == 8:
                e.wait_ge(S["tr_done"], t_at(c, "oT0"))
            if s == 0:
                reached(e, S["tr_done"], t_at(c - 1, "oT1") if not (isinstance(c, int) and c == 0) else 0)
            e.tensor_tensor(obuf[:, b % 2, 64 * g:64 * g + 64].rearrange("p (n d) -> p n d", n=8), osum[:, k],
                            ap(rinv, 0, P, 8 * k, [(1, 8), (0, 8)]), ALU.mult).then_inc(S["o_ready"], 1)

        def dve_ffn(e, f, slot):
            for u in range(UNITS):
                blocks = min(2, FB - 2 * u)
                m, cols = width(2 * u), blocks * TOK
                hb = hbuf[0:m, u % 2, 0:cols]
                if G_AT[u] == slot:
                    e.wait_ge(S["tanh_done"], UNITS * f + u + 1)
                    e.scalar_tensor_tensor(hb, hb, 1.0, GB[0:m, 0:cols], ALU.add, ALU.mult).then_inc(S["g_freed"], 1)
                if U_AT[u] == slot:
                    e.wait_ge(S["u_done"], UNITS * f + u + 1)
                    e.wait_ge(S["g_freed"], UNITS * f + u + 1)
                    e.scalar_tensor_tensor(hb, hb, KH[0:m], UB[0:m, 0:cols], ALU.mult, ALU.mult).then_inc(S["h_ready"], 1)
            for t in range(TILES):
                if D_AT[t] == slot:
                    e.wait_ge(S["d_done"], 2 * f + t + 1)
                    e.scalar_tensor_tensor(x2[:, t, :], (GB, UB)[t][:, :], KY, x2[:, t, :], ALU.mult, ALU.add).then_inc(S["y_ready"], 1)

        def dve_chunk(e, c, first=False, last=False):
            f = None if first else c - 1
            if first:
                dve_lo(e, -1, "cT0"), dve_lo(e, -1, "cT1")
            e.wait_ge(S["x_loaded"], 16 * (c + 1))
            for t in range(TILES):
                ln_stats(e, c, t, xin[:, t, :])
            dve_mask(e, c, 0, 1, 0)
            dve_mask(e, c, 1, 1, 1)
            if not first:
                dve_lo(e, c, "x2T0"), dve_lo(e, c, "x2T1")
            for t in range(TILES):
                e.wait_ge(S["proj_done"], 6 * c + 3 + t)
                e.scalar_tensor_tensor(pring[:, t, :], JB[t][:, :], KV, bv_row[:, :], ALU.mult, ALU.add).then_inc(S["v_evicted"], 1)
                e.wait_ge(S["v_hi"], 2 * c + t + 1)
                e.tensor_tensor(ap(vsb[:, t], 0, P, 16, [(VROW, HEADS), (HEADS * VROW, 2), (1, 16)]),
                                pring[:, t, :].rearrange("p (h q n) -> p h q n", h=HEADS, q=2),
                                ap(vsb[:, t], 0, P, 0, [(VROW, HEADS), (HEADS * VROW, 2), (1, 16)]), ALU.subtract).then_inc(S["v_lo"], 1)
            for t in range(TILES):
                if not first:
                    e.wait_ge(S["tr_done"], t_at(c, f"x2T{t}"))
                ln_apply(e, c, t, xin[:, t, :], S["xln_ready"])
            dve_lo(e, c, "xT0"), dve_lo(e, c, "xT1")
            dve_mask(e, c, 2, 0, 0)
            dve_mask(e, c, 3, 0, 1)
            for step in range(STEPS + 1):
                if step >= 3:
                    dve_o(e, c, step - 3)
                if not first:
                    dve_ffn(e, f, 2 * step - 1)
                if step < SLOTS:
                    s = step
                    src = SB[s % 2][:, :].rearrange("p (n k) -> p n k", n=8)
                    e.wait_ge(S["s_done"], SLOTS * c + s + 1)
                    e.tensor_reduce(negmax[:, s % 2, :], src, AX_X, ALU.max, negate=True).then_inc(S["max_done"], 1)
                    e.wait_ge(S["max_done"], SLOTS * c + s + 1)
                    if s >= 2:
                        e.wait_ge(S["tr_done"], t_at(c, f"pT{s - 2}"))
                    e.tensor_tensor(pring[:, s % 2, :].rearrange("p (n k) -> p n k", n=8), src,
                                    ap(negmax, 0, P, 8 * (s % 2), [(1, 8), (0, 64)]), ALU.add).then_inc(S["sub_done"], 1)
                if step == OT_STEP + 1:
                    dve_lo(e, c, "oT0")
                if 1 <= step <= SLOTS:
                    dve_lo(e, c, f"pT{step - 1}")
                if not first:
                    dve_ffn(e, f, 2 * step)
            dve_lo(e, c, "oT1")
            for t in range(TILES):
                e.wait_ge(S["wo_done"], 2 * c + t + 1)
                if not first:
                    e.wait_ge(S[f"y_stored{t}"], 16 * (f + 1))
                e.scalar_tensor_tensor(x2[:, t, :], JB[t][:, :], KWO, xin[:, t, :], ALU.mult, ALU.add).then_inc(S["x2_part"], 1)
                e.wait_ge(S["x2_part"], 2 * c + t + 1)
                e.tensor_tensor(x2[:, t, :], x2[:, t, :], bo_row[:, :], ALU.add).then_inc(S["x2_ready"], 1)
                e.wait_ge(S["x2_ready"], 2 * c + t + 1)
                ln_stats(e, c, 2 + t, x2[:, t, :])
            for t in range(TILES):
                ln_apply(e, c, 2 + t, x2[:, t, :], S["x2ln_ready"])
            if not last:
                dve_lo(e, c, "cT0"), dve_lo(e, c, "cT1")

        def pool_setup(e):
            e.iota(smalli[:, 0:1], [[0, 1]], base=0, channel_multiplier=1)
            e.iota(eye4, [[1, 4]], base=0, channel_multiplier=0, allow_small_or_imprecise_dtypes=True).then_inc(S["pool_iv"], 1)
            e.memset(ident[:, :], 0.0).then_inc(S["zero_done"], 1)
            e.memset(maskm, 1.0).then_inc(S["zero_done"], 1)
            e.wait_ge(S["zero_done"], 2)
            e.affine_select(out=ident[:, :], in_=ident[:, :], compare_op=ALU.not_equal, fill=1.0, base=0,
                            pattern=[[-1, P]], channel_multiplier=1).then_inc(S["pool_const"], 1)
            v = maskm.rearrange("p (a m d) -> p a m d", a=4, m=4)
            pat = [[-32, 4], [0, 4], [-4, 8]]
            e.affine_select(out=v, in_=v, compare_op=ALU.is_ge, fill=0.0, base=0, pattern=pat,
                            channel_multiplier=1).then_inc(S["zero_done"], 1)
            e.wait_ge(S["zero_done"], 3)
            e.affine_select(out=v, in_=v, compare_op=ALU.is_ge, fill=0.0, base=3, pattern=[[32, 4], [0, 4], [4, 8]],
                            channel_multiplier=-1).then_inc(S["pool_const"], 1)
            e.wait_ge(S["max_ready"], 1)
            e.partition_all_reduce(MR, MX, P, ABSMAX).then_inc(S["max_all"], 1)

        def pool_ln(e, c, ks):
            for k in ks:
                e.wait_ge(S["ln_var"], 4 * c + k + 1)
                e.tensor_tensor(rstd[:, k:k + 1], vareps[:, k:k + 1], NHALF, ALU.pow).then_inc(S["ln_rstd"], 1)

        def pool_ffn(e, f):
            for u in range(UNITS):
                blocks = min(2, FB - 2 * u)
                m, cols = width(2 * u), blocks * TOK
                flat = lambda i: hT[0:m, i, 2 * u:2 * u + blocks, :].rearrange("p a t -> p (a t)")
                e.wait_ge(S["h_hi"], UNITS * f + u + 1)
                e.tensor_tensor(flat(1), hbuf[0:m, u % 2, 0:cols], flat(0), ALU.subtract).then_inc(S["h_lo"], 1)

        block = stack.enter_context(nc.Block())
        ready = ["setup_pe", "setup_act", "setup_dve", "setup_pool"]
        R = {n: sem(n) for n in ready}

        @block.sync
        def _(sp):
            sync_setup(sp)
            for n in ("setup_act", "setup_dve", "setup_pe"):
                sp.wait_ge(R[n], 1)
            sp.dma_start(cin, c_d[0]).then_inc(S["ctx_loaded"], 16)
            sp.dma_start(xin, x_d[0]).then_inc(S["x_loaded"], 16)
            sync_chunk(sp, 0, first=True)
            with sp.Fori(1, NCHUNK - 1) as c:
                sync_chunk(sp, c)
            sync_chunk(sp, NCHUNK - 1, last=True)
            store(sp, NCHUNK - 1)
            for t in range(TILES):
                sp.wait_ge(S[f"y_stored{t}"], 16 * NCHUNK)

        @block.tensor
        def _(pe):
            pe_setup(pe)
            for n in ("setup_act", "setup_dve"):
                pe.wait_ge(R[n], 1)
            pe.matmul(bank[0][:, 0:1], ident[:, :], ident[:, 0:1], start=True, stop=True).then_inc(R["setup_pe"], 1)
            pe_chunk(pe, 0, first=True)
            with pe.Fori(1, NCHUNK - 1) as c:
                pe_chunk(pe, c)
            pe_chunk(pe, NCHUNK - 1, last=True)
            pe_transpose_tiles(pe, NCHUNK, "x2T", xln, S["x2ln_ready"], lambda t: 2 * (NCHUNK - 1) + t + 1)
            pe.wait_ge(S["t_lo"], t_at(NCHUNK, "x2T1"))
            for _ in pe_ffn(pe, NCHUNK - 1):
                pass

        @block.scalar
        def _(act):
            act_setup(act)
            act.activation(small[:, 83:84], small[:, 82:83], ACT.Copy).then_inc(R["setup_act"], 1)
            act.wait_ge(R["setup_pe"], 1)
            act.wait_ge(R["setup_dve"], 1)
            act_chunk(act, 0, first=True)
            with act.Fori(1, NCHUNK - 1) as c:
                act_chunk(act, c)
            act_chunk(act, NCHUNK - 1, last=True)
            act_hi(act, NCHUNK, "x2T0"), act_hi(act, NCHUNK, "x2T1")
            for slot in range(SLICES + 1):
                act_ffn(act, NCHUNK - 1, slot)

        @block.vector
        def _(dve):
            dve_setup(dve)
            dve.wait_ge(R["setup_act"], 1)
            link(dve, dve.memset(vv_words, 0.0))
            dve.memset(vsb[:, 0, :, :, VROW - 1:VROW], 1.0)
            dve.memset(vsb[:, 1, :, :, VROW - 1:VROW], 1.0).then_inc(R["setup_dve"], 1)
            dve.wait_ge(R["setup_pe"], 1)
            dve_chunk(dve, 0, first=True)
            with dve.Fori(1, NCHUNK - 1) as c:
                dve_chunk(dve, c)
            dve_chunk(dve, NCHUNK - 1, last=True)
            dve_lo(dve, NCHUNK, "x2T0"), dve_lo(dve, NCHUNK, "x2T1")
            for slot in range(SLICES + 1):
                dve_ffn(dve, NCHUNK - 1, slot)

        @block.gpsimd
        def _(pool):
            pool_setup(pool)
            pool.wait_ge(R["setup_dve"], 1)
            pool_ln(pool, 0, (0, 1, 2, 3))
            with pool.Fori(1, NCHUNK) as c:
                pool_ln(pool, c, (0, 1))
                pool_ffn(pool, c - 1)
                pool_ln(pool, c, (2, 3))
            pool_ffn(pool, NCHUNK - 1)


_INS = ["x", "ctx_4096", "L0_xattn_Wq", "L0_xattn_bq", "L0_xattn_Wk", "L0_xattn_bk", "L0_xattn_Wv", "L0_xattn_bv",
        "L0_xattn_interference", "L0_xattn_amp", "L0_xattn_Wo", "L0_xattn_bo", "L0_ffn_qweight_gu", "L0_ffn_qzeros_gu",
        "L0_ffn_scales_gu", "L0_ffn_g_idx_gu", "L0_ffn_qweight_down", "L0_ffn_qzeros_down", "L0_ffn_scales_down",
        "L0_ffn_g_idx_down"]


def kernel(**inputs):
    import numpy as np
    import concourse.bacc as bacc
    from concourse.bass_utils import run_bass_kernel_spmd

    nc = bacc.Bacc("TRN2", target_bir_lowering=False, num_devices=1)
    arrays, args = {}, []
    for name in _INS:
        a = np.ascontiguousarray(inputs[name])
        arrays[f"in_{name}"] = a
        args.append(nc.dram_tensor(f"in_{name}", a.shape, mybir.dt.from_np(a.dtype), kind="ExternalInput").ap())
    out = nc.dram_tensor("out_y", (BATCH, SEQ, DM), F32, kind="ExternalOutput").ap()
    build(nc, *args, out)
    r = run_bass_kernel_spmd(nc, [arrays], core_ids=[0])
    return r.results[0]["out_y"]
```

```python
from contextlib import ExitStack

import concourse.bass as bass
from concourse import mybir

P = 128
F32 = mybir.dt.float32
F16 = mybir.dt.float16
BF16 = mybir.dt.bfloat16
I32 = mybir.dt.int32
U32 = mybir.dt.uint32
ALU = mybir.AluOpType
ACT = mybir.ActivationFunctionType
AX_X = mybir.AxisListType.X
ABSMAX = bass.bass_isa.ReduceOp.absmax

BATCH, SEQ, DM = 32, 64, 512
HEADS, SUP, DK = 16, 4, 8
INTER, GROUPS_GU, GROUPS_D = 1376, 4, 10
EPS = 1e-5

KB = DM // P
TOK = 256
TILES = TOK // P
NCHUNK = BATCH * SEQ // TOK
NB = TOK // SEQ
SLOTS = NB * HEADS // 4
FB = (INTER + P - 1) // P
UNITS = (FB + 1) // 2
VROW = 2 * 2 * DK + 1
LN_SCALE = 64.0
P_SCALE = 4096.0
TOP = 14

PASSES = ((0, 0), (0, 1), (1, 0))

OT_STEP = 10
T_ORDER = (["x2T0", "x2T1", "xT0", "xT1"] + [f"pT{s}" for s in range(OT_STEP)] + ["oT0"]
           + [f"pT{s}" for s in range(OT_STEP, SLOTS)] + ["oT1", "cT0", "cT1"])
T_USES = len(T_ORDER)
STEPS = SLOTS + 2
SLICES = 2 * STEPS
WORDER = (1, 2, 0, 3)

GU_COLS = [(h * INTER + c0, n) for h in range(2) for c0, n in ((0, 512), (512, 512), (1024, INTER - 1024))]
PIECES = [[(kb, False, c0, n) for c0, n in GU_COLS] for kb in range(KB)]
PIECES += [[(fb, True, 0, DM) for fb in range(f0, min(f0 + 4, FB))] for f0 in range(0, FB, 4)]
DQ_UNITS = [(i, unit) for i, piece in enumerate(PIECES) for unit in piece]
ND = len(DQ_UNITS)
PARTS = 3


def width(block):
    return min(P, INTER - P * block)


def reached(engine, semaphore, value):
    if isinstance(value, int) and value <= 0:
        return
    engine.wait_ge(semaphore, value)


def build(nc, x, ctx_in, Wq, bq, Wk, bk, Wv, bv, interference, amp, Wo, bo,
          qw_gu, qz_gu, sc_gu, gi_gu, qw_d, qz_d, sc_d, gi_d, out):
    with ExitStack() as stack:
        def sb(name, shape, dt):
            return stack.enter_context(nc.sbuf_tensor(name, shape, dt))

        def sem(name):
            return stack.enter_context(nc.semaphore(name))

        WT = sb("WT", [P, 4, 2, KB, DM], F16)
        WGU = sb("WGU", [P, 2, KB, 2 * INTER], F16)
        WD = sb("WD", [P, 2, FB, DM], F16)

        ident = sb("ident", [P, P], F32)
        ident16 = sb("ident16", [P, P], BF16)
        bv_row = sb("bv_row", [P, DM], F32)
        bo_row = sb("bo_row", [P, DM], F32)
        small = sb("small", [P, 104], F32)
        smalli = sb("smalli", [P, 8], I32)
        bqk = sb("bqk", [P, 2, KB], F32)
        stats = sb("stats", [P, 4, 6], F32)
        mv = sb("mv", [P, 4, 2], F32)
        vareps = sb("vareps", [P, 4], F32)
        rstd = sb("rstd", [P, 4], F32)
        negmax = sb("negmax", [P, 2, 8], F32)
        osum = sb("osum", [P, 2, 8, DK], F32)
        rinv = sb("rinv", [P, 2, 8], F32)

        arena_bytes = 103 * 1024
        arena = sb("arena", [P, arena_bytes // 4], F32)
        at = [0]

        def carve(nbytes, dt, start=None):
            a = at[0] if start is None else start
            if start is None:
                at[0] += nbytes
            assert a % 4 == 0 and nbytes % 4 == 0 and a + nbytes <= arena_bytes, (a, nbytes)
            v = arena[:, a // 4:(a + nbytes) // 4]
            return v if dt == F32 else v.bitcast(dt)

        xin = carve(4096, F32).rearrange("p (t n) -> p t n", t=TILES)
        cin = carve(4096, F32).rearrange("p (t n) -> p t n", t=TILES)
        actT = carve(4096, F16).rearrange("p (s k t) -> p s k t", s=2, k=KB)
        pring = carve(4096, F32).rearrange("p (r n) -> p r n", r=2)
        setup_at = at[0]
        x2 = carve(4096, F32).rearrange("p (t n) -> p t n", t=TILES)
        xln = carve(4096, F32).rearrange("p (t n) -> p t n", t=TILES)
        qm = carve(8192, F16).rearrange("p (s n v t) -> p s n v t", s=2, n=KB * NB, v=2)
        km = carve(8192, F16).rearrange("p (s n v t) -> p s n v t", s=2, n=KB * NB, v=2)
        vsb = carve(2 * 2 * HEADS * VROW * 2, F16).rearrange("p (r q h n) -> p r q h n", r=2, q=2, h=HEADS)
        vv_words = carve(NB * 2 * HEADS * VROW * 2, F32)
        vv = vv_words.bitcast(F16).rearrange("p (b q h n) -> p b q h n", b=NB, q=2, h=HEADS)
        phl = carve(4096, F16).rearrange("p (r s n) -> p r s n", r=2, s=2)
        obuf = carve(2048, F32).rearrange("p (r n) -> p r n", r=2)
        body0_end = at[0]
        x2T = carve(4096, F16).rearrange("p (s k t) -> p s k t", s=2, k=KB)
        hbuf = carve(4096, F32).rearrange("p (r n) -> p r n", r=2)
        hT = carve(FB * TOK * 2 * 2, F16).rearrange("p (s f t) -> p s f t", s=2, f=FB)

        def carver(start):
            pos = [start]

            def take(nbytes, dt):
                pos[0] += nbytes
                return carve(nbytes, dt, pos[0] - nbytes)
            return take, pos

        take, pos = carver(setup_at)
        wraw = take(32768, F32).rearrange("p (w g n) -> p w g n", w=4, g=KB)
        tmat = take(2048, F32).rearrange("p (g n) -> p g n", g=KB)
        maskm = take(512, F32)
        iv = take(64, F32)
        eye4 = take(16, F32)
        wop = [take(2048, F32) for _ in range(KB)]
        bvx = take(2048, F32)
        inter_all, inter_own, own = wop[0][:, 0:HEADS * SUP * SUP], wop[1][:, 0:HEADS * SUP * SUP], wop[2][:, 0:4 * SUP]
        take, pos = carver(max(pos[0], body0_end))
        PIECE = 2 * INTER * 4
        qw_st = [take(PIECE, U32) for _ in range(2)]
        wint = [take(DM * 4, U32) for _ in range(2)]
        wbf = [take(DM * 2, BF16) for _ in range(2)]
        dq = [take(DM * 4, F32) for _ in range(4)]
        hot_gu = take(DM * 2, BF16)
        hot_d = take(INTER * 2, BF16)
        sc3_d = take(DM * 2, BF16)
        z_d = take(DM * 2, BF16)
        WD_f = WD[:, :, :, :].rearrange("p s f n -> p (s f n)").bitcast(F32)
        WGU_f = WGU[:, :, :, :].rearrange("p s f n -> p (s f n)").bitcast(F32)

        def words(base, start, n):
            assert start + n <= base.shape[1]
            return base[:, start:start + n]
        sc3_gu = words(WD_f, 0, INTER).bitcast(BF16)
        z_gu = words(WD_f, INTER, INTER).bitcast(BF16)
        scgu = words(WD_f, 2 * INTER, 2 * INTER)
        o = [0]

        def temp(n):
            o[0] += n
            return words(WGU_f, o[0] - n, n)
        rest_gu, rest_d, scd = temp(2 * INTER), temp(DM), temp(DM)
        zint = temp(2 * INTER).bitcast(U32)
        zraw_gu, zraw_d = temp(2 * INTER // 8).bitcast(U32), temp(DM // 8).bitcast(U32)
        gidx_gu, gidx_d, hot_f = temp(DM), temp(INTER), temp(INTER)
        cmax_st = WT[:, :, :, :, :].rearrange("p w s k n -> p (w s k n)").bitcast(F32).rearrange(
            "p (c n) -> p c n", c=NCHUNK)

        bank = [stack.enter_context(nc.psum_tensor(f"bank{i}", [P, 512], F32)) for i in range(8)]
        SB, TB, JB, GB, UB = bank[0:2], bank[2:4], bank[4:6], bank[6], bank[7]

        MX = small[:, 0:10]
        MR = small[:, 10:20]
        BD = small[:, 20:31]
        PW = small[:, 31:42]
        SC = small[:, 42:53]
        IV = small[:, 53:64]
        KQ, KK, KV, KSM, KWO, KTANH, KH, KY = (small[:, 64 + i:65 + i] for i in range(8))
        T1, T2, T3, T4 = (small[:, 72 + i:73 + i] for i in range(4))
        MASK = small[:, 76:80]
        AMP = small[:, 80:81]
        GID = small[:, 81:82]
        NHALF = small[:, 82:83]
        BQR = small[:, 84:92]
        MXC = small[:, 92:92 + NCHUNK]
        GM = small[:, 100:101]

        S = {n: sem(n) for n in (
            *(f"w_loaded{w}" for w in range(4)), *(f"ctxm_loaded{c}" for c in range(NCHUNK)),
            "wo_permuted", "const_loaded", "bo_loaded", "vv_zeroed", "sc_zeroed", "sc_loaded", "qw_loaded0", "qw_loaded1", "gi_loaded",
            "pool_const", "pool_iv", "pool_setup", "dve_setup", "t_ready", "fold_done", "fold_evicted", "bias_done", "bias_evicted",
            "max_ready", "max_all", "scale_ready", "whi_done", "wlo_done", "cmax_done", "gm_ready", "ident16_ready",
            "sc_high", "sc_rest", "hot_ready", "z_ready",
            "d_int", "d_conv", "d_gathered", "d_scaled", "d_w", "d_hi", "d_lo",
            "x_loaded", "ctx_loaded", "v_stacked", "y_stored0", "y_stored1",
            "tr_done", "proj_done", "s_done", "pv_done", "wo_done", "g_done", "u_done", "d_done",
            "t_hi", "qk_evicted", "v_hi", "exp_done", "tanh_done", "h_hi",
            "t_lo", "m_hi", "qm_ready", "v_evicted", "v_lo", "max_done", "sub_done", "o_step", "o_ready",
            "x2_part", "x2_ready", "ln_step", "ln_var", "xln_ready", "x2ln_ready", "g_freed", "h_ready", "y_ready",
            "ln_rstd", "h_lo")}

        tile_rows = lambda a: a.rearrange("b s n -> (b s) n").rearrange("(c t p) n -> c p t n", p=P, t=TILES)
        x_d, c_d, y_d = tile_rows(x), tile_rows(ctx_in), tile_rows(out)

        def ap(base, part, nparts, off, dims):
            a = base[part:part + nparts]
            return bass.AP(a.tensor, a.offset + off, [list(a.ap[0])] + [list(d) for d in dims])

        def t_at(c, name):
            if name.startswith("cT") and isinstance(c, int) and c < 0:
                return int(name[2:]) + 1
            if isinstance(c, int) and c == NCHUNK:
                return t_at(c - 1, f"cT{name[-1]}")
            return c * T_USES + T_ORDER.index(name) + 1

        def v_dmas(e, c, first):
            e.wait_ge(S["v_lo"], 2 * c + 2)
            if first:
                e.wait_ge(S["vv_zeroed"], 1)
            row = HEADS * VROW
            for bb in range(2):
                for q in range(2):
                    e.dma_start(ap(vv, 64 * q, 64, (2 * bb + q) * row, [(4 * row, 2), (1, row)]),
                                ap(vsb, 64 * bb, 64, q * row, [(2 * row, 2), (1, row)])).then_inc(S["v_stacked"], 16)

        def sync_chunk(e, c, first=False, last=False):
            reached(e, S["pv_done"], SLOTS * c)
            v_dmas(e, c, first)
            if not last:
                e.wait_ge(S["tr_done"], t_at(c - 1, "cT1"))
                e.dma_start(cin, c_d[c + 1]).then_inc(S["ctx_loaded"], 16)
            if not first:
                store(e, c - 1)
            else:
                for i in range(2, len(PIECES)):
                    e.wait_ge(S["d_int"], units_before(i - 1))
                    load_piece(e, i)
            if not last:
                e.wait_ge(S["x2_ready"], 2 * c + 2)
                e.dma_start(xin, x_d[c + 1]).then_inc(S["x_loaded"], 16)

        def store(e, f):
            for t in range(TILES):
                e.wait_ge(S["y_ready"], 2 * f + t + 1)
                e.dma_start(y_d[f, :, t, :], x2[:, t, :]).then_inc(S[f"y_stored{t}"], 16)

        def sync_setup(e):
            e.dma_start(inter_all, interference.rearrange("h i j -> (h i j)").partition_broadcast(P)).then_inc(S["const_loaded"], 16)
            e.dma_start(AMP, amp.partition_broadcast(P)).then_inc(S["const_loaded"], 16)
            for i, b in enumerate((bq, bk)):
                e.dma_start(BQR[:, 4 * i:4 * i + 4], b.rearrange("(g p) -> p g", p=P), allow_slow_non_contiguous=True).then_inc(S["const_loaded"], 16)
            e.dma_start(bv_row[:, 0:KB], bv.rearrange("(g p) -> p g", p=P), allow_slow_non_contiguous=True).then_inc(S["const_loaded"], 16)
            for w in WORDER:
                e.dma_start(wraw[:, w], (Wq, Wk, Wv, Wo)[w].rearrange("(g p) n -> p g n", p=P)).then_inc(S[f"w_loaded{w}"], 16)
            e.wait_ge(S["sc_zeroed"], 1)
            for i in range(PARTS):
                e.dma_start(scgu[32 * i:32 * i + GROUPS_GU, :], sc_gu).then_inc(S["sc_loaded"], 16)
                e.dma_start(scd[32 * i:32 * i + GROUPS_D, :], sc_d).then_inc(S["sc_loaded"], 16)
            e.dma_start(zraw_gu[0:GROUPS_GU, :], qz_gu).then_inc(S["gi_loaded"], 16)
            e.dma_start(zraw_d[0:GROUPS_D, :], qz_d).then_inc(S["gi_loaded"], 16)
            e.dma_start(gidx_gu[0:96, :].bitcast(I32), gi_gu.partition_broadcast(96)).then_inc(S["gi_loaded"], 16)
            e.dma_start(gidx_d[0:96, :].bitcast(I32), gi_d.partition_broadcast(96)).then_inc(S["gi_loaded"], 16)
            for c in range(NCHUNK):
                e.dma_start(cmax_st[:, c].rearrange("p (t n) -> p t n", t=TILES), c_d[c]).then_inc(S[f"ctxm_loaded{c}"], 16)
            e.dma_start(cin, c_d[0]).then_inc(S["ctx_loaded"], 16)
            e.dma_start(xin, x_d[0]).then_inc(S["x_loaded"], 16)
            load_piece(e, 0)
            load_piece(e, 1)
            e.dma_start(bo_row[:, :], bo.partition_broadcast(P)).then_inc(S["bo_loaded"], 16)

        piece_loads = lambda i: 1 if i < KB else len(PIECES[i])

        def load_piece(e, i):
            dst = qw_st[i % 2]
            if i < KB:
                e.dma_start(dst[:, 0:2 * INTER],
                            bass.AP(qw_gu.tensor, qw_gu.offset + i * 16 * 2 * INTER, [[2 * INTER, 16], [0, 8], [1, 2 * INTER]])
                            ).then_inc(S[f"qw_loaded{i % 2}"], 16)
                return
            for k, (fb, _, _, _) in enumerate(PIECES[i]):
                m = width(fb)
                e.dma_start(dst[0:m, k * DM:(k + 1) * DM],
                            bass.AP(qw_d.tensor, qw_d.offset + fb * 16 * DM, [[DM, m // 8], [0, 8], [1, DM]])
                            ).then_inc(S[f"qw_loaded{i % 2}"], 16)

        def units_before(i):
            return sum(len(piece) for piece in PIECES[:i])

        def pe_setup(e):
            e.wait_ge(S["t_ready"], 2)
            e.wait_ge(S["pool_const"], 1)
            for i in range(2):
                for g in range(KB):
                    mm = e.matmul(bank[4][:, 4 * i + g:4 * i + g + 1], tmat[:, g, :], BQR[:, 4 * i + g:4 * i + g + 1],
                                  start=True, stop=True)
            for g in range(KB):
                mm = e.matmul(bank[5][:, g * P:(g + 1) * P], bvx[:, g * P:(g + 1) * P], tmat[:, g, :],
                              start=True, stop=True)
            mm.then_inc(S["bias_done"], 1)
            for i, w in enumerate(WORDER):
                banks = bank[4 * (i % 2):4 * (i % 2) + 4]
                e.wait_ge(S[f"w_loaded{w}"], 16)
                reached(e, S["fold_evicted"], i - 1)
                if i == 1:
                    e.wait_ge(S["bias_evicted"], 1)
                if w == 3:
                    e.wait_ge(S["wo_permuted"], 1)
                for cb in range(KB):
                    for g in range(KB):
                        if w < 3:
                            mm = e.matmul(banks[cb][:, g * P:(g + 1) * P], wraw[:, w, g, cb * P:(cb + 1) * P],
                                          tmat[:, g, :], start=True, stop=True)
                        else:
                            mm = e.transpose(banks[cb][:, g * P:(g + 1) * P], wop[g][:, cb * P:(cb + 1) * P], ident[:, :])
                mm.then_inc(S["fold_done"], 1)

        def pe_dequant(e, n):
            if not 0 <= n < ND:
                return
            _, (blk, down, c0, cols) = DQ_UNITS[n]
            m = width(blk) if down else P
            hot, z, sc3, groups = (hot_d, z_d, sc3_d, GROUPS_D) if down else (hot_gu, z_gu, sc3_gu, GROUPS_GU)
            pick = slice(blk * P, blk * P + m)
            if n == 0:
                e.wait_ge(S["hot_ready"], 2)
                e.wait_ge(S["z_ready"], 2)
                e.wait_ge(S["sc_high"], 6)
                e.wait_ge(S["ident16_ready"], 1)
            reached(e, S["d_w"], n)
            e.matmul(UB[0:m, 0:cols], hot[0:64 + groups, pick], sc3[0:64 + groups, c0:c0 + cols], start=True, stop=True)
            e.matmul(GB[0:m, 0:cols], hot[0:groups, pick], z[0:groups, c0:c0 + cols], start=True, stop=False)
            e.wait_ge(S["d_conv"], n + 1)
            e.matmul(GB[0:m, 0:cols], ident16[0:m, 0:m], wbf[n % 2][0:m, 0:cols], start=False, stop=True).then_inc(S["d_gathered"], 1)

        def t_free(e, c, name):
            n = t_at(c, name)
            reached(e, S["t_hi"], n - 2)
            reached(e, S["t_lo"], n - 2)
            return TB[(T_ORDER.index(name)) % 2]

        def pe_transpose_tiles(e, c, kind, src, ready, count):
            for t in range(TILES):
                name = f"{kind}{t}"
                tb = t_free(e, c, name)
                e.wait_ge(ready, count(t))
                for kb in range(KB):
                    mm = e.transpose(tb[:, kb * P:(kb + 1) * P], src[:, t, kb * P:(kb + 1) * P], ident[:, :])
                mm.then_inc(S["tr_done"], 1)

        def pe_project(e, w, G, jb):
            for g2 in range(2):
                g = 2 * G + g2
                n = 0
                for kb in range(KB):
                    for sp, mp in PASSES:
                        mm = e.matmul(jb[:, g2 * TOK:(g2 + 1) * TOK], WT[:, w, sp, kb, g * P:(g + 1) * P],
                                      actT[:, mp, kb, :], start=(n == 0), stop=(n == 11))
                        n += 1
            mm.then_inc(S["proj_done"], 1)

        def pe_rows(e, w, t, jb, done):
            n = 0
            for kb in range(KB):
                for sp, mp in PASSES:
                    mm = e.matmul(jb[:, :], actT[:, sp, kb, t * P:(t + 1) * P], WT[:, w, mp, kb, :],
                                  start=(n == 0), stop=(n == 11))
                    n += 1
            mm.then_inc(done, 1)

        def pe_ffn(e, f):
            for u in range(UNITS):
                blocks = range(2 * u, min(2 * u + 2, FB))
                for half, pb in ((0, GB), (1, UB)):
                    if u >= 1:
                        e.wait_ge(S["g_freed" if half == 0 else "h_ready"], UNITS * f + u)
                    for i, fb in enumerate(blocks):
                        m = width(fb)
                        n = 0
                        for kb in range(KB):
                            for sp, mp in PASSES:
                                mm = e.matmul(pb[0:m, i * TOK:(i + 1) * TOK],
                                              WGU[:, sp, kb, half * INTER + fb * P:half * INTER + fb * P + m],
                                              x2T[:, mp, kb, :], start=(n == 0), stop=(n == 11))
                                if i == len(blocks) - 1 and n == 11:
                                    mm.then_inc(S["g_done" if half == 0 else "u_done"], 1)
                                n += 1
                                yield 1
            for t, pb in ((0, GB), (1, UB)):
                e.wait_ge(S["g_freed" if t == 0 else "h_ready"], UNITS * (f + 1))
                n = 0
                for fb in range(FB):
                    if fb % 2 == 0:
                        e.wait_ge(S["h_lo"], UNITS * f + fb // 2 + 1)
                    m = width(fb)
                    for sp, mp in PASSES:
                        mm = e.matmul(pb[:, :], hT[0:m, sp, fb, t * P:(t + 1) * P], WD[0:m, mp, fb, :],
                                      start=(n == 0), stop=(n == 3 * FB - 1))
                        n += 1
                        if n == 3 * FB:
                            mm.then_inc(S["d_done"], 1)
                        yield 2

        def pe_chunk(e, c, first=False, last=False):
            f = None if first else c - 1
            if first:
                e.wait_ge(S["fold_evicted"], 4)
                pe_transpose_tiles(e, -1, "cT", cin, S["ctx_loaded"], lambda t: 16)
                e.wait_ge(S["wlo_done"], 1)
            e.wait_ge(S["t_lo"], t_at(c - 1, "cT1"))
            reached(e, S["x2_part"], 2 * c - 1)
            pe_project(e, 1, 0, JB[0])
            reached(e, S["x2_part"], 2 * c)
            pe_project(e, 1, 1, JB[1])
            if not first:
                pe_transpose_tiles(e, c, "x2T", xln, S["x2ln_ready"], lambda t: 2 * (c - 1) + t + 1)
            if first:
                e.wait_ge(S["wlo_done"], 2)
            for t in range(TILES):
                e.wait_ge(S["qk_evicted"], 4 * c + t + 1)
                pe_rows(e, 2, t, JB[t], S["proj_done"])
            pe_transpose_tiles(e, c, "xT", xln, S["xln_ready"], lambda t: 2 * c + t + 1)
            e.wait_ge(S["t_lo"], t_at(c, "xT1"))
            for G in range(2):
                e.wait_ge(S["v_evicted"], 2 * c + G + 1)
                pe_project(e, 0, G, JB[G])

            ffn = iter(()) if first else pe_ffn(e, f)
            total = 12 * 2 * FB + 2 * 2 * 3 * FB
            spent, due = [0], [0]

            def ffn_slice():
                due[0] += 1
                if first:
                    pe_dequant(e, due[0] - 2)
                    return
                while spent[0] < total * due[0] / SLICES:
                    cost = next(ffn, None)
                    if cost is None:
                        break
                    spent[0] += cost

            for step in range(STEPS):
                if step < SLOTS:
                    s = step
                    if s == 0:
                        e.wait_ge(S["qm_ready"], 4 * c + 4)
                    reached(e, S["sub_done"], SLOTS * c + s - 1)
                    b, a = s // 4, s % 4
                    rows = slice(32 * a, 32 * a + 32)
                    for i in range(KB):
                        for n, (qp, kp) in enumerate(PASSES):
                            mm = e.matmul(SB[s % 2][:, i * P:(i + 1) * P],
                                          qm[rows, qp, NB * i + b, :, :].rearrange("p v t -> p (v t)"),
                                          km[rows, kp, NB * i + b, :, :].rearrange("p v t -> p (v t)"),
                                          start=(n == 0), stop=(n == 2))
                    mm.then_inc(S["s_done"], 1)
                ffn_slice()
                if 1 <= step <= SLOTS:
                    s = step - 1
                    tb = t_free(e, c, f"pT{s}")
                    e.wait_ge(S["exp_done"], SLOTS * c + s + 1)
                    for i in range(4):
                        mm = e.transpose(tb[:, i * P:(i + 1) * P], pring[:, s % 2, i * P:(i + 1) * P], ident[:, :])
                    mm.then_inc(S["tr_done"], 1)
                ffn_slice()
                if step >= 2:
                    s = step - 2
                    b, a = s // 4, s % 4
                    if s == 0:
                        e.wait_ge(S["v_stacked"], 64 * (c + 1))
                    if s < 2:
                        e.wait_ge(S["qk_evicted"], 4 * c + 3 + s)
                    else:
                        reached(e, S["o_ready"], SLOTS * c + s - 1)
                    e.wait_ge(S["t_lo"], t_at(c, f"pT{s}"))
                    for i in range(4):
                        for part in range(2):
                            mm = e.matmul(JB[s % 2][:, i * 2 * VROW:(i + 1) * 2 * VROW], phl[:, s % 2, part, i * P:(i + 1) * P],
                                          vv[:, b, :, 4 * i + a, :], start=(part == 0), stop=(part == 1))
                    mm.then_inc(S["pv_done"], 1)
                if step == OT_STEP:
                    pe_o_transpose(e, c, 0)
            for _ in ffn:
                pass
            pe_o_transpose(e, c, 1)
            e.wait_ge(S["t_lo"], t_at(c, "oT1"))
            for t in range(TILES):
                reached(e, S["o_ready"], SLOTS * c + SLOTS - 1 + t)
                pe_rows(e, 3, t, JB[t], S["wo_done"])
            if not last:
                pe_transpose_tiles(e, c, "cT", cin, S["ctx_loaded"], lambda t: 16 * (c + 2))

        def pe_o_transpose(e, c, pair):
            tb = t_free(e, c, f"oT{pair}")
            e.wait_ge(S["o_ready"], SLOTS * c + 8 * pair + 8)
            for b2 in range(2):
                for hh in range(2):
                    k = 2 * b2 + hh
                    mm = e.transpose(tb[:, k * P:(k + 1) * P], obuf[:, b2, hh * P:(hh + 1) * P], ident[:, :])
            mm.then_inc(S["tr_done"], 1)

        def halves(name):
            tb = TB[T_ORDER.index(name) % 2]
            if name.startswith("pT"):
                s = int(name[2:])
                return tb[:, :], [phl[:, s % 2, i, :] for i in range(2)], P_SCALE
            t = int(name[-1])
            if name.startswith("oT"):
                views = []
                for b2 in range(2):
                    views.append([ap(actT[:, i], 0, P, 128 * t + 64 * b2, [(TOK, 4), (1, 64)]) for i in range(2)])
                return [ap(tb, 0, P, 256 * b2, [(64, 4), (1, 64)]) for b2 in range(2)], views, 1.0
            dst = x2T if name.startswith("x2T") else actT
            scale = SC[:, 4:5] if name.startswith("cT") else 1.0
            return (tb[:, :].rearrange("p (k t) -> p k t", k=KB),
                    [dst[:, i, :, t * P:(t + 1) * P] for i in range(2)], scale)

        def act_hi(e, c, name):
            e.wait_ge(S["tr_done"], t_at(c, name))
            src, dst, scale = halves(name)
            if name.startswith("oT"):
                for b2 in range(2):
                    ins = e.activation(dst[b2][0], src[b2], ACT.Copy)
            else:
                ins = e.activation(dst[0], src, ACT.Copy, scale=scale)
            ins.then_inc(S["t_hi"], 1)

        def dve_lo(e, c, name):
            e.wait_ge(S["t_hi"], t_at(c, name))
            src, dst, scale = halves(name)
            if name.startswith("oT"):
                for b2 in range(2):
                    ins = e.scalar_tensor_tensor(dst[b2][1], src[b2], scale, dst[b2][0], ALU.mult, ALU.subtract)
            else:
                ins = e.scalar_tensor_tensor(dst[1], src, scale, dst[0], ALU.mult, ALU.subtract)
            ins.then_inc(S["t_lo"], 1)

        def ffn_slots():
            total = 12 * 2 * FB + 2 * 2 * 3 * FB
            g, u, spent = [], [], 0
            for n in range(UNITS):
                k = 12 * min(2, FB - 2 * n)
                g.append(spent + k)
                u.append(spent + 2 * k)
                spent += 2 * k
            d = [spent + 6 * FB, spent + 12 * FB]
            where = lambda x: -(-x * SLICES // total) - 1
            return [where(v) for v in g], [where(v) for v in u], [where(v) for v in d]

        G_AT, U_AT, D_AT = ffn_slots()

        def act_setup(e):
            e.wait_ge(S["sc_loaded"], 32 * PARTS)
            def scale_part(i):
                if i > 0:
                    e.wait_ge(S["sc_rest"], 2 * i)
                for k, (dst, src) in enumerate(((sc3_gu, scgu if i == 0 else rest_gu), (sc3_d, scd if i == 0 else rest_d))):
                    e.activation(dst[0:96 - 32 * i, :], src[0:96 - 32 * i, :], ACT.Copy).then_inc(S["sc_high"], 1)

            e.wait_ge(S["bias_done"], 1)
            e.activation(bv_row[:, :], bank[5][:, :], ACT.Copy)
            e.activation(bqk[:, :, :].rearrange("p a b -> p (a b)"), bank[4][:, 0:8], ACT.Copy).then_inc(S["bias_evicted"], 1)
            for i, w in enumerate(WORDER):
                e.wait_ge(S["fold_done"], i + 1)
                for cb in range(KB):
                    ins = e.activation(wraw[:, w, cb], bank[4 * (i % 2) + cb][:, :], ACT.Copy)
                ins.then_inc(S["fold_evicted"], 1)
                if i == 1:
                    scale_part(0)
            scale_part(1)
            e.wait_ge(S["scale_ready"], 1)
            for i, w in enumerate(WORDER):
                e.activation(WT[:, w, 0], wraw[:, w], ACT.Copy, scale=SC[:, w:w + 1]).then_inc(S["whi_done"], 1)
                if i == 0:
                    act_hi(e, -1, "cT0"), act_hi(e, -1, "cT1")
            scale_part(2)

        def act_dequant_hi(e, n):
            if not 0 <= n < ND:
                return
            _, (blk, down, c0, cols) = DQ_UNITS[n]
            m = width(blk) if down else P
            dst = WD[0:m, 0, blk, :] if down else WGU[:, 0, blk, c0:c0 + cols]
            e.wait_ge(S["d_w"], n + 1)
            e.activation(dst, dq[n % 4][0:m, 0:cols], ACT.Copy).then_inc(S["d_hi"], 1)

        def act_dequant_scaled(e, n):
            if not 0 <= n < ND:
                return
            _, (blk, down, c0, cols) = DQ_UNITS[n]
            m = width(blk) if down else P
            e.wait_ge(S["d_gathered"], n + 1)
            reached(e, S["d_lo"], n - 3)
            e.activation(dq[n % 4][0:m, 0:cols], GB[0:m, 0:cols], ACT.Copy,
                         scale=SC[0:m, 6:7] if down else SC[0:m, 5:6]).then_inc(S["d_scaled"], 1)

        def act_dequant(e, k):
            act_dequant_scaled(e, k - 1)
            act_dequant_hi(e, k - 2)
            act_dequant_conv(e, k)

        def act_dequant_conv(e, n):
            if not 0 <= n < ND:
                return
            _, (blk, down, c0, cols) = DQ_UNITS[n]
            m = width(blk) if down else P
            e.wait_ge(S["d_int"], n + 1)
            reached(e, S["d_gathered"], n - 1)
            e.activation(wbf[n % 2][0:m, 0:cols], wint[n % 2][0:m, 0:cols], ACT.Copy).then_inc(S["d_conv"], 1)

        def act_qk(e, c, i, w, G):
            e.wait_ge(S["proj_done"], 6 * c + i + 1)
            if w == 1:
                if not (isinstance(c, int) and c == 0):
                    e.wait_ge(S["tr_done"], t_at(c - 1, f"pT{SLOTS - 2 + G}"))
            else:
                e.wait_ge(S["v_lo"], 2 * c + G + 1)
            for g2 in range(2):
                g = 2 * G + g2
                ins = e.activation(pring[:, G, g2 * TOK:(g2 + 1) * TOK], JB[G][:, g2 * TOK:(g2 + 1) * TOK], ACT.Identity,
                                   bias=bqk[:, w, g:g + 1], scale=(KQ if w == 0 else KK))
            ins.then_inc(S["qk_evicted"], 1)

        def act_ffn(e, f, slot):
            for u in range(UNITS):
                blocks = min(2, FB - 2 * u)
                m, cols = width(2 * u), blocks * TOK
                if G_AT[u] == slot:
                    e.wait_ge(S["g_done"], UNITS * f + u + 1)
                    if u >= 2:
                        e.wait_ge(S["h_lo"], UNITS * f + u - 1)
                    e.activation(hbuf[0:m, u % 2, 0:cols], GB[0:m, 0:cols], ACT.Tanh,
                                 scale=KTANH[0:m]).then_inc(S["tanh_done"], 1)
                if U_AT[u] + 1 == slot:
                    e.wait_ge(S["h_ready"], UNITS * f + u + 1)
                    e.activation(hT[0:m, 0, 2 * u:2 * u + blocks, :].rearrange("p a t -> p (a t)"),
                                 hbuf[0:m, u % 2, 0:cols], ACT.Copy).then_inc(S["h_hi"], 1)

        def act_chunk(e, c, first=False, last=False):
            f = None if first else c - 1
            act_qk(e, c, 0, 1, 0)
            act_qk(e, c, 1, 1, 1)
            if not first:
                act_hi(e, c, "x2T0"), act_hi(e, c, "x2T1")
            for t in range(TILES):
                e.wait_ge(S["v_evicted"], 2 * c + t + 1)
                reached(e, S["v_stacked"], 64 * c)
                e.activation(ap(vsb[:, t], 0, P, 0, [(VROW, HEADS), (HEADS * VROW, 2), (1, 16)]),
                             pring[:, t, :].rearrange("p (h q n) -> p h q n", h=HEADS, q=2), ACT.Copy).then_inc(S["v_hi"], 1)
            act_hi(e, c, "xT0"), act_hi(e, c, "xT1")
            act_qk(e, c, 4, 0, 0)
            act_qk(e, c, 5, 0, 1)
            for step in range(STEPS + 1):
                if not first:
                    act_ffn(e, f, 2 * step - 1)
                else:
                    act_dequant(e, 2 * step - 1)
                if step == OT_STEP + 1:
                    act_hi(e, c, "oT0")
                if 1 <= step <= SLOTS:
                    s = step - 1
                    reached(e, S["pv_done"], SLOTS * c + s - 1)
                    act_hi(e, c, f"pT{s}")
                if not first:
                    act_ffn(e, f, 2 * step)
                else:
                    act_dequant(e, 2 * step)
                if step < SLOTS:
                    e.wait_ge(S["sub_done"], SLOTS * c + step + 1)
                    e.activation(pring[:, step % 2, :], pring[:, step % 2, :], ACT.Exp, scale=KSM).then_inc(S["exp_done"], 1)
            act_hi(e, c, "oT1")
            if not last:
                e.wait_ge(S["wo_done"], 2 * c + 2)
                act_hi(e, c, "cT0"), act_hi(e, c, "cT1")

        n_setup = [0]

        def link(e, ins):
            n_setup[0] += 1
            ins.then_inc(S["dve_setup"], 1)
            e.wait_ge(S["dve_setup"], n_setup[0])

        def dve_setup(e):
            e.memset(MX, 0.0)
            link(e, e.memset(NHALF, -0.5))
            e.wait_ge(S["pool_iv"], 1)
            e.tensor_scalar(smalli[:, 5:6], smalli[:, 0:1], 31, None, ALU.bitwise_and)
            e.tensor_scalar(smalli[:, 1:2], smalli[:, 0:1], 7, 2, ALU.bitwise_and, ALU.logical_shift_left)
            e.tensor_scalar(smalli[:, 2:3], smalli[:, 0:1], 3, 1, ALU.logical_shift_right, ALU.bitwise_and)
            e.tensor_scalar(smalli[:, 3:4], smalli[:, 0:1], 4, 1, ALU.logical_shift_right, ALU.bitwise_and)
            e.tensor_scalar(smalli[:, 6:7], smalli[:, 0:1], 5, 2, ALU.logical_shift_right, ALU.logical_shift_left)
            link(e, e.tensor_scalar(smalli[:, 4:5], smalli[:, 0:1], 3, None, ALU.bitwise_and))
            e.tensor_copy(GM, smalli[:, 5:6]).then_inc(S["gm_ready"], 1)
            for k in range(2):
                for v in range(2):
                    e.tensor_scalar(MASK[:, 2 * k + v:2 * k + v + 1], smalli[:, 2 + k:3 + k], float(v), None, ALU.is_equal)
            link(e, e.tensor_copy(T1, smalli[:, 4:5]))
            e.tensor_scalar(eye4, eye4, T1, None, ALU.is_equal)
            link(e, e.tensor_tensor(T3, smalli[:, 6:7], T1, ALU.add))
            link(e, e.tensor_scalar(own, own, T3, None, ALU.is_equal))
            e.wait_ge(S["const_loaded"], 16 * 5)
            link(e, e.tensor_tensor(inter_own.rearrange("p (g j n) -> p g j n", g=KB, j=SUP),
                                    ap(inter_all, 0, P, 0, [(64, KB), (1, SUP), (SUP, 16)]),
                                    ap(own, 0, P, 0, [(0, KB), (0, SUP), (1, 16)]), ALU.mult))
            link(e, e.tensor_reduce(iv, inter_own.rearrange("p (n k) -> p n k", k=16), AX_X, ALU.add))
            link(e, e.tensor_scalar(T2, AMP, 0.1, None, ALU.mult))
            for g in range(KB):
                link(e, e.scalar_tensor_tensor(iv[:, 4 * g:4 * g + 4], iv[:, 4 * g:4 * g + 4], T2, eye4, ALU.mult, ALU.add))
            e.wait_ge(S["pool_const"], 2)
            for g in range(KB):
                ins = e.tensor_tensor(tmat[:, g, :].rearrange("p (a m d) -> p a m d", a=4, m=4),
                                      maskm.rearrange("p (a m d) -> p a m d", a=4, m=4),
                                      ap(iv, 0, P, 4 * g, [(0, 4), (1, 4), (0, 8)]), ALU.mult)
            ins.then_inc(S["t_ready"], 1)
            for g in range(KB):
                ins = e.tensor_copy(bvx[:, g * P:(g + 1) * P], ap(bv_row, 0, P, g, [(0, P)]))
            ins.then_inc(S["t_ready"], 1)
            e.tensor_copy(ident16[:, :], ident[:, :]).then_inc(S["ident16_ready"], 1)
            e.wait_ge(S["w_loaded3"], 16)
            for g in range(KB):
                for hh in range(2):
                    for j in range(2):
                        ins = e.tensor_copy(wop[g][:, (2 * hh + j) * P:(2 * hh + j + 1) * P].rearrange("p (h q d) -> p h q d", h=8, q=2),
                                            ap(wraw[:, 3, g], 0, P, 256 * hh + j, [(32, 8), (2, 2), (4, 8)]))
            ins.then_inc(S["wo_permuted"], 1)
            e.wait_ge(S["gi_loaded"], 64)
            for i, (groups, cols, raw, dst) in enumerate(((GROUPS_GU, 2 * INTER, zraw_gu, z_gu), (GROUPS_D, DM, zraw_d, z_d))):
                reached(e, S["z_ready"], i)
                for k in range(8):
                    ins = e.tensor_scalar(ap(zint, 0, groups, k, [(8, cols // 8)]), raw[0:groups, :], 4 * k, 15,
                                          ALU.logical_shift_right, ALU.bitwise_and)
                link(e, ins)
                e.tensor_scalar(dst[0:groups, 0:cols], zint[0:groups, 0:cols], -1.0, -1.0, ALU.mult, ALU.add).then_inc(S["z_ready"], 1)
            e.wait_ge(S["sc_loaded"], 32 * PARTS)
            e.tensor_reduce(MX[0:GROUPS_GU, 8:9], scgu[0:GROUPS_GU, :], AX_X, ALU.max, apply_absolute_value=True)
            e.tensor_reduce(MX[0:GROUPS_D, 9:10], scd[0:GROUPS_D, :], AX_X, ALU.max, apply_absolute_value=True)
            e.wait_ge(S["bias_evicted"], 1)
            e.tensor_reduce(MX[:, 5:6], bqk[:, 0, :], AX_X, ALU.max, apply_absolute_value=True)
            e.tensor_reduce(MX[:, 6:7], bqk[:, 1, :], AX_X, ALU.max, apply_absolute_value=True)
            e.tensor_reduce(MX[:, 7:8], bv_row[:, :], AX_X, ALU.max, apply_absolute_value=True)
            for i, w in enumerate(WORDER):
                e.wait_ge(S["fold_evicted"], i + 1)
                e.tensor_reduce(MX[:, w:w + 1], wraw[:, w], mybir.AxisListType.XY, ALU.max, apply_absolute_value=True)
            for c in range(NCHUNK):
                e.wait_ge(S[f"ctxm_loaded{c}"], 16)
                ins = e.tensor_reduce(MXC[:, c:c + 1], cmax_st[:, c], AX_X, ALU.max, apply_absolute_value=True)
            link(e, ins)
            e.tensor_reduce(MX[:, 4:5], MXC, AX_X, ALU.max).then_inc(S["max_ready"], 1)
            e.wait_ge(S["x_loaded"], 16)
            for t in range(TILES):
                ln_stats(e, 0, t, xin[:, t, :])
            e.wait_ge(S["max_all"], 1)
            link(e, e.tensor_copy(BD[:, 0:5], MR[:, 0:5]))
            link(e, e.tensor_scalar(BD[:, 5:7], MR[:, 8:10], 16.0, None, ALU.mult))
            link(e, e.scalar_tensor_tensor(BD[:, 7:8], MR[:, 0:1], float(DM), MR[:, 5:6], ALU.mult, ALU.add))
            link(e, e.tensor_scalar(T1, MR[:, 4:5], float(DM), None, ALU.mult))
            link(e, e.scalar_tensor_tensor(BD[:, 8:9], MR[:, 1:2], T1, MR[:, 6:7], ALU.mult, ALU.add))
            link(e, e.scalar_tensor_tensor(BD[:, 9:10], MR[:, 2:3], T1, MR[:, 7:8], ALU.mult, ALU.add))
            link(e, e.tensor_scalar(T2, BD[:, 5:6], float(DM), None, ALU.mult))
            link(e, e.tensor_tensor(BD[:, 10:11], T2, T2, ALU.mult))
            link(e, e.tensor_scalar(BD, BD, 1e-30, None, ALU.max))
            link(e, e.tensor_scalar(PW.bitcast(I32), BD.bitcast(I32), 0x7F800000, None, ALU.bitwise_and))
            link(e, e.tensor_scalar(SC.bitcast(I32), PW.bitcast(I32), -1.0, float((254 + TOP) << 23), ALU.mult, ALU.add))
            link(e, e.tensor_scalar(IV.bitcast(I32), PW.bitcast(I32), float(-(TOP << 23)), None, ALU.add))

            def product(dst, terms, factor):
                link(e, e.tensor_scalar(dst, terms[0], factor, None, ALU.mult))
                for t in terms[1:]:
                    link(e, e.tensor_scalar(dst, dst, t, None, ALU.mult))

            sc = lambda i: SC[:, i:i + 1]
            inv = lambda i: IV[:, i:i + 1]
            product(KQ, [sc(7), inv(0)], 1.0 / LN_SCALE)
            product(KK, [sc(8), inv(1), inv(4)], 1.0)
            product(KV, [sc(9), inv(2), inv(4)], 1.0)
            product(KSM, [inv(7), inv(8)], DK ** -0.5)
            product(KWO, [inv(9), inv(3)], 1.0)
            product(KTANH, [inv(5)], 0.5 / LN_SCALE)
            product(KH, [inv(5), inv(5), sc(10)], 0.5 / LN_SCALE ** 2)
            product(KY, [inv(10), inv(6)], 1.0)
            link(e, e.tensor_scalar(bqk[:, 0, :], bqk[:, 0, :], sc(7), None, ALU.mult))
            link(e, e.tensor_scalar(bqk[:, 1, :], bqk[:, 1, :], sc(8), None, ALU.mult))
            e.tensor_scalar(bv_row[:, :], bv_row[:, :], sc(9), None, ALU.mult).then_inc(S["scale_ready"], 1)
            for i, w in enumerate(WORDER):
                e.wait_ge(S["whi_done"], i + 1)
                e.scalar_tensor_tensor(WT[:, w, 1], wraw[:, w], sc(w), WT[:, w, 0], ALU.mult, ALU.subtract).then_inc(S["wlo_done"], 1)
                if i == 0:
                    dve_lo(e, -1, "cT0"), dve_lo(e, -1, "cT1")
            e.wait_ge(S["wlo_done"], 4)
            e.memset(vsb[:, 0, :, :, VROW - 1:VROW], 1.0)
            link(e, e.memset(vsb[:, 1, :, :, VROW - 1:VROW], 1.0))

        def dve_dequant_int(e, n):
            if not 0 <= n < ND:
                return
            i, (blk, down, c0, cols) = DQ_UNITS[n]
            m = width(blk) if down else P
            if n == units_before(i):
                earlier = sum(piece_loads(k) for k in range(i % 2, i + 1, 2))
                e.wait_ge(S[f"qw_loaded{i % 2}"], 16 * earlier)
            reached(e, S["d_conv"], n - 1)
            at_col = (blk % 4) * DM if down else c0
            e.tensor_scalar(wint[n % 2][0:m, 0:cols], qw_st[i % 2][0:m, at_col:at_col + cols],
                            smalli[0:m, 1:2].bitcast(U32), 15,
                            ALU.logical_shift_right, ALU.bitwise_and).then_inc(S["d_int"], 1)

        def dve_dequant_w(e, n):
            if not 0 <= n < ND:
                return
            _, (blk, down, c0, cols) = DQ_UNITS[n]
            m = width(blk) if down else P
            w = dq[n % 4][0:m, 0:cols]
            e.wait_ge(S["d_scaled"], n + 1)
            e.tensor_tensor(w, w, UB[0:m, 0:cols], ALU.mult).then_inc(S["d_w"], 1)

        def ln_stats(e, c, k, src):
            e.bn_stats(stats[:, k, :], src).then_inc(S["ln_step"], 1)
            e.wait_ge(S["ln_step"], 8 * c + 2 * k + 1)
            e.memset(T4, 0.0)
            e.bn_aggr(mv[:, k, :], stats[:, k, :]).then_inc(S["ln_step"], 1)
            e.wait_ge(S["ln_step"], 8 * c + 2 * k + 2)
            e.tensor_scalar(vareps[:, k:k + 1], mv[:, k, 1:2], EPS, LN_SCALE ** -2, ALU.add, ALU.mult).then_inc(S["ln_var"], 1)

        def ln_apply(e, c, k, src, done):
            e.wait_ge(S["ln_rstd"], 4 * c + k + 1)
            e.tensor_scalar(xln[:, k % 2, :], src, mv[:, k, 0:1], rstd[:, k:k + 1], ALU.subtract, ALU.mult).then_inc(done, 1)

        def dve_mask(e, c, n, w, G):
            e.wait_ge(S["qk_evicted"], 4 * c + n + 1)
            if n == 0:
                reached(e, S["s_done"], SLOTS * c)
            dst = (qm, km)[w][:, :, 8 * G:8 * G + 8]
            src = pring[:, G, :].rearrange("p (n t) -> p n t", n=8)
            for v in range(2):
                mk = MASK[:, 2 * w + v:2 * w + v + 1]
                ins = e.tensor_scalar(dst[:, 0, :, v, :], src, mk, None, ALU.mult)
            ins.then_inc(S["m_hi"], 1)
            e.wait_ge(S["m_hi"], 4 * c + n + 1)
            for v in range(2):
                mk = MASK[:, 2 * w + v:2 * w + v + 1]
                ins = e.scalar_tensor_tensor(dst[:, 1, :, v, :], src, mk, dst[:, 0, :, v, :], ALU.mult, ALU.subtract)
            ins.then_inc(S["qm_ready"], 1)

        def dve_o(e, c, s):
            b, a = s // 4, s % 4
            jb = JB[s % 2]
            e.wait_ge(S["pv_done"], SLOTS * c + s + 1)
            k = s % 2
            for j in range(2):
                e.tensor_reduce(osum[64 * j:64 * j + 64, k, :, :], ap(jb, 64 * j, 64, 8 * j, [(VROW, 8), (1, 8), (16, 2)]), AX_X, ALU.add)
            e.reciprocal(rinv[:, k, :], ap(jb, 0, P, VROW - 1, [(VROW, 8)])).then_inc(S["o_step"], 1)
            e.wait_ge(S["o_step"], SLOTS * c + s + 1)
            if s == 8:
                e.wait_ge(S["tr_done"], t_at(c, "oT0"))
            if s == 0:
                reached(e, S["tr_done"], t_at(c - 1, "oT1") if not (isinstance(c, int) and c == 0) else 0)
            e.tensor_tensor(ap(obuf, 0, P, 256 * (b % 2) + 16 * a, [(64, 4), (8, 2), (1, 8)]),
                            osum[:, k].rearrange("p (h q) d -> p h q d", q=2),
                            ap(rinv, 0, P, 8 * k, [(2, 4), (1, 2), (0, 8)]), ALU.mult).then_inc(S["o_ready"], 1)

        def dve_ffn(e, f, slot):
            for u in range(UNITS):
                blocks = min(2, FB - 2 * u)
                m, cols = width(2 * u), blocks * TOK
                hb = hbuf[0:m, u % 2, 0:cols]
                if G_AT[u] == slot:
                    e.wait_ge(S["tanh_done"], UNITS * f + u + 1)
                    e.scalar_tensor_tensor(hb, hb, 1.0, GB[0:m, 0:cols], ALU.add, ALU.mult).then_inc(S["g_freed"], 1)
                if U_AT[u] == slot:
                    e.wait_ge(S["u_done"], UNITS * f + u + 1)
                    e.wait_ge(S["g_freed"], UNITS * f + u + 1)
                    e.scalar_tensor_tensor(hb, hb, KH[0:m], UB[0:m, 0:cols], ALU.mult, ALU.mult).then_inc(S["h_ready"], 1)
            for t in range(TILES):
                if D_AT[t] == slot:
                    e.wait_ge(S["d_done"], 2 * f + t + 1)
                    e.scalar_tensor_tensor(x2[:, t, :], (GB, UB)[t][:, :], KY, x2[:, t, :], ALU.mult, ALU.add).then_inc(S["y_ready"], 1)

        def dve_chunk(e, c, first=False, last=False):
            f = None if first else c - 1
            if not first:
                e.wait_ge(S["x_loaded"], 16 * (c + 1))
                for t in range(TILES):
                    ln_stats(e, c, t, xin[:, t, :])
            dve_mask(e, c, 0, 1, 0)
            dve_mask(e, c, 1, 1, 1)
            if not first:
                dve_lo(e, c, "x2T0"), dve_lo(e, c, "x2T1")
            for t in range(TILES):
                e.wait_ge(S["proj_done"], 6 * c + 3 + t)
                e.scalar_tensor_tensor(pring[:, t, :], JB[t][:, :], KV, bv_row[:, :], ALU.mult, ALU.add).then_inc(S["v_evicted"], 1)
                e.wait_ge(S["v_hi"], 2 * c + t + 1)
                e.tensor_tensor(ap(vsb[:, t], 0, P, 16, [(VROW, HEADS), (HEADS * VROW, 2), (1, 16)]),
                                pring[:, t, :].rearrange("p (h q n) -> p h q n", h=HEADS, q=2),
                                ap(vsb[:, t], 0, P, 0, [(VROW, HEADS), (HEADS * VROW, 2), (1, 16)]), ALU.subtract).then_inc(S["v_lo"], 1)
            for t in range(TILES):
                if not first:
                    e.wait_ge(S["tr_done"], t_at(c, f"x2T{t}"))
                ln_apply(e, c, t, xin[:, t, :], S["xln_ready"])
            dve_lo(e, c, "xT0"), dve_lo(e, c, "xT1")
            dve_mask(e, c, 2, 0, 0)
            dve_mask(e, c, 3, 0, 1)
            for step in range(STEPS + 1):
                if step >= 3:
                    dve_o(e, c, step - 3)
                if not first:
                    dve_ffn(e, f, 2 * step - 1)
                else:
                    dve_dequant_int(e, 2 * step - 1), dve_dequant_w(e, 2 * step - 2)
                if step < SLOTS:
                    s = step
                    src = SB[s % 2][:, :].rearrange("p (n k) -> p n k", n=8)
                    e.wait_ge(S["s_done"], SLOTS * c + s + 1)
                    e.tensor_reduce(negmax[:, s % 2, :], src, AX_X, ALU.max, negate=True).then_inc(S["max_done"], 1)
                    e.wait_ge(S["max_done"], SLOTS * c + s + 1)
                    if s >= 2:
                        e.wait_ge(S["tr_done"], t_at(c, f"pT{s - 2}"))
                    e.tensor_tensor(pring[:, s % 2, :].rearrange("p (n k) -> p n k", n=8), src,
                                    ap(negmax, 0, P, 8 * (s % 2), [(1, 8), (0, 64)]), ALU.add).then_inc(S["sub_done"], 1)
                if step == OT_STEP + 1:
                    dve_lo(e, c, "oT0")
                if 1 <= step <= SLOTS:
                    dve_lo(e, c, f"pT{step - 1}")
                if not first:
                    dve_ffn(e, f, 2 * step)
                else:
                    dve_dequant_int(e, 2 * step), dve_dequant_w(e, 2 * step - 1)
            dve_lo(e, c, "oT1")
            for t in range(TILES):
                e.wait_ge(S["wo_done"], 2 * c + t + 1)
                if not first:
                    e.wait_ge(S[f"y_stored{t}"], 16 * (f + 1))
                e.scalar_tensor_tensor(x2[:, t, :], JB[t][:, :], KWO, xin[:, t, :], ALU.mult, ALU.add).then_inc(S["x2_part"], 1)
                e.wait_ge(S["x2_part"], 2 * c + t + 1)
                if first and t == 0:
                    e.wait_ge(S["bo_loaded"], 16)
                e.tensor_tensor(x2[:, t, :], x2[:, t, :], bo_row[:, :], ALU.add).then_inc(S["x2_ready"], 1)
                e.wait_ge(S["x2_ready"], 2 * c + t + 1)
                ln_stats(e, c, 2 + t, x2[:, t, :])
            for t in range(TILES):
                ln_apply(e, c, 2 + t, x2[:, t, :], S["x2ln_ready"])
            if not last:
                dve_lo(e, c, "cT0"), dve_lo(e, c, "cT1")

        def pool_link(e, ins):
            n_pool[0] += 1
            ins.then_inc(S["pool_setup"], 1)
            e.wait_ge(S["pool_setup"], n_pool[0])

        n_pool = [0]

        def pool_setup(e):
            e.iota(smalli[:, 0:1], [[0, 1]], base=0, channel_multiplier=1)
            e.iota(own, [[1, 16]], base=0, channel_multiplier=0, allow_small_or_imprecise_dtypes=True)
            e.iota(eye4, [[1, 4]], base=0, channel_multiplier=0, allow_small_or_imprecise_dtypes=True).then_inc(S["pool_iv"], 1)
            e.memset(ident[:, :], 0.0)
            pool_link(e, e.memset(maskm, 1.0))
            e.affine_select(out=ident[:, :], in_=ident[:, :], compare_op=ALU.not_equal, fill=1.0, base=0,
                            pattern=[[-1, P]], channel_multiplier=1).then_inc(S["pool_const"], 1)
            v = maskm.rearrange("p (a m d) -> p a m d", a=4, m=4)
            pat = [[-32, 4], [0, 4], [-4, 8]]
            pool_link(e, e.affine_select(out=v, in_=v, compare_op=ALU.is_ge, fill=0.0, base=0, pattern=pat,
                                         channel_multiplier=1))
            e.affine_select(out=v, in_=v, compare_op=ALU.is_ge, fill=0.0, base=3, pattern=[[32, 4], [0, 4], [4, 8]],
                            channel_multiplier=-1).then_inc(S["pool_const"], 1)
            e.memset(scd[0:96, :], 0.0)
            e.memset(scgu[0:96, :], 0.0).then_inc(S["sc_zeroed"], 1)
            e.wait_ge(S["sc_high"], 2)
            e.tensor_tensor(rest_gu[0:96, :], scgu[0:96, :], sc3_gu[0:96, :], ALU.subtract).then_inc(S["sc_rest"], 1)
            e.tensor_tensor(rest_d[0:96, :], scd[0:96, :], sc3_d[0:96, :], ALU.subtract).then_inc(S["sc_rest"], 1)
            e.wait_ge(S["max_ready"], 1)
            e.partition_all_reduce(MR, MX, P, ABSMAX).then_inc(S["max_all"], 1)
            pool_ln(e, 0, (0, 1))
            e.wait_ge(S["sc_rest"], 2)
            e.wait_ge(S["sc_high"], 4)
            e.tensor_tensor(rest_gu[0:64, :], rest_gu[0:64, :], sc3_gu[0:64, :], ALU.subtract).then_inc(S["sc_rest"], 1)
            e.tensor_tensor(rest_d[0:64, :], rest_d[0:64, :], sc3_d[0:64, :], ALU.subtract).then_inc(S["sc_rest"], 1)
            e.wait_ge(S["gi_loaded"], 64)
            e.wait_ge(S["gm_ready"], 1)
            for groups, rows, gidx, hot in ((GROUPS_GU, DM, gidx_gu, hot_gu), (GROUPS_D, INTER, gidx_d, hot_d)):
                h, g = hot_f[0:96, 0:rows], gidx[0:96, :]
                pool_link(e, e.tensor_copy(h, g.bitcast(I32)))
                pool_link(e, e.tensor_scalar(g, h, 0.0, float(groups), ALU.is_lt, ALU.mult))
                pool_link(e, e.tensor_tensor(h, h, g, ALU.add))
                pool_link(e, e.tensor_scalar(h, h, 0.0, float(groups - 1), ALU.max, ALU.min))
                pool_link(e, e.tensor_scalar(hot[0:96, :], h, GM[0:96], None, ALU.is_equal))
            ins = e.memset(small[:, 101:102], 0.0).then_inc(S["hot_ready"], 2)
            e.wait_ge(S["wlo_done"], 4)
            e.memset(vv_words, 0.0).then_inc(S["vv_zeroed"], 1)

        def pool_dequant_lo(e):
            for n, (_, (blk, down, c0, cols)) in enumerate(DQ_UNITS):
                m = width(blk) if down else P
                hi, lo = ((WD[0:m, i, blk, :] if down else WGU[:, i, blk, c0:c0 + cols]) for i in range(2))
                e.wait_ge(S["d_hi"], n + 1)
                e.tensor_tensor(lo, dq[n % 4][0:m, 0:cols], hi, ALU.subtract).then_inc(S["d_lo"], 1)

        def pool_ln(e, c, ks):
            for k in ks:
                e.wait_ge(S["ln_var"], 4 * c + k + 1)
                e.tensor_tensor(rstd[:, k:k + 1], vareps[:, k:k + 1], NHALF, ALU.pow).then_inc(S["ln_rstd"], 1)

        def pool_ffn(e, f):
            for u in range(UNITS):
                blocks = min(2, FB - 2 * u)
                m, cols = width(2 * u), blocks * TOK
                flat = lambda i: hT[0:m, i, 2 * u:2 * u + blocks, :].rearrange("p a t -> p (a t)")
                e.wait_ge(S["h_hi"], UNITS * f + u + 1)
                e.tensor_tensor(flat(1), hbuf[0:m, u % 2, 0:cols], flat(0), ALU.subtract).then_inc(S["h_lo"], 1)

        block = stack.enter_context(nc.Block())

        @block.sync
        def _(sp):
            sync_setup(sp)
            sync_chunk(sp, 0, first=True)
            with sp.Fori(1, NCHUNK - 1) as c:
                sync_chunk(sp, c)
            sync_chunk(sp, NCHUNK - 1, last=True)
            store(sp, NCHUNK - 1)
            for t in range(TILES):
                sp.wait_ge(S[f"y_stored{t}"], 16 * NCHUNK)

        @block.tensor
        def _(pe):
            pe_setup(pe)
            pe_chunk(pe, 0, first=True)
            pe.wait_ge(S["d_lo"], ND)
            with pe.Fori(1, NCHUNK - 1) as c:
                pe_chunk(pe, c)
            pe_chunk(pe, NCHUNK - 1, last=True)
            pe_transpose_tiles(pe, NCHUNK, "x2T", xln, S["x2ln_ready"], lambda t: 2 * (NCHUNK - 1) + t + 1)
            pe.wait_ge(S["t_lo"], t_at(NCHUNK, "x2T1"))
            for _ in pe_ffn(pe, NCHUNK - 1):
                pass

        @block.scalar
        def _(act):
            act_setup(act)
            act_chunk(act, 0, first=True)
            act.wait_ge(S["d_lo"], ND)
            with act.Fori(1, NCHUNK - 1) as c:
                act_chunk(act, c)
            act_chunk(act, NCHUNK - 1, last=True)
            act_hi(act, NCHUNK, "x2T0"), act_hi(act, NCHUNK, "x2T1")
            for slot in range(SLICES + 1):
                act_ffn(act, NCHUNK - 1, slot)

        @block.vector
        def _(dve):
            dve_setup(dve)
            dve_chunk(dve, 0, first=True)
            with dve.Fori(1, NCHUNK - 1) as c:
                dve_chunk(dve, c)
            dve_chunk(dve, NCHUNK - 1, last=True)
            dve_lo(dve, NCHUNK, "x2T0"), dve_lo(dve, NCHUNK, "x2T1")
            for slot in range(SLICES + 1):
                dve_ffn(dve, NCHUNK - 1, slot)

        @block.gpsimd
        def _(pool):
            pool_setup(pool)
            pool_dequant_lo(pool)
            pool_ln(pool, 0, (2, 3))
            with pool.Fori(1, NCHUNK) as c:
                pool_ln(pool, c, (0, 1))
                pool_ffn(pool, c - 1)
                pool_ln(pool, c, (2, 3))
            pool_ffn(pool, NCHUNK - 1)


_INS = ["x", "ctx_4096", "L0_xattn_Wq", "L0_xattn_bq", "L0_xattn_Wk", "L0_xattn_bk", "L0_xattn_Wv", "L0_xattn_bv",
        "L0_xattn_interference", "L0_xattn_amp", "L0_xattn_Wo", "L0_xattn_bo", "L0_ffn_qweight_gu", "L0_ffn_qzeros_gu",
        "L0_ffn_scales_gu", "L0_ffn_g_idx_gu", "L0_ffn_qweight_down", "L0_ffn_qzeros_down", "L0_ffn_scales_down",
        "L0_ffn_g_idx_down"]


def kernel(**inputs):
    import numpy as np
    import concourse.bacc as bacc
    from concourse.bass_utils import run_bass_kernel_spmd

    nc = bacc.Bacc("TRN2", target_bir_lowering=False, num_devices=1)
    arrays, args = {}, []
    for name in _INS:
        a = np.ascontiguousarray(inputs[name])
        arrays[f"in_{name}"] = a
        args.append(nc.dram_tensor(f"in_{name}", a.shape, mybir.dt.from_np(a.dtype), kind="ExternalInput").ap())
    out = nc.dram_tensor("out_y", (BATCH, SEQ, DM), F32, kind="ExternalOutput").ap()
    build(nc, *args, out)
    r = run_bass_kernel_spmd(nc, [arrays], core_ids=[0])
    return r.results[0]["out_y"]
```

```python
from contextlib import ExitStack

import concourse.bass as bass
from concourse import mybir

P = 128
F32 = mybir.dt.float32
F16 = mybir.dt.float16
BF16 = mybir.dt.bfloat16
I32 = mybir.dt.int32
U32 = mybir.dt.uint32
ALU = mybir.AluOpType
ACT = mybir.ActivationFunctionType
AX_X = mybir.AxisListType.X
ABSMAX = bass.bass_isa.ReduceOp.absmax

BATCH, SEQ, DM = 32, 64, 512
HEADS, SUP, DK = 16, 4, 8
INTER, GROUPS_GU, GROUPS_D = 1376, 4, 10
EPS = 1e-5

KB = DM // P
TOK = 256
TILES = TOK // P
NCHUNK = BATCH * SEQ // TOK
NB = TOK // SEQ
SLOTS = NB * HEADS // 4
FB = (INTER + P - 1) // P
UNITS = (FB + 1) // 2
VROW = 2 * 2 * DK + 1
LN_SCALE = 64.0
P_SCALE = 4096.0
TOP = 14

PASSES = ((0, 0), (0, 1), (1, 0))

EXTRA = {8: "cT0", 10: "cT1", 12: "xT0", 14: "xT1", 15: "oT0"}
T_ORDER = ["x2T0", "x2T1"]
for _s in range(SLOTS):
    T_ORDER.append(f"pT{_s}")
    if _s + 1 in EXTRA:
        T_ORDER.append(EXTRA[_s + 1])
T_ORDER.append("oT1")
T_LAST = [n for n in T_ORDER if n[0] not in "cx" or n[:2] == "x2"]
T_USES = len(T_ORDER)
T_BEFORE = 2
STEPS = SLOTS + 2

FFN_UNITS = 12 * 2 * FB + 2 * 2 * 3 * FB
PRE, POST = (24, 44), (20, 20)
EACH = (FFN_UNITS - sum(PRE) - sum(POST)) / (2 * STEPS)
SLICES = len(PRE) + 2 * STEPS + len(POST)
ENDS = [sum(PRE[:k + 1]) for k in range(len(PRE))]
ENDS += [sum(PRE) + EACH * (k + 1) for k in range(2 * STEPS)]
ENDS += [FFN_UNITS - sum(POST[k + 1:]) for k in range(len(POST))]
WORDER = (1, 2, 0, 3)

GU_COLS = [(h * INTER + c0, n) for h in range(2) for c0, n in ((0, 512), (512, 512), (1024, INTER - 1024))]
PIECES = [[(kb, False, c0, n) for c0, n in GU_COLS[3 * h:3 * h + 3]] for kb in range(KB) for h in range(2)]
PIECES += [[(fb, True, 0, DM) for fb in range(f0, min(f0 + 2, FB))] for f0 in range(0, FB, 2)]
DQ_UNITS = [(i, unit) for i, piece in enumerate(PIECES) for unit in piece]
ND = len(DQ_UNITS)
PARTS = 3


def width(block):
    return min(P, INTER - P * block)


def reached(engine, semaphore, value):
    if isinstance(value, int) and value <= 0:
        return
    engine.wait_ge(semaphore, value)


def build(nc, x, ctx_in, Wq, bq, Wk, bk, Wv, bv, interference, amp, Wo, bo,
          qw_gu, qz_gu, sc_gu, gi_gu, qw_d, qz_d, sc_d, gi_d, out):
    with ExitStack() as stack:
        def sb(name, shape, dt):
            return stack.enter_context(nc.sbuf_tensor(name, shape, dt))

        def sem(name):
            return stack.enter_context(nc.semaphore(name))

        WT = sb("WT", [P, 4, 2, KB, DM], F16)
        WGU = sb("WGU", [P, 2, KB, 2 * INTER], F16)
        WD = sb("WD", [P, 2, FB, DM], F16)

        ident = sb("ident", [P, P], F32)
        ident16 = sb("ident16", [P, P], BF16)
        bv_row = sb("bv_row", [P, DM], F32)
        bo_row = sb("bo_row", [P, DM], F32)
        small = sb("small", [P, 124], F32)
        maxima = sb("maxima", [P, 2, 12], F32)
        smalli = sb("smalli", [P, 8], I32)
        bqk = sb("bqk", [P, 2, KB], F32)
        stats = sb("stats", [P, 4, 6], F32)
        mv = sb("mv", [P, 4, 2], F32)
        vareps = sb("vareps", [P, 4], F32)
        rstd = sb("rstd", [P, 4], F32)
        negmax = sb("negmax", [P, 2, 8], F32)
        osum = sb("osum", [P, 2, 8, DK], F32)
        rinv = sb("rinv", [P, 2, 8], F32)

        arena_bytes = 106752
        arena = sb("arena", [P, arena_bytes // 4], F32)
        at = [0]

        def carve(nbytes, dt, start=None):
            a = at[0] if start is None else start
            if start is None:
                at[0] += nbytes
            assert a % 4 == 0 and nbytes % 4 == 0 and a + nbytes <= arena_bytes, (a, nbytes)
            v = arena[:, a // 4:(a + nbytes) // 4]
            return v if dt == F32 else v.bitcast(dt)

        xin = carve(4096, F32).rearrange("p (t n) -> p t n", t=TILES)
        cin = carve(4096, F32).rearrange("p (t n) -> p t n", t=TILES)
        cxT = carve(4096, F16).rearrange("p (s k t) -> p s k t", s=2, k=KB)
        pring = carve(4096, F32).rearrange("p (r n) -> p r n", r=2)
        setup_at = at[0]
        x2 = carve(4096, F32).rearrange("p (t n) -> p t n", t=TILES)
        xln = carve(4096, F32).rearrange("p (t n) -> p t n", t=TILES)
        km = carve(8192, F16).rearrange("p (s n v t) -> p s n v t", s=2, n=KB * NB, v=2)
        xres = carve(4096, F32).rearrange("p (t n) -> p t n", t=TILES)
        xnT = carve(4096, F16).rearrange("p (s k t) -> p s k t", s=2, k=KB)
        oxT = carve(4096, F16).rearrange("p (s k t) -> p s k t", s=2, k=KB)
        qm = carve(8192, F16).rearrange("p (s n v t) -> p s n v t", s=2, n=KB * NB, v=2)
        vsb = carve(2 * 2 * HEADS * VROW * 2, F16).rearrange("p (r q h n) -> p r q h n", r=2, q=2, h=HEADS)
        vv_words = carve(NB * 2 * HEADS * VROW * 2, F32)
        vv = vv_words.bitcast(F16).rearrange("p (b q h n) -> p b q h n", b=NB, q=2, h=HEADS)
        phl = carve(4096, F16).rearrange("p (r s n) -> p r s n", r=2, s=2)
        obuf = carve(4096, F32).rearrange("p (r n) -> p r n", r=4)
        body0_end = at[0]
        x2T = carve(4096, F16).rearrange("p (s k t) -> p s k t", s=2, k=KB)
        hbuf = carve(4096, F32).rearrange("p (r n) -> p r n", r=2)
        hT = carve(FB * TOK * 2 * 2, F16).rearrange("p (s f t) -> p s f t", s=2, f=FB)
        yout = carve(4096, F32).rearrange("p (t n) -> p t n", t=TILES)

        def carver(start):
            pos = [start]

            def take(nbytes, dt):
                pos[0] += nbytes
                return carve(nbytes, dt, pos[0] - nbytes)
            return take, pos

        take, pos = carver(setup_at)
        wraw_all = take(32768, F32).rearrange("p (w g n) -> p w g n", w=4, g=KB)
        wraw = [wraw_all[:, i] for i in (2, 1, 0, 3)]
        tmat = take(2048, F32).rearrange("p (g n) -> p g n", g=KB)
        maskm = take(512, F32)
        iv = take(64, F32)
        eye4 = take(16, F32)
        wop = [take(2048, F32) for _ in range(KB)]
        bvx = take(2048, F32)
        inter_all, inter_own, own = wop[0][:, 0:HEADS * SUP * SUP], wop[1][:, 0:HEADS * SUP * SUP], wop[2][:, 0:4 * SUP]
        take, pos = carver(max(pos[0], body0_end))
        PIECE = INTER * 4
        qw_st = [take(PIECE, U32) for _ in range(2)]
        wint = [take(DM * 4, U32) for _ in range(2)]
        wbf = [take(DM * 2, BF16) for _ in range(2)]
        dq = [take(DM * 4, F32) for _ in range(4)]
        hot_gu = take(DM * 2, BF16)
        hot_d = take(INTER * 2, BF16)
        sc3_d = take(DM * 2, BF16)
        z_d = take(DM * 2, BF16)
        WD_f = WD[:, :, :, :].rearrange("p s f n -> p (s f n)").bitcast(F32)
        WGU_f = WGU[:, :, :, :].rearrange("p s f n -> p (s f n)").bitcast(F32)

        def words(base, start, n):
            assert start + n <= base.shape[1]
            return base[:, start:start + n]
        sc3_gu = words(WD_f, 0, INTER).bitcast(BF16)
        z_gu = words(WD_f, INTER, INTER).bitcast(BF16)
        scgu = words(WD_f, 2 * INTER, 2 * INTER)
        o = [0]

        def temp(n):
            o[0] += n
            return words(WGU_f, o[0] - n, n)
        rest_gu, rest_d, scd = temp(2 * INTER), temp(DM), temp(DM)
        zint = temp(2 * INTER).bitcast(U32)
        zraw_gu, zraw_d = temp(2 * INTER // 8).bitcast(U32), temp(DM // 8).bitcast(U32)
        gidx_gu, gidx_d, hot_f = temp(DM), temp(INTER), temp(INTER)
        cmax_st = WT[:, :, :, :, :].rearrange("p w s k n -> p (w s k n)").bitcast(F32).rearrange(
            "p (c n) -> p c n", c=NCHUNK)

        bank = [stack.enter_context(nc.psum_tensor(f"bank{i}", [P, 512], F32)) for i in range(8)]
        SB, TB, JB, GB, UB = bank[0:2], bank[2:4], bank[4:6], bank[6], bank[7]

        MX = maxima[:, 0, 0:11]
        MR = maxima[:, 1, 0:11]
        BD = small[:, 20:31]
        PW = small[:, 31:42]
        SC = small[:, 42:53]
        IV = small[:, 53:64]
        KQ, KK, KV, KSM, KWO, KTANH, KH, KY = (small[:, 64 + i:65 + i] for i in range(8))
        T1, T2, T3, T4 = (small[:, 72 + i:73 + i] for i in range(4))
        MASK = small[:, 76:80]
        AMP = small[:, 80:81]
        NHALF = small[:, 82:83]
        BQR = small[:, 84:92]
        MXC = small[:, 92:92 + NCHUNK]
        KMASK = small[:, 104:108]
        BMASK = small[:, 108:124].rearrange("p (w v k) -> p w v k", w=2, v=2)
        GM = small[:, 100:101]

        S = {n: sem(n) for n in (
            *(f"w_loaded{w}" for w in range(4)), *(f"ctxm_loaded{c}" for c in range(NCHUNK)),
            "const_loaded", "bo_loaded", "sc_loaded", "gi_loaded", "z_loaded", "qw_loaded0", "qw_loaded1",
            "pool_const", "pool_iv", "pool_setup", "dve_setup", "gm_ready", "ident16_ready", "vv_zeroed", "sc_zeroed",
            "t_ready", "wmax_done", "wo_permuted", "fold_done", "fold_evicted", "bias_done", "bias_evicted",
            "max_ready", "max_all", "scale_ready", "whi_done", "wlo_done",
            "sc_high", "sc_rest", "hot_ready", "z_ready",
            "d_int", "d_conv", "d_gathered", "d_scaled", "d_w", "d_hi", "d_lo",
            "x_loaded", "ctx_loaded", "v_stacked", "y_stored0", "y_stored1",
            "tr_done", "proj_done", "s_done", "pv_done", "wo_done", "g_done", "u_done", "d_done",
            "t_hi", "t_lo", "qk_evicted", "qm_ready", "v_evicted", "v_hi", "v_lo",
            "s_copied", "max_done", "sub_done", "exp_done", "o_step", "o_ready",
            "xres_ready", "x2_part", "lnx_step", "lny_step", "lnx_var", "lny_var", "lnx_rstd", "lny_rstd",
            "xln_ready", "x2ln_ready",
            "tanh_done", "g_freed", "h_ready", "h_hi", "h_lo", "y_ready")}

        tile_rows = lambda a: a.rearrange("b s n -> (b s) n").rearrange("(c t p) n -> c p t n", p=P, t=TILES)
        x_d, c_d, y_d = tile_rows(x), tile_rows(ctx_in), tile_rows(out)

        def ap(base, part, nparts, off, dims):
            a = base[part:part + nparts]
            return bass.AP(a.tensor, a.offset + off, [list(a.ap[0])] + [list(d) for d in dims])

        is_last = lambda c: isinstance(c, int) and c == NCHUNK - 1

        def t_index(c, name):
            if isinstance(c, int) and c < 0:
                return int(name[-1])
            return (T_LAST if is_last(c) else T_ORDER).index(name)

        def t_at(c, name):
            if isinstance(c, int) and c < 0:
                return int(name[-1]) + (1 if name[0] == "c" else 3)
            if isinstance(c, int) and c == NCHUNK:
                return T_BEFORE + (NCHUNK - 1) * T_USES + len(T_LAST) + int(name[-1]) + 1
            return c * T_USES + (T_BEFORE + t_index(c, name) + 1)

        def v_dmas(e, c, first):
            e.wait_ge(S["v_lo"], 2 * c + 2)
            if first:
                e.wait_ge(S["vv_zeroed"], 1)
            row = HEADS * VROW
            for bb in range(2):
                for q in range(2):
                    e.dma_start(ap(vv, 64 * q, 64, (2 * bb + q) * row, [(4 * row, 2), (1, row)]),
                                ap(vsb, 64 * bb, 64, q * row, [(2 * row, 2), (1, row)])).then_inc(S["v_stacked"], 16)

        def sync_chunk(e, c, first=False):
            if first:
                load_ctx(e, 1)
            if not is_last(c):
                e.wait_ge(S["xres_ready"], 2 * c + 2)
                e.wait_ge(S["xln_ready"], 2 * c + 2)
                e.dma_start(xin, x_d[c + 1]).then_inc(S["x_loaded"], 16)
            reached(e, S["pv_done"], SLOTS * c)
            v_dmas(e, c, first)
            if first:
                for i in range(2, len(PIECES)):
                    e.wait_ge(S["d_int"], units_before(i - 1))
                    load_piece(e, i)
            else:
                store(e, c - 1)
                for t in range(TILES):
                    e.wait_ge(S[f"y_stored{t}"], 16 * c)
            if not isinstance(c, int) or c + 2 < NCHUNK:
                load_ctx(e, c + 2)

        def load_ctx(e, n):
            e.wait_ge(S["tr_done"], t_at(n - 2, "cT1"))
            e.dma_start(cin, c_d[n]).then_inc(S["ctx_loaded"], 16)

        def store(e, f):
            for t in range(TILES):
                e.wait_ge(S["y_ready"], 2 * f + t + 1)
                e.dma_start(y_d[f, :, t, :], yout[:, t, :]).then_inc(S[f"y_stored{t}"], 16)

        def sync_setup(e):
            e.dma_start(inter_all, interference.rearrange("h i j -> (h i j)").partition_broadcast(P)).then_inc(S["const_loaded"], 16)
            e.dma_start(AMP, amp.partition_broadcast(P)).then_inc(S["const_loaded"], 16)
            for i, b in enumerate((bq, bk)):
                e.dma_start(BQR[:, 4 * i:4 * i + 4], b.rearrange("(g p) -> p g", p=P), allow_slow_non_contiguous=True).then_inc(S["const_loaded"], 16)
            e.dma_start(bv_row[:, 0:KB], bv.rearrange("(g p) -> p g", p=P), allow_slow_non_contiguous=True).then_inc(S["const_loaded"], 16)
            e.dma_start(zraw_gu[0:GROUPS_GU, :], qz_gu).then_inc(S["z_loaded"], 16)
            e.dma_start(zraw_d[0:GROUPS_D, :], qz_d).then_inc(S["z_loaded"], 16)
            for w in WORDER:
                e.dma_start(wraw[w], (Wq, Wk, Wv, Wo)[w].rearrange("(g p) n -> p g n", p=P)).then_inc(S[f"w_loaded{w}"], 16)
                if w == WORDER[0]:
                    e.dma_start(gidx_gu[0:96, :].bitcast(I32), gi_gu.partition_broadcast(96)).then_inc(S["gi_loaded"], 16)
                    e.dma_start(gidx_d[0:96, :].bitcast(I32), gi_d.partition_broadcast(96)).then_inc(S["gi_loaded"], 16)
            e.wait_ge(S["sc_zeroed"], 1)
            for i in range(PARTS):
                e.dma_start(scgu[32 * i:32 * i + GROUPS_GU, :], sc_gu).then_inc(S["sc_loaded"], 16)
                e.dma_start(scd[32 * i:32 * i + GROUPS_D, :], sc_d).then_inc(S["sc_loaded"], 16)
            for c in range(NCHUNK):
                e.dma_start(cmax_st[:, c].rearrange("p (t n) -> p t n", t=TILES), c_d[c]).then_inc(S[f"ctxm_loaded{c}"], 16)
            e.dma_start(cin, c_d[0]).then_inc(S["ctx_loaded"], 16)
            e.dma_start(xin, x_d[0]).then_inc(S["x_loaded"], 16)
            load_piece(e, 0)
            load_piece(e, 1)
            e.dma_start(bo_row[:, :], bo.partition_broadcast(P)).then_inc(S["bo_loaded"], 16)

        is_gu = lambda i: i < 2 * KB
        piece_loads = lambda i: 1 if is_gu(i) else len(PIECES[i])

        def load_piece(e, i):
            dst = qw_st[i % 2]
            if is_gu(i):
                e.dma_start(dst[:, 0:INTER],
                            bass.AP(qw_gu.tensor, qw_gu.offset + (i // 2) * 16 * 2 * INTER + (i % 2) * INTER,
                                    [[2 * INTER, 16], [0, 8], [1, INTER]])
                            ).then_inc(S[f"qw_loaded{i % 2}"], 16)
                return
            for k, (fb, _, _, _) in enumerate(PIECES[i]):
                m = width(fb)
                e.dma_start(dst[0:m, k * DM:(k + 1) * DM],
                            bass.AP(qw_d.tensor, qw_d.offset + fb * 16 * DM, [[DM, m // 8], [0, 8], [1, DM]])
                            ).then_inc(S[f"qw_loaded{i % 2}"], 16)

        def units_before(i):
            return sum(len(piece) for piece in PIECES[:i])

        def pe_setup(e):
            e.wait_ge(S["t_ready"], 2)
            e.wait_ge(S["pool_const"], 1)
            for i in range(2):
                for g in range(KB):
                    mm = e.matmul(bank[4][:, 4 * i + g:4 * i + g + 1], tmat[:, g, :], BQR[:, 4 * i + g:4 * i + g + 1],
                                  start=True, stop=True)
            for g in range(KB):
                mm = e.matmul(bank[5][:, g * P:(g + 1) * P], bvx[:, g * P:(g + 1) * P], tmat[:, g, :],
                              start=True, stop=True)
            mm.then_inc(S["bias_done"], 1)
            for i, w in enumerate(WORDER):
                banks = bank[4 * (i % 2):4 * (i % 2) + 4]
                e.wait_ge(S[f"w_loaded{w}"], 16)
                reached(e, S["fold_evicted"], i - 1)
                if i == 1:
                    e.wait_ge(S["bias_evicted"], 1)
                if w == 3:
                    e.wait_ge(S["wo_permuted"], 1)
                for cb in range(KB):
                    for g in range(KB):
                        if w < 3:
                            mm = e.matmul(banks[cb][:, g * P:(g + 1) * P], wraw[w][:, g, cb * P:(cb + 1) * P],
                                          tmat[:, g, :], start=True, stop=True)
                        else:
                            mm = e.transpose(banks[cb][:, g * P:(g + 1) * P], wop[g][:, cb * P:(cb + 1) * P], ident[:, :])
                mm.then_inc(S["fold_done"], 1)

        def pe_dequant(e, n):
            if not 0 <= n < ND:
                return
            _, (blk, down, c0, cols) = DQ_UNITS[n]
            m = width(blk) if down else P
            hot, z, sc3, groups = (hot_d, z_d, sc3_d, GROUPS_D) if down else (hot_gu, z_gu, sc3_gu, GROUPS_GU)
            pick = slice(blk * P, blk * P + m)
            if n == 0:
                e.wait_ge(S["hot_ready"], 2)
                e.wait_ge(S["z_ready"], 2)
                e.wait_ge(S["sc_high"], 6)
                e.wait_ge(S["ident16_ready"], 1)
            reached(e, S["d_w"], n)
            e.matmul(UB[0:m, 0:cols], hot[0:64 + groups, pick], sc3[0:64 + groups, c0:c0 + cols], start=True, stop=True)
            e.matmul(GB[0:m, 0:cols], hot[0:groups, pick], z[0:groups, c0:c0 + cols], start=True, stop=False)
            e.wait_ge(S["d_conv"], n + 1)
            e.matmul(GB[0:m, 0:cols], ident16[0:m, 0:m], wbf[n % 2][0:m, 0:cols], start=False, stop=True).then_inc(S["d_gathered"], 1)

        def t_free(e, c, name):
            n = t_at(c, name)
            reached(e, S["t_hi"], n - 2)
            reached(e, S["t_lo"], n - 2)
            return TB[t_index(c, name) % 2]

        def pe_transpose_tile(e, c, name, src, ready, count):
            tb = t_free(e, c, name)
            e.wait_ge(ready, count)
            t = int(name[-1])
            for kb in range(KB):
                mm = e.transpose(tb[:, kb * P:(kb + 1) * P], src[:, t, kb * P:(kb + 1) * P], ident[:, :])
            mm.then_inc(S["tr_done"], 1)

        def pe_extra(e, c, name):
            if name[0] == "o":
                pe_o_transpose(e, c, 0)
            elif not is_last(c):
                src, ready, count = (cin, S["ctx_loaded"], 16 * (c + 2)) if name[0] == "c" else (
                    xln, S["xln_ready"], 2 * (c + 1) + int(name[-1]) + 1)
                pe_transpose_tile(e, c, name, src, ready, count)

        def pe_project(e, w, G, jb, src):
            for g2 in range(2):
                g = 2 * G + g2
                n = 0
                for kb in range(KB):
                    for sp, mp in PASSES:
                        mm = e.matmul(jb[:, g2 * TOK:(g2 + 1) * TOK], WT[:, w, sp, kb, g * P:(g + 1) * P],
                                      src[:, mp, kb, :], start=(n == 0), stop=(n == 11))
                        n += 1
            mm.then_inc(S["proj_done"], 1)

        def pe_rows(e, w, t, jb, src, done):
            n = 0
            for kb in range(KB):
                for sp, mp in PASSES:
                    mm = e.matmul(jb[:, :], src[:, sp, kb, t * P:(t + 1) * P], WT[:, w, mp, kb, :],
                                  start=(n == 0), stop=(n == 11))
                    n += 1
            mm.then_inc(done, 1)

        def pe_ffn(e, f):
            for u in range(UNITS):
                blocks = range(2 * u, min(2 * u + 2, FB))
                for half, pb in ((0, GB), (1, UB)):
                    if u >= 1:
                        e.wait_ge(S["g_freed" if half == 0 else "h_ready"], UNITS * f + u)
                    for i, fb in enumerate(blocks):
                        m = width(fb)
                        n = 0
                        for kb in range(KB):
                            for sp, mp in PASSES:
                                mm = e.matmul(pb[0:m, i * TOK:(i + 1) * TOK],
                                              WGU[:, sp, kb, half * INTER + fb * P:half * INTER + fb * P + m],
                                              x2T[:, mp, kb, :], start=(n == 0), stop=(n == 11))
                                if i == len(blocks) - 1 and n == 11:
                                    mm.then_inc(S["g_done" if half == 0 else "u_done"], 1)
                                n += 1
                                yield 1
            for t, pb in ((0, GB), (1, UB)):
                e.wait_ge(S["g_freed" if t == 0 else "h_ready"], UNITS * (f + 1))
                n = 0
                for fb in range(FB):
                    if fb % 2 == 0:
                        e.wait_ge(S["h_lo"], UNITS * f + fb // 2 + 1)
                    m = width(fb)
                    for sp, mp in PASSES:
                        mm = e.matmul(pb[:, :], hT[0:m, sp, fb, t * P:(t + 1) * P], WD[0:m, mp, fb, :],
                                      start=(n == 0), stop=(n == 3 * FB - 1))
                        n += 1
                        if n == 3 * FB:
                            mm.then_inc(S["d_done"], 1)
                        yield 2

        def pe_chunk(e, c, first=False, last=False):
            f = None if first else c - 1
            ffn = iter(()) if first else pe_ffn(e, f)
            spent, k = [0], [0]

            def ffn_slice():
                k[0] += 1
                if first:
                    pe_dequant(e, k[0] - 2 - len(PRE))
                    return
                while spent[0] < ENDS[k[0] - 1] - 1e-6:
                    cost = next(ffn, None)
                    if cost is None:
                        break
                    spent[0] += cost

            if first:
                e.wait_ge(S["fold_evicted"], 4)
                for t in range(TILES):
                    pe_transpose_tile(e, -1, f"cT{t}", cin, S["ctx_loaded"], 16)
                e.wait_ge(S["wlo_done"], 1)
                e.wait_ge(S["t_lo"], t_at(-1, "cT1"))
            reached(e, S["x2_part"], 2 * c - 1)
            pe_project(e, 1, 0, JB[0], cxT)
            reached(e, S["x2_part"], 2 * c)
            pe_project(e, 1, 1, JB[1], cxT)
            if first:
                e.wait_ge(S["wlo_done"], 2)
            for t in range(TILES):
                e.wait_ge(S["qk_evicted"], 4 * c + t + 1)
                pe_rows(e, 2, t, JB[t], cxT, S["proj_done"])
                if not first and t == 0:
                    for i in range(TILES):
                        pe_transpose_tile(e, c, f"x2T{i}", xln, S["x2ln_ready"], 2 * (c - 1) + i + 1)
            if first:
                for i in range(TILES):
                    pe_transpose_tile(e, -1, f"xT{i}", xln, S["xln_ready"], i + 1)
                e.wait_ge(S["wlo_done"], 3)
                e.wait_ge(S["t_lo"], t_at(-1, "xT1"))
            for G in range(2):
                e.wait_ge(S["v_evicted"], 2 * c + G + 1)
                pe_project(e, 0, G, JB[G], xnT)
                if not first and G == 0:
                    e.wait_ge(S["t_lo"], t_at(c, "x2T1"))
                ffn_slice()

            if first:
                pe_scores(e, c, 0)
                for step in range(STEPS):
                    if 1 <= step <= SLOTS:
                        pe_transpose_p(e, c, step - 1)
                    ffn_slice()
                    if step + 1 < SLOTS:
                        pe_scores(e, c, step + 1)
                    if step >= 2:
                        pe_values(e, c, step - 2)
                    ffn_slice()
                    if step in EXTRA:
                        pe_extra(e, c, EXTRA[step])
            else:
                for step in range(STEPS):
                    if step < SLOTS:
                        pe_scores(e, c, step)
                    ffn_slice()
                    if 1 <= step <= SLOTS:
                        pe_transpose_p(e, c, step - 1)
                    ffn_slice()
                    if step >= 2:
                        pe_values(e, c, step - 2)
                    if step in EXTRA:
                        pe_extra(e, c, EXTRA[step])
            ffn_slice()
            pe_o_transpose(e, c, 1)
            ffn_slice()
            e.wait_ge(S["t_lo"], t_at(c, "oT1"))
            for t in range(TILES):
                reached(e, S["o_ready"], SLOTS * c + SLOTS - 1 + t)
                pe_rows(e, 3, t, JB[t], oxT, S["wo_done"])

        def pe_scores(e, c, s):
            if s == 0:
                e.wait_ge(S["qm_ready"], 4 * c + 4)
            reached(e, S["s_copied"], SLOTS * c + s - 1)
            b, a = s // 4, s % 4
            rows = slice(32 * a, 32 * a + 32)
            for i in range(KB):
                for n, (qp, kp) in enumerate(PASSES):
                    mm = e.matmul(SB[s % 2][:, i * P:(i + 1) * P],
                                  qm[rows, qp, NB * i + b, :, :].rearrange("p v t -> p (v t)"),
                                  km[rows, kp, NB * i + b, :, :].rearrange("p v t -> p (v t)"),
                                  start=(n == 0), stop=(n == 2))
            mm.then_inc(S["s_done"], 1)

        def pe_transpose_p(e, c, s):
            tb = t_free(e, c, f"pT{s}")
            e.wait_ge(S["exp_done"], SLOTS * c + s + 1)
            for i in range(KB):
                mm = e.transpose(tb[:, i * P:(i + 1) * P], pring[:, s % 2, i * P:(i + 1) * P], ident[:, :])
            mm.then_inc(S["tr_done"], 1)

        def pe_values(e, c, s):
            b, a = s // 4, s % 4
            if s == 0:
                e.wait_ge(S["v_stacked"], 64 * (c + 1))
            if s < 2:
                e.wait_ge(S["qk_evicted"], 4 * c + 3 + s)
            else:
                reached(e, S["o_ready"], SLOTS * c + s - 1)
            e.wait_ge(S["t_lo"], t_at(c, f"pT{s}"))
            for i in range(KB):
                for part in range(2):
                    mm = e.matmul(JB[s % 2][:, i * 2 * VROW:(i + 1) * 2 * VROW], phl[:, s % 2, part, i * P:(i + 1) * P],
                                  vv[:, b, :, 4 * i + a, :], start=(part == 0), stop=(part == 1))
            mm.then_inc(S["pv_done"], 1)

        def pe_o_transpose(e, c, pair):
            tb = t_free(e, c, f"oT{pair}")
            e.wait_ge(S["o_ready"], SLOTS * c + 8 * pair + 8)
            for b2 in range(2):
                for hh in range(2):
                    k = 2 * b2 + hh
                    mm = e.transpose(tb[:, k * P:(k + 1) * P], obuf[:, 2 * pair + b2, hh * P:(hh + 1) * P], ident[:, :])
            mm.then_inc(S["tr_done"], 1)

        def halves(c, name):
            tb = TB[t_index(c, name) % 2]
            if name.startswith("pT"):
                s = int(name[2:])
                return tb[:, :], [phl[:, s % 2, i, :] for i in range(2)], P_SCALE
            t = int(name[-1])
            if name.startswith("oT"):
                views = []
                for b2 in range(2):
                    views.append([ap(oxT[:, i], 0, P, 128 * t + 64 * b2, [(TOK, 4), (1, 64)]) for i in range(2)])
                return [ap(tb, 0, P, 256 * b2, [(64, 4), (1, 64)]) for b2 in range(2)], views, 1.0
            dst = {"c": cxT, "2": x2T, "T": xnT}["c" if name[0] == "c" else name[1]]
            scale = SC[:, 4:5] if name.startswith("cT") else 1.0
            return (tb[:, :].rearrange("p (k t) -> p k t", k=KB),
                    [dst[:, i, :, t * P:(t + 1) * P] for i in range(2)], scale)

        def act_hi(e, c, name):
            e.wait_ge(S["tr_done"], t_at(c, name))
            src, dst, scale = halves(c, name)
            if name.startswith("oT"):
                for b2 in range(2):
                    ins = e.activation(dst[b2][0], src[b2], ACT.Copy)
            else:
                ins = e.activation(dst[0], src, ACT.Copy, scale=scale)
            ins.then_inc(S["t_hi"], 1)

        def dve_lo(e, c, name):
            e.wait_ge(S["t_hi"], t_at(c, name))
            src, dst, scale = halves(c, name)
            if name.startswith("oT"):
                for b2 in range(2):
                    ins = e.scalar_tensor_tensor(dst[b2][1], src[b2], scale, dst[b2][0], ALU.mult, ALU.subtract)
            else:
                ins = e.scalar_tensor_tensor(dst[1], src, scale, dst[0], ALU.mult, ALU.subtract)
            ins.then_inc(S["t_lo"], 1)

        def ffn_slots():
            g, u, spent = [], [], 0
            for n in range(UNITS):
                k = 12 * min(2, FB - 2 * n)
                g.append(spent + k)
                u.append(spent + 2 * k)
                spent += 2 * k
            d = [spent + 6 * FB, spent + 12 * FB]
            where = lambda x: min(k for k in range(SLICES) if ENDS[k] > x - 1e-6)
            return [where(v) for v in g], [where(v) for v in u], [where(v) for v in d]

        G_AT, U_AT, D_AT = ffn_slots()

        def act_setup(e):
            e.wait_ge(S["bias_done"], 1)
            e.activation(bv_row[:, :], bank[5][:, :], ACT.Copy)
            e.activation(bqk[:, :, :].rearrange("p a b -> p (a b)"), bank[4][:, 0:8], ACT.Copy).then_inc(S["bias_evicted"], 1)
            for i, w in enumerate(WORDER):
                e.wait_ge(S["fold_done"], i + 1)
                e.wait_ge(S["wmax_done"], i + 1)
                for cb in range(KB):
                    ins = e.activation(wraw[w][:, cb], bank[4 * (i % 2) + cb][:, :], ACT.Copy)
                ins.then_inc(S["fold_evicted"], 1)
                if i == 1:
                    act_scale_part(e, 0)
            e.wait_ge(S["scale_ready"], 1)
            act_whi(e, 0)
            act_hi(e, -1, "cT0"), act_hi(e, -1, "cT1")
            act_whi(e, 1)

        def act_whi(e, i):
            w = WORDER[i]
            e.activation(WT[:, w, 0], wraw[w], ACT.Copy, scale=SC[:, w:w + 1]).then_inc(S["whi_done"], 1)

        def act_scale_part(e, i):
            if i == 0:
                e.wait_ge(S["sc_loaded"], 32 * PARTS)
            else:
                e.wait_ge(S["sc_rest"], 2 * i)
            for k, (dst, src) in enumerate(((sc3_gu, scgu if i == 0 else rest_gu), (sc3_d, scd if i == 0 else rest_d))):
                e.activation(dst[0:96 - 32 * i, :], src[0:96 - 32 * i, :], ACT.Copy).then_inc(S["sc_high"], 1)

        def act_dequant_hi(e, n):
            if not 0 <= n < ND:
                return
            _, (blk, down, c0, cols) = DQ_UNITS[n]
            m = width(blk) if down else P
            dst = WD[0:m, 0, blk, :] if down else WGU[:, 0, blk, c0:c0 + cols]
            e.wait_ge(S["d_w"], n + 1)
            e.activation(dst, dq[n % 4][0:m, 0:cols], ACT.Copy).then_inc(S["d_hi"], 1)

        def act_dequant_scaled(e, n):
            if not 0 <= n < ND:
                return
            _, (blk, down, c0, cols) = DQ_UNITS[n]
            m = width(blk) if down else P
            e.wait_ge(S["d_gathered"], n + 1)
            reached(e, S["d_lo"], n - 3)
            e.activation(dq[n % 4][0:m, 0:cols], GB[0:m, 0:cols], ACT.Copy,
                         scale=SC[0:m, 6:7] if down else SC[0:m, 5:6]).then_inc(S["d_scaled"], 1)

        def act_dequant(e, k):
            act_dequant_scaled(e, k - 1)
            act_dequant_hi(e, k - 2)
            act_dequant_conv(e, k)

        def act_dequant_conv(e, n):
            if not 0 <= n < ND:
                return
            _, (blk, down, c0, cols) = DQ_UNITS[n]
            m = width(blk) if down else P
            e.wait_ge(S["d_int"], n + 1)
            reached(e, S["d_gathered"], n - 1)
            e.activation(wbf[n % 2][0:m, 0:cols], wint[n % 2][0:m, 0:cols], ACT.Copy).then_inc(S["d_conv"], 1)

        def act_qk(e, c, i, w, G):
            e.wait_ge(S["proj_done"], 6 * c + i + 1)
            if w == 1:
                if not (isinstance(c, int) and c == 0):
                    e.wait_ge(S["tr_done"], t_at(c - 1, f"pT{SLOTS - 2 + G}"))
            else:
                e.wait_ge(S["v_lo"], 2 * c + G + 1)
            if isinstance(c, int) and c == 0 and G == 0:
                e.wait_ge(S["wlo_done"], 1 if w == 1 else 4)
            for g2 in range(2):
                g = 2 * G + g2
                src = JB[G][:, g2 * TOK:(g2 + 1) * TOK]
                e.activation(pring[:, G, g2 * TOK:(g2 + 1) * TOK], src, ACT.Identity,
                             bias=bqk[:, w, g:g + 1], scale=(KQ if w == 0 else KK))
                for v in range(2):
                    ins = e.activation((qm, km)[w][:, 0, NB * g:NB * g + NB, v, :], src.rearrange("p (n t) -> p n t", n=NB),
                                       ACT.Identity, bias=BMASK[:, w, v, g:g + 1], scale=KMASK[:, 2 * w + v:2 * w + v + 1])
            ins.then_inc(S["qk_evicted"], 1)

        def act_ffn(e, f, slot):
            for u in range(UNITS):
                blocks = min(2, FB - 2 * u)
                m, cols = width(2 * u), blocks * TOK
                if G_AT[u] == slot:
                    e.wait_ge(S["g_done"], UNITS * f + u + 1)
                    if u >= 2:
                        e.wait_ge(S["h_lo"], UNITS * f + u - 1)
                    e.activation(hbuf[0:m, u % 2, 0:cols], GB[0:m, 0:cols], ACT.Tanh,
                                 scale=KTANH[0:m]).then_inc(S["tanh_done"], 1)
                if U_AT[u] + 1 == slot:
                    e.wait_ge(S["h_ready"], UNITS * f + u + 1)
                    e.activation(hT[0:m, 0, 2 * u:2 * u + blocks, :].rearrange("p a t -> p (a t)"),
                                 hbuf[0:m, u % 2, 0:cols], ACT.Copy).then_inc(S["h_hi"], 1)

        def act_slice(e, c, k, first):
            if first:
                act_dequant(e, k - len(PRE))
            else:
                act_ffn(e, c - 1, k)

        def act_chunk(e, c, first=False, last=False):
            act_qk(e, c, 0, 1, 0)
            if first:
                act_whi(e, 2)
            act_qk(e, c, 1, 1, 1)
            if first:
                act_whi(e, 3)
                act_scale_part(e, 1)
            if not first:
                act_hi(e, c, "x2T0"), act_hi(e, c, "x2T1")
            for t in range(TILES):
                e.wait_ge(S["v_evicted"], 2 * c + t + 1)
                reached(e, S["v_stacked"], 64 * c)
                e.activation(ap(vsb[:, t], 0, P, 0, [(VROW, HEADS), (HEADS * VROW, 2), (1, 16)]),
                             pring[:, t, :].rearrange("p (h q n) -> p h q n", h=HEADS, q=2), ACT.Copy).then_inc(S["v_hi"], 1)
            if first:
                e.wait_ge(S["wlo_done"], 3)
                act_hi(e, -1, "xT0"), act_hi(e, -1, "xT1")
                act_scale_part(e, 2)
            act_qk(e, c, 4, 0, 0)
            act_slice(e, c, 0, first)
            act_qk(e, c, 5, 0, 1)
            for step in range(STEPS + 1):
                if not first:
                    act_slice(e, c, len(PRE) + 2 * step - 1, first)
                if step < SLOTS:
                    s = step
                    e.wait_ge(S["s_done"], SLOTS * c + s + 1)
                    if s >= 2:
                        e.wait_ge(S["tr_done"], t_at(c, f"pT{s - 2}"))
                    e.activation(pring[:, s % 2, :], SB[s % 2][:, :], ACT.Copy).then_inc(S["s_copied"], 1)
                if first:
                    act_slice(e, c, len(PRE) + 2 * step - 1, first)
                if step - 1 in EXTRA and EXTRA[step - 1] in (T_LAST if last else T_ORDER):
                    act_hi(e, c, EXTRA[step - 1])
                if 1 <= step <= SLOTS:
                    s = step - 1
                    reached(e, S["pv_done"], SLOTS * c + s - 1)
                    act_hi(e, c, f"pT{s}")
                if not first:
                    act_slice(e, c, len(PRE) + 2 * step, first)
                if step < SLOTS:
                    e.wait_ge(S["sub_done"], SLOTS * c + step + 1)
                    e.activation(pring[:, step % 2, :], pring[:, step % 2, :], ACT.Exp, scale=KSM).then_inc(S["exp_done"], 1)
                if first:
                    act_slice(e, c, len(PRE) + 2 * step, first)
            act_hi(e, c, "oT1")
            for k in range(len(PRE) + 2 * STEPS + 1, SLICES + 1):
                if not first:
                    act_ffn(e, c - 1, k)

        n_setup = [0]

        def link(e, ins):
            n_setup[0] += 1
            ins.then_inc(S["dve_setup"], 1)
            e.wait_ge(S["dve_setup"], n_setup[0])

        def dve_setup(e):
            e.memset(MX, 0.0)
            link(e, e.memset(NHALF, -0.5))
            e.wait_ge(S["pool_iv"], 1)
            e.tensor_scalar(smalli[:, 5:6], smalli[:, 0:1], 31, None, ALU.bitwise_and)
            e.tensor_scalar(smalli[:, 1:2], smalli[:, 0:1], 7, 2, ALU.bitwise_and, ALU.logical_shift_left)
            e.tensor_scalar(smalli[:, 2:3], smalli[:, 0:1], 3, 1, ALU.logical_shift_right, ALU.bitwise_and)
            e.tensor_scalar(smalli[:, 3:4], smalli[:, 0:1], 4, 1, ALU.logical_shift_right, ALU.bitwise_and)
            e.tensor_scalar(smalli[:, 6:7], smalli[:, 0:1], 5, 2, ALU.logical_shift_right, ALU.logical_shift_left)
            link(e, e.tensor_scalar(smalli[:, 4:5], smalli[:, 0:1], 3, None, ALU.bitwise_and))
            e.tensor_copy(GM, smalli[:, 5:6]).then_inc(S["gm_ready"], 1)
            for k in range(2):
                for v in range(2):
                    e.tensor_scalar(MASK[:, 2 * k + v:2 * k + v + 1], smalli[:, 2 + k:3 + k], float(v), None, ALU.is_equal)
            link(e, e.tensor_copy(T1, smalli[:, 4:5]))
            e.tensor_scalar(eye4, eye4, T1, None, ALU.is_equal)
            link(e, e.tensor_tensor(T3, smalli[:, 6:7], T1, ALU.add))
            link(e, e.tensor_scalar(own, own, T3, None, ALU.is_equal))
            e.wait_ge(S["const_loaded"], 16 * 5)
            link(e, e.tensor_tensor(inter_own.rearrange("p (g j n) -> p g j n", g=KB, j=SUP),
                                    ap(inter_all, 0, P, 0, [(64, KB), (1, SUP), (SUP, 16)]),
                                    ap(own, 0, P, 0, [(0, KB), (0, SUP), (1, 16)]), ALU.mult))
            link(e, e.tensor_reduce(iv, inter_own.rearrange("p (n k) -> p n k", k=16), AX_X, ALU.add))
            link(e, e.tensor_scalar(T2, AMP, 0.1, None, ALU.mult))
            for g in range(KB):
                link(e, e.scalar_tensor_tensor(iv[:, 4 * g:4 * g + 4], iv[:, 4 * g:4 * g + 4], T2, eye4, ALU.mult, ALU.add))
            e.wait_ge(S["pool_const"], 2)
            for g in range(KB):
                ins = e.tensor_tensor(tmat[:, g, :].rearrange("p (a m d) -> p a m d", a=4, m=4),
                                      maskm.rearrange("p (a m d) -> p a m d", a=4, m=4),
                                      ap(iv, 0, P, 4 * g, [(0, 4), (1, 4), (0, 8)]), ALU.mult)
            ins.then_inc(S["t_ready"], 1)
            for g in range(KB):
                ins = e.tensor_copy(bvx[:, g * P:(g + 1) * P], ap(bv_row, 0, P, g, [(0, P)]))
            ins.then_inc(S["t_ready"], 1)
            e.tensor_copy(ident16[:, :], ident[:, :]).then_inc(S["ident16_ready"], 1)
            e.tensor_reduce(MX[:, 10:11], iv, AX_X, ALU.max, apply_absolute_value=True)
            for i, w in enumerate(WORDER):
                e.wait_ge(S[f"w_loaded{w}"], 16)
                if i == 3:
                    for g in range(KB):
                        for hh in range(2):
                            for j in range(2):
                                ins = e.tensor_copy(wop[g][:, (2 * hh + j) * P:(2 * hh + j + 1) * P].rearrange("p (h q d) -> p h q d", h=8, q=2),
                                                    ap(wraw[3][:, g], 0, P, 256 * hh + j, [(32, 8), (2, 2), (4, 8)]))
                    ins.then_inc(S["wo_permuted"], 1)
                e.tensor_reduce(MX[:, w:w + 1], wraw[w], mybir.AxisListType.XY, ALU.max, apply_absolute_value=True).then_inc(S["wmax_done"], 1)
                if i == 0:
                    dve_zeros(e)
            e.wait_ge(S["bias_evicted"], 1)
            e.tensor_reduce(MX[:, 5:6], bqk[:, 0, :], AX_X, ALU.max, apply_absolute_value=True)
            e.tensor_reduce(MX[:, 6:7], bqk[:, 1, :], AX_X, ALU.max, apply_absolute_value=True)
            e.tensor_reduce(MX[:, 7:8], bv_row[:, :], AX_X, ALU.max, apply_absolute_value=True)
            e.wait_ge(S["sc_loaded"], 32 * PARTS)
            e.tensor_reduce(MX[0:GROUPS_GU, 8:9], scgu[0:GROUPS_GU, :], AX_X, ALU.max, apply_absolute_value=True)
            e.tensor_reduce(MX[0:GROUPS_D, 9:10], scd[0:GROUPS_D, :], AX_X, ALU.max, apply_absolute_value=True)
            for c in range(NCHUNK):
                e.wait_ge(S[f"ctxm_loaded{c}"], 16)
                ins = e.tensor_reduce(MXC[:, c:c + 1], cmax_st[:, c], AX_X, ALU.max, apply_absolute_value=True)
            link(e, ins)
            e.tensor_reduce(MX[:, 4:5], MXC, AX_X, ALU.max).then_inc(S["max_ready"], 1)
            e.wait_ge(S["x_loaded"], 16)
            for t in range(TILES):
                ln_stats(e, "x", 0, t, xin[:, t, :])
            e.wait_ge(S["max_all"], 1)
            e.tensor_copy(BD[:, 3:5], MR[:, 3:5])
            e.tensor_scalar(BD[:, 5:7], MR[:, 8:10], 16.0, None, ALU.mult)
            e.tensor_scalar(T1, MR[:, 4:5], float(DM), None, ALU.mult)
            link(e, e.tensor_scalar(BD[:, 0:3], MR[:, 0:3], MR[:, 10:11], float(SUP), ALU.mult, ALU.mult))
            e.scalar_tensor_tensor(BD[:, 7:8], BD[:, 0:1], float(DM), MR[:, 5:6], ALU.mult, ALU.add)
            e.scalar_tensor_tensor(BD[:, 8:9], BD[:, 1:2], T1, MR[:, 6:7], ALU.mult, ALU.add)
            e.scalar_tensor_tensor(BD[:, 9:10], BD[:, 2:3], T1, MR[:, 7:8], ALU.mult, ALU.add)
            link(e, e.tensor_scalar(T2, BD[:, 5:6], float(DM), None, ALU.mult))
            link(e, e.tensor_tensor(BD[:, 10:11], T2, T2, ALU.mult))
            link(e, e.tensor_scalar(BD, BD, 1e-30, None, ALU.max))
            link(e, e.tensor_scalar(PW.bitcast(I32), BD.bitcast(I32), 0x7F800000, None, ALU.bitwise_and))
            link(e, e.tensor_scalar(SC.bitcast(I32), PW.bitcast(I32), -1.0, float((254 + TOP) << 23), ALU.mult, ALU.add))
            link(e, e.tensor_scalar(IV.bitcast(I32), PW.bitcast(I32), float(-(TOP << 23)), None, ALU.add))

            sc = lambda i: SC[:, i:i + 1]
            inv = lambda i: IV[:, i:i + 1]
            products = [(KQ, [sc(7), inv(0)], 1.0 / LN_SCALE), (KK, [sc(8), inv(1), inv(4)], 1.0),
                        (KV, [sc(9), inv(2), inv(4)], 1.0), (KSM, [inv(7), inv(8)], DK ** -0.5),
                        (KWO, [inv(9), inv(3)], 1.0), (KTANH, [inv(5)], 0.5 / LN_SCALE),
                        (KH, [inv(5), inv(5), sc(10)], 0.5 / LN_SCALE ** 2), (KY, [inv(10), inv(6)], 1.0)]
            for level in range(3):
                for dst, terms, factor in products:
                    if level == 0:
                        ins = e.tensor_scalar(dst, terms[0], factor, None, ALU.mult)
                    elif level < len(terms):
                        ins = e.tensor_scalar(dst, dst, terms[level], None, ALU.mult)
                if level == 0:
                    e.tensor_scalar(bqk[:, 0, :], bqk[:, 0, :], sc(7), None, ALU.mult)
                    ins = e.tensor_scalar(bqk[:, 1, :], bqk[:, 1, :], sc(8), None, ALU.mult)
                link(e, ins)
            for w, kw in enumerate((KQ, KK)):
                for v in range(2):
                    mk = MASK[:, 2 * w + v:2 * w + v + 1]
                    e.tensor_tensor(KMASK[:, 2 * w + v:2 * w + v + 1], kw, mk, ALU.mult)
                    e.tensor_scalar(BMASK[:, w, v, :], bqk[:, w, :], mk, None, ALU.mult)
            e.tensor_scalar(bv_row[:, :], bv_row[:, :], sc(9), None, ALU.mult).then_inc(S["scale_ready"], 1)
            dve_wlo(e, 0)
            dve_lo(e, -1, "cT0"), dve_lo(e, -1, "cT1")
            dve_wlo(e, 1)
            e.wait_ge(S["fold_done"], 4)
            e.memset(vsb[:, 0, :, :, VROW - 1:VROW], 1.0)
            link(e, e.memset(vsb[:, 1, :, :, VROW - 1:VROW], 1.0))

        def dve_wlo(e, i):
            w = WORDER[i]
            e.wait_ge(S["whi_done"], i + 1)
            e.scalar_tensor_tensor(WT[:, w, 1], wraw[w], SC[:, w:w + 1], WT[:, w, 0], ALU.mult, ALU.subtract).then_inc(S["wlo_done"], 1)

        def dve_zeros(e):
            e.wait_ge(S["z_loaded"], 32)
            for i, (groups, cols, raw, dst) in enumerate(((GROUPS_GU, 2 * INTER, zraw_gu, z_gu), (GROUPS_D, DM, zraw_d, z_d))):
                reached(e, S["z_ready"], i)
                for k in range(8):
                    ins = e.tensor_scalar(ap(zint, 0, groups, k, [(8, cols // 8)]), raw[0:groups, :], 4 * k, 15,
                                          ALU.logical_shift_right, ALU.bitwise_and)
                link(e, ins)
                e.tensor_scalar(dst[0:groups, 0:cols], zint[0:groups, 0:cols], -1.0, -1.0, ALU.mult, ALU.add).then_inc(S["z_ready"], 1)

        def dve_dequant_int(e, n):
            if not 0 <= n < ND:
                return
            i, (blk, down, c0, cols) = DQ_UNITS[n]
            m = width(blk) if down else P
            if n == units_before(i):
                earlier = sum(piece_loads(k) for k in range(i % 2, i + 1, 2))
                e.wait_ge(S[f"qw_loaded{i % 2}"], 16 * earlier)
            reached(e, S["d_conv"], n - 1)
            at_col = (blk % 2) * DM if down else c0 % INTER
            e.tensor_scalar(wint[n % 2][0:m, 0:cols], qw_st[i % 2][0:m, at_col:at_col + cols],
                            smalli[0:m, 1:2].bitcast(U32), 15,
                            ALU.logical_shift_right, ALU.bitwise_and).then_inc(S["d_int"], 1)

        def dve_dequant_w(e, n):
            if not 0 <= n < ND:
                return
            _, (blk, down, c0, cols) = DQ_UNITS[n]
            m = width(blk) if down else P
            w = dq[n % 4][0:m, 0:cols]
            e.wait_ge(S["d_scaled"], n + 1)
            e.tensor_tensor(w, w, UB[0:m, 0:cols], ALU.mult).then_inc(S["d_w"], 1)

        def ln_stats(e, which, c, t, src):
            k, step = t + (2 if which == "y" else 0), S[f"ln{which}_step"]
            e.bn_stats(stats[:, k, :], src).then_inc(step, 1)
            e.wait_ge(step, 4 * c + 2 * t + 1)
            e.memset(T4, 0.0)
            e.bn_aggr(mv[:, k, :], stats[:, k, :]).then_inc(step, 1)
            e.wait_ge(step, 4 * c + 2 * t + 2)
            e.tensor_scalar(vareps[:, k:k + 1], mv[:, k, 1:2], EPS, LN_SCALE ** -2, ALU.add, ALU.mult).then_inc(S[f"ln{which}_var"], 1)

        def ln_apply(e, which, c, t, src, done):
            k = t + (2 if which == "y" else 0)
            e.wait_ge(S[f"ln{which}_rstd"], 2 * c + t + 1)
            e.tensor_scalar(xln[:, t, :], src, mv[:, k, 0:1], rstd[:, k:k + 1], ALU.subtract, ALU.mult).then_inc(done, 1)

        def dve_mask(e, c, n, w, G):
            e.wait_ge(S["qk_evicted"], 4 * c + n + 1)
            dst = (qm, km)[w][:, :, 8 * G:8 * G + 8]
            src = pring[:, G, :].rearrange("p (n t) -> p n t", n=8)
            for v in range(2):
                mk = MASK[:, 2 * w + v:2 * w + v + 1]
                ins = e.scalar_tensor_tensor(dst[:, 1, :, v, :], src, mk, dst[:, 0, :, v, :], ALU.mult, ALU.subtract)
            ins.then_inc(S["qm_ready"], 1)

        def dve_o(e, c, s):
            b, a = s // 4, s % 4
            jb = JB[s % 2]
            e.wait_ge(S["pv_done"], SLOTS * c + s + 1)
            k = s % 2
            for j in range(2):
                e.tensor_reduce(osum[64 * j:64 * j + 64, k, :, :], ap(jb, 64 * j, 64, 8 * j, [(VROW, 8), (1, 8), (16, 2)]), AX_X, ALU.add)
            e.reciprocal(rinv[:, k, :], ap(jb, 0, P, VROW - 1, [(VROW, 8)])).then_inc(S["o_step"], 1)
            e.wait_ge(S["o_step"], SLOTS * c + s + 1)
            if s in (0, 8) and not (isinstance(c, int) and c == 0):
                e.wait_ge(S["tr_done"], t_at(c - 1, f"oT{s // 8}"))
            e.tensor_tensor(ap(obuf, 0, P, 256 * b + 16 * a, [(64, 4), (8, 2), (1, 8)]),
                            osum[:, k].rearrange("p (h q) d -> p h q d", q=2),
                            ap(rinv, 0, P, 8 * k, [(2, 4), (1, 2), (0, 8)]), ALU.mult).then_inc(S["o_ready"], 1)

        def dve_ffn(e, f, slot):
            for u in range(UNITS):
                blocks = min(2, FB - 2 * u)
                m, cols = width(2 * u), blocks * TOK
                hb = hbuf[0:m, u % 2, 0:cols]
                if G_AT[u] == slot:
                    e.wait_ge(S["tanh_done"], UNITS * f + u + 1)
                    e.scalar_tensor_tensor(hb, hb, 1.0, GB[0:m, 0:cols], ALU.add, ALU.mult).then_inc(S["g_freed"], 1)
                if U_AT[u] == slot:
                    e.wait_ge(S["u_done"], UNITS * f + u + 1)
                    e.wait_ge(S["g_freed"], UNITS * f + u + 1)
                    e.scalar_tensor_tensor(hb, hb, KH[0:m], UB[0:m, 0:cols], ALU.mult, ALU.mult).then_inc(S["h_ready"], 1)
            for t in range(TILES):
                if D_AT[t] == slot:
                    e.wait_ge(S["d_done"], 2 * f + t + 1)
                    if is_last(f):
                        e.wait_ge(S[f"y_stored{t}"], 16 * f)
                    e.scalar_tensor_tensor(yout[:, t, :], (GB, UB)[t][:, :], KY, x2[:, t, :], ALU.mult, ALU.add).then_inc(S["y_ready"], 1)

        def dve_next_x(e, c, step, first):
            if step == 1:
                e.wait_ge(S["x_loaded"], 16 * (c + 2))
            if 1 <= step <= TILES:
                t = step - 1
                ln_stats(e, "x", c + 1, t, xin[:, t, :])
            if 4 <= step < 4 + TILES:
                t = step - 4
                e.wait_ge(S["tr_done"], t_at(-1, f"xT{t}") if first else t_at(c, f"x2T{t}"))
                ln_apply(e, "x", c + 1, t, xin[:, t, :], S["xln_ready"])

        def dve_chunk(e, c, first=False, last=False):
            if first:
                for t in range(TILES):
                    ln_apply(e, "x", c, t, xin[:, t, :], S["xln_ready"])
            dve_mask(e, c, 0, 1, 0)
            if first:
                dve_wlo(e, 2)
            dve_mask(e, c, 1, 1, 1)
            if first:
                dve_wlo(e, 3)
            for t in range(TILES):
                e.wait_ge(S["proj_done"], 6 * c + 3 + t)
                e.wait_ge(S["qm_ready"], 4 * c + t + 1)
                e.scalar_tensor_tensor(pring[:, t, :], JB[t][:, :], KV, bv_row[:, :], ALU.mult, ALU.add).then_inc(S["v_evicted"], 1)
                if not first and t == 0:
                    dve_lo(e, c, "x2T0"), dve_lo(e, c, "x2T1")
            for t in range(TILES):
                e.wait_ge(S["v_hi"], 2 * c + t + 1)
                e.tensor_tensor(ap(vsb[:, t], 0, P, 16, [(VROW, HEADS), (HEADS * VROW, 2), (1, 16)]),
                                pring[:, t, :].rearrange("p (h q n) -> p h q n", h=HEADS, q=2),
                                ap(vsb[:, t], 0, P, 0, [(VROW, HEADS), (HEADS * VROW, 2), (1, 16)]), ALU.subtract).then_inc(S["v_lo"], 1)
            if first:
                dve_lo(e, -1, "xT0"), dve_lo(e, -1, "xT1")
            dve_mask(e, c, 2, 0, 0)
            if not first:
                dve_ffn(e, c - 1, 0)
            dve_mask(e, c, 3, 0, 1)
            for step in range(STEPS + 1):
                if step >= 3:
                    dve_o(e, c, step - 3)
                if first:
                    dve_dequant_int(e, 2 * step - 1)
                else:
                    dve_ffn(e, c - 1, len(PRE) + 2 * step - 1)
                if step < SLOTS:
                    s = step
                    e.wait_ge(S["s_copied"], SLOTS * c + s + 1)
                    e.tensor_reduce(negmax[:, s % 2, :], pring[:, s % 2, :].rearrange("p (n k) -> p n k", n=8), AX_X, ALU.max,
                                    negate=True).then_inc(S["max_done"], 1)
                if first:
                    dve_dequant_w(e, 2 * step - 2)
                if step - 1 in EXTRA and EXTRA[step - 1] in (T_LAST if last else T_ORDER):
                    dve_lo(e, c, EXTRA[step - 1])
                if 1 <= step <= SLOTS:
                    dve_lo(e, c, f"pT{step - 1}")
                if first:
                    dve_dequant_int(e, 2 * step), dve_dequant_w(e, 2 * step - 1)
                else:
                    dve_ffn(e, c - 1, len(PRE) + 2 * step)
                if not last:
                    dve_next_x(e, c, step, first)
            dve_lo(e, c, "oT1")
            for k in range(len(PRE) + 2 * STEPS + 1, SLICES):
                if not first:
                    dve_ffn(e, c - 1, k)
            for t in range(TILES):
                e.wait_ge(S["wo_done"], 2 * c + t + 1)
                e.wait_ge(S["xres_ready"], 2 * c + t + 1)
                e.scalar_tensor_tensor(x2[:, t, :], JB[t][:, :], KWO, xres[:, t, :], ALU.mult, ALU.add).then_inc(S["x2_part"], 1)
                e.wait_ge(S["x2_part"], 2 * c + t + 1)
                ln_stats(e, "y", c, t, x2[:, t, :])
            for t in range(TILES):
                if last:
                    e.wait_ge(S["tr_done"], t_at(c - 1, f"xT{t}"))
                else:
                    e.wait_ge(S["tr_done"], t_at(c, f"xT{t}"))
                ln_apply(e, "y", c, t, x2[:, t, :], S["x2ln_ready"])

        def pool_link(e, ins):
            n_pool[0] += 1
            ins.then_inc(S["pool_setup"], 1)
            e.wait_ge(S["pool_setup"], n_pool[0])

        n_pool = [0]

        def pool_setup(e):
            e.iota(smalli[:, 0:1], [[0, 1]], base=0, channel_multiplier=1)
            e.iota(own, [[1, 16]], base=0, channel_multiplier=0, allow_small_or_imprecise_dtypes=True)
            e.iota(eye4, [[1, 4]], base=0, channel_multiplier=0, allow_small_or_imprecise_dtypes=True).then_inc(S["pool_iv"], 1)
            e.memset(ident[:, :], 0.0)
            pool_link(e, e.memset(maskm, 1.0))
            e.affine_select(out=ident[:, :], in_=ident[:, :], compare_op=ALU.not_equal, fill=1.0, base=0,
                            pattern=[[-1, P]], channel_multiplier=1).then_inc(S["pool_const"], 1)
            v = maskm.rearrange("p (a m d) -> p a m d", a=4, m=4)
            pat = [[-32, 4], [0, 4], [-4, 8]]
            pool_link(e, e.affine_select(out=v, in_=v, compare_op=ALU.is_ge, fill=0.0, base=0, pattern=pat,
                                         channel_multiplier=1))
            e.affine_select(out=v, in_=v, compare_op=ALU.is_ge, fill=0.0, base=3, pattern=[[32, 4], [0, 4], [4, 8]],
                            channel_multiplier=-1).then_inc(S["pool_const"], 1)
            e.memset(scd[0:96, :], 0.0)
            e.memset(scgu[0:96, :], 0.0).then_inc(S["sc_zeroed"], 1)
            pool_hot(e, GROUPS_D, INTER, gidx_d, hot_d)
            e.wait_ge(S["max_ready"], 1)
            e.partition_all_reduce(MR, MX, P, ABSMAX).then_inc(S["max_all"], 1)
            pool_ln(e, "x", 0)
            e.wait_ge(S["sc_high"], 2)
            e.tensor_tensor(rest_gu[0:96, :], scgu[0:96, :], sc3_gu[0:96, :], ALU.subtract).then_inc(S["sc_rest"], 1)
            e.tensor_tensor(rest_d[0:96, :], scd[0:96, :], sc3_d[0:96, :], ALU.subtract).then_inc(S["sc_rest"], 1)
            e.wait_ge(S["fold_done"], 4)
            e.memset(vv_words, 0.0).then_inc(S["vv_zeroed"], 1)
            e.wait_ge(S["sc_rest"], 2)
            e.wait_ge(S["sc_high"], 4)
            e.tensor_tensor(rest_gu[0:64, :], rest_gu[0:64, :], sc3_gu[0:64, :], ALU.subtract).then_inc(S["sc_rest"], 1)
            e.tensor_tensor(rest_d[0:64, :], rest_d[0:64, :], sc3_d[0:64, :], ALU.subtract).then_inc(S["sc_rest"], 1)
            e.wait_ge(S["bo_loaded"], 16)
            e.wait_ge(S["wlo_done"], 3)
            pool_xres(e, 0)
            pool_hot(e, GROUPS_GU, DM, gidx_gu, hot_gu)

        def pool_hot(e, groups, rows, gidx, hot):
            e.wait_ge(S["gi_loaded"], 32)
            e.wait_ge(S["gm_ready"], 1)
            h, g = hot_f[0:96, 0:rows], gidx[0:96, :]
            pool_link(e, e.tensor_copy(h, g.bitcast(I32)))
            pool_link(e, e.tensor_scalar(g, h, 0.0, float(groups), ALU.is_lt, ALU.mult))
            pool_link(e, e.tensor_tensor(h, h, g, ALU.add))
            pool_link(e, e.tensor_scalar(h, h, 0.0, float(groups - 1), ALU.max, ALU.min))
            e.tensor_scalar(hot[0:96, :], h, GM[0:96], None, ALU.is_equal).then_inc(S["hot_ready"], 1)
            e.wait_ge(S["hot_ready"], 1)

        def pool_dequant_lo(e, n):
            if not 0 <= n < ND:
                return
            _, (blk, down, c0, cols) = DQ_UNITS[n]
            m = width(blk) if down else P
            hi, lo = ((WD[0:m, i, blk, :] if down else WGU[:, i, blk, c0:c0 + cols]) for i in range(2))
            e.wait_ge(S["d_hi"], n + 1)
            e.tensor_tensor(lo, dq[n % 4][0:m, 0:cols], hi, ALU.subtract).then_inc(S["d_lo"], 1)

        def pool_ln(e, which, c):
            for t in range(TILES):
                k = t + (2 if which == "y" else 0)
                e.wait_ge(S[f"ln{which}_var"], 2 * c + t + 1)
                e.tensor_tensor(rstd[:, k:k + 1], vareps[:, k:k + 1], NHALF, ALU.pow).then_inc(S[f"ln{which}_rstd"], 1)

        def pool_xres(e, c):
            for t in range(TILES):
                e.tensor_tensor(xres[:, t, :], xin[:, t, :], bo_row[:, :], ALU.add).then_inc(S["xres_ready"], 1)

        def pool_ffn(e, f, slot):
            for u in range(UNITS):
                if U_AT[u] + 1 == slot:
                    blocks = min(2, FB - 2 * u)
                    m, cols = width(2 * u), blocks * TOK
                    flat = lambda i: hT[0:m, i, 2 * u:2 * u + blocks, :].rearrange("p a t -> p (a t)")
                    e.wait_ge(S["h_hi"], UNITS * f + u + 1)
                    e.tensor_tensor(flat(1), hbuf[0:m, u % 2, 0:cols], flat(0), ALU.subtract).then_inc(S["h_lo"], 1)

        def pool_chunk(e, c, first=False, last=False):
            for step in range(STEPS + 1):
                if step < SLOTS:
                    s = step
                    e.wait_ge(S["max_done"], SLOTS * c + s + 1)
                    ring = pring[:, s % 2, :].rearrange("p (n k) -> p n k", n=8)
                    e.tensor_tensor(ring, ring,
                                    ap(negmax, 0, P, 8 * (s % 2), [(1, 8), (0, 64)]), ALU.add).then_inc(S["sub_done"], 1)
                if step == 3 and not last:
                    pool_ln(e, "x", c + 1)
                for k in (2 * step - 1, 2 * step):
                    if first:
                        pool_dequant_lo(e, k - 2)
                    else:
                        pool_ffn(e, c - 1, len(PRE) + k)
            pool_ln(e, "y", c)
            if not last:
                e.wait_ge(S["x2_part"], 2 * c + 2)
                pool_xres(e, c + 1)

        block = stack.enter_context(nc.Block())

        @block.sync
        def _(sp):
            sync_setup(sp)
            sync_chunk(sp, 0, first=True)
            with sp.Fori(1, NCHUNK - 2) as c:
                sync_chunk(sp, c)
            for c in (NCHUNK - 2, NCHUNK - 1):
                sync_chunk(sp, c)
            store(sp, NCHUNK - 1)
            for t in range(TILES):
                sp.wait_ge(S[f"y_stored{t}"], 16 * NCHUNK)

        @block.tensor
        def _(pe):
            pe_setup(pe)
            pe_chunk(pe, 0, first=True)
            pe.wait_ge(S["d_lo"], ND)
            with pe.Fori(1, NCHUNK - 1) as c:
                pe_chunk(pe, c)
            pe_chunk(pe, NCHUNK - 1, last=True)
            for t in range(TILES):
                pe_transpose_tile(pe, NCHUNK, f"x2T{t}", xln, S["x2ln_ready"], 2 * (NCHUNK - 1) + t + 1)
            pe.wait_ge(S["t_lo"], t_at(NCHUNK, "x2T1"))
            for _ in pe_ffn(pe, NCHUNK - 1):
                pass

        @block.scalar
        def _(act):
            act_setup(act)
            act_chunk(act, 0, first=True)
            act.wait_ge(S["d_lo"], ND)
            with act.Fori(1, NCHUNK - 1) as c:
                act_chunk(act, c)
            act_chunk(act, NCHUNK - 1, last=True)
            act_hi(act, NCHUNK, "x2T0"), act_hi(act, NCHUNK, "x2T1")
            for slot in range(SLICES + 1):
                act_ffn(act, NCHUNK - 1, slot)

        @block.vector
        def _(dve):
            dve_setup(dve)
            dve_chunk(dve, 0, first=True)
            with dve.Fori(1, NCHUNK - 1) as c:
                dve_chunk(dve, c)
            dve_chunk(dve, NCHUNK - 1, last=True)
            dve_lo(dve, NCHUNK, "x2T0"), dve_lo(dve, NCHUNK, "x2T1")
            for slot in range(SLICES + 1):
                dve_ffn(dve, NCHUNK - 1, slot)

        @block.gpsimd
        def _(pool):
            pool_setup(pool)
            pool_chunk(pool, 0, first=True)
            with pool.Fori(1, NCHUNK - 1) as c:
                pool_chunk(pool, c)
            pool_chunk(pool, NCHUNK - 1, last=True)
            for slot in range(SLICES + 1):
                pool_ffn(pool, NCHUNK - 1, slot)


_INS = ["x", "ctx_4096", "L0_xattn_Wq", "L0_xattn_bq", "L0_xattn_Wk", "L0_xattn_bk", "L0_xattn_Wv", "L0_xattn_bv",
        "L0_xattn_interference", "L0_xattn_amp", "L0_xattn_Wo", "L0_xattn_bo", "L0_ffn_qweight_gu", "L0_ffn_qzeros_gu",
        "L0_ffn_scales_gu", "L0_ffn_g_idx_gu", "L0_ffn_qweight_down", "L0_ffn_qzeros_down", "L0_ffn_scales_down",
        "L0_ffn_g_idx_down"]


def kernel(**inputs):
    import numpy as np
    import concourse.bacc as bacc
    from concourse.bass_utils import run_bass_kernel_spmd

    nc = bacc.Bacc("TRN2", target_bir_lowering=False, num_devices=1)
    arrays, args = {}, []
    for name in _INS:
        a = np.ascontiguousarray(inputs[name])
        arrays[f"in_{name}"] = a
        args.append(nc.dram_tensor(f"in_{name}", a.shape, mybir.dt.from_np(a.dtype), kind="ExternalInput").ap())
    out = nc.dram_tensor("out_y", (BATCH, SEQ, DM), F32, kind="ExternalOutput").ap()
    build(nc, *args, out)
    r = run_bass_kernel_spmd(nc, [arrays], core_ids=[0])
    return r.results[0]["out_y"]
```
